# Optimizing a Trainium2 kernel written in Bass

```python
import numpy as np
import jax
import jax.numpy as jnp

def _softmax(x, axis=-1):
    return jax.nn.softmax(x, axis=axis)

def _gelu(x):
    return jax.nn.gelu(x, approximate=True)

def _silu(x):
    return jax.nn.silu(x)

def _sigmoid(x):
    return jax.nn.sigmoid(x)

def _layernorm(x, axis=-1, eps=1e-05):
    m = jnp.mean(x, axis=axis, keepdims=True)
    v = jnp.var(x, axis=axis, keepdims=True)
    return (x - m) / jnp.sqrt(v + eps)

def _scatter_add(tgt, idx, src, axis=0):
    return tgt.at[idx].add(src)

def _segment_sum(src, seg, n):
    return jax.ops.segment_sum(src, seg, n)
kernel_name = 'mk_vit_tower_cls_d1_tok_img256_r4_8b1b0c'

def setup_inputs(seed: int=0):
    np.random.seed(seed)
    _w = jnp.asarray

    def _rec_inputs():
        import jax
        import jax.numpy as jnp
        _rk = jax.random.key(seed)
        x = 9.04603e-05 + 1.00016 * jax.random.normal(jax.random.fold_in(_rk, 1), (4, 1, 224, 224), jnp.float32)
        cls_tok = 0.02 * jax.random.normal(jax.random.fold_in(_rk, 5), (1, 1, 64), jnp.float32)
        return (x, cls_tok)
    x, cls_tok = _rec_inputs()

    def _L0_tok_setup():
        import jax, jax.numpy as jnp
        import numpy as np
        WS = 7
        H = W = 56
        C = 64
        NH = 8
        HD = C // NH
        SCALE = HD ** (-0.5)
        SHIFT = WS // 2
        N = WS * WS

        def _rel_pos_index():
            coords = np.stack(np.meshgrid(np.arange(WS), np.arange(WS), indexing='ij'))
            cf = coords.reshape(2, -1)
            rel = (cf[:, :, None] - cf[:, None, :]).transpose(1, 2, 0).copy()
            rel[..., 0] += WS - 1
            rel[..., 1] += WS - 1
            rel[..., 0] *= 2 * WS - 1
            return jnp.array(rel.sum(-1))

        def _attn_mask():
            img = np.zeros((H, W), np.int32)
            cnt = 0
            for h in (slice(0, -WS), slice(-WS, -SHIFT), slice(-SHIFT, None)):
                for w in (slice(0, -WS), slice(-WS, -SHIFT), slice(-SHIFT, None)):
                    cnt += 1
                    img[h, w] = cnt
            mw = img.reshape(H // WS, WS, W // WS, WS).transpose(0, 2, 1, 3).reshape(-1, N)
            diff = mw[:, None, :] - mw[:, :, None]
            return jnp.array(np.where(diff != 0, -100.0, 0.0).astype(np.float32))

        def _layernorm(x, g, b):
            m = x.mean(-1, keepdims=True)
            v = ((x - m) ** 2).mean(-1, keepdims=True)
            return (x - m) * jax.lax.rsqrt(v + 1e-05) * g + b

        def _window_partition(x):
            B = x.shape[0]
            x = x.reshape(B, H // WS, WS, W // WS, WS, C).transpose(0, 1, 3, 2, 4, 5)
            return x.reshape(-1, N, C)

        def _window_reverse(xw, B):
            x = xw.reshape(B, H // WS, W // WS, WS, WS, C).transpose(0, 1, 3, 2, 4, 5)
            return x.reshape(B, H, W, C)

        def _swin_block(x, p, shift, rpi, amask):
            B = x.shape[0]
            shortcut = x
            h = _layernorm(x, p['n1g'], p['n1b']).reshape(B, H, W, C)
            if shift > 0:
                h = jnp.roll(h, (-shift, -shift), axis=(1, 2))
            xw = _window_partition(h)
            B_ = xw.shape[0]
            qkv = (xw @ p['qkv_w'].T + p['qkv_b']).reshape(B_, N, 3, NH, HD).transpose(2, 0, 3, 1, 4)
            q, k, v = (qkv[0], qkv[1], qkv[2])
            attn = jnp.einsum('bhnd,bhmd->bhnm', q * SCALE, k)
            attn = attn + p['rpb'][rpi].transpose(2, 0, 1)[None]
            if shift > 0:
                nW = amask.shape[0]
                attn = attn.reshape(B_ // nW, nW, NH, N, N) + amask[None, :, None]
                attn = attn.reshape(B_, NH, N, N)
            attn = jax.nn.softmax(attn, axis=-1)
            o = jnp.einsum('bhnm,bhmd->bhnd', attn, v).transpose(0, 2, 1, 3).reshape(B_, N, C)
            o = o @ p['proj_w'].T + p['proj_b']
            h = _window_reverse(o, B)
            if shift > 0:
                h = jnp.roll(h, (shift, shift), axis=(1, 2))
            x = shortcut + h.reshape(B, H * W, C)
            y = _layernorm(x, p['n2g'], p['n2b'])
            y = jax.nn.gelu(y @ p['w1'].T + p['b1'], approximate=False)
            return x + y @ p['w2'].T + p['b2']
        key = jax.random.key(seed)
        ks = jax.random.split(key, 8)
        s = 0.02
        return {'x': jax.random.normal(ks[0], (16, 1, 224, 224), jnp.float32), 'pe_w': jax.random.normal(ks[1], (C, 1, 4, 4), jnp.float32) * s, 'pe_b': jnp.zeros((C,), jnp.float32), 'pe_ng': jnp.ones((C,), jnp.float32), 'pe_nb': jnp.zeros((C,), jnp.float32), 'n1g': jnp.ones((2, C), jnp.float32), 'n1b': jnp.zeros((2, C), jnp.float32), 'qkv_w': jax.random.normal(ks[2], (2, 3 * C, C), jnp.float32) * s, 'qkv_b': jnp.zeros((2, 3 * C), jnp.float32), 'rpb': jax.random.normal(ks[3], (2, (2 * WS - 1) ** 2, NH), jnp.float32) * s, 'proj_w': jax.random.normal(ks[4], (2, C, C), jnp.float32) * s, 'proj_b': jnp.zeros((2, C), jnp.float32), 'n2g': jnp.ones((2, C), jnp.float32), 'n2b': jnp.zeros((2, C), jnp.float32), 'w1': jax.random.normal(ks[5], (2, 4 * C, C), jnp.float32) * s, 'b1': jnp.zeros((2, 4 * C), jnp.float32), 'w2': jax.random.normal(ks[6], (2, C, 4 * C), jnp.float32) * s, 'b2': jnp.zeros((2, C), jnp.float32)}
    _L0_tok_all = _L0_tok_setup()
    _L0_tok_in = {k: v for k, v in _L0_tok_all.items() if k in ('pe_w', 'pe_b', 'pe_ng', 'pe_nb', 'n1g', 'n1b', 'qkv_w', 'qkv_b', 'rpb', 'proj_w', 'proj_b', 'n2g', 'n2b', 'w1', 'b1', 'w2', 'b2')}
    del _L0_tok_all

    def _L0_attn_setup():
        import jax, jax.numpy as jnp
        import numpy as np
        from jax import lax

        def _solve_im(u, a, W_B, b_B, dt):
            s = 1.0 / (1.0 + dt * dt * a)
            Bu = jnp.einsum('bnq,pq->bnp', u, W_B) + b_B
            f_x = dt * s * Bu
            f_z = dt * dt * s * Bu
            dsa = dt * s * a
            ds = dt * s

            def step(carry, f):
                x, z = carry
                fx, fz = f
                x_new = s * x - dsa * z + fx
                z_new = ds * x + s * z + fz
                return ((x_new, z_new), z_new)
            Bsz, _, q = u.shape
            init = (jnp.zeros((Bsz, q), u.dtype), jnp.zeros((Bsz, q), u.dtype))
            _, z_t = lax.scan(step, init, (jnp.moveaxis(f_x, 1, 0), jnp.moveaxis(f_z, 1, 0)))
            return jnp.moveaxis(z_t, 0, 1)

        def _reference_tuple_inner(u, a, W_B, b_B, W_C, b_C, W_D, b_D):
            N = u.shape[1]
            dt = 1.0 / N
            y = _solve_im(u, a, W_B, b_B, dt)
            x = jnp.einsum('bnq,pq->bnp', y, W_C) + b_C + (jnp.einsum('bnq,pq->bnp', u, W_D) + b_D)
            x = jax.nn.gelu(x, approximate=False)
            out = x * jax.nn.sigmoid(x) + u
            return (out, y)
        key = jax.random.key(seed)
        ks = jax.random.split(key, 8)
        B, N, q = (16, 1024, 64)
        sc = float(1.0 / np.sqrt(q))
        return {'u': jax.random.normal(ks[0], (B, N, q), jnp.float32), 'a': jax.random.normal(ks[1], (q,), jnp.float32), 'W_B': jax.random.normal(ks[2], (q, q), jnp.float32) * sc, 'b_B': jax.random.normal(ks[3], (q,), jnp.float32) * sc, 'W_C': jax.random.normal(ks[4], (q, q), jnp.float32) * sc, 'b_C': jax.random.normal(ks[5], (q,), jnp.float32) * sc, 'W_D': jax.random.normal(ks[6], (q, q), jnp.float32) * sc, 'b_D': jax.random.normal(ks[7], (q,), jnp.float32) * sc}
    _L0_attn_all = _L0_attn_setup()
    _L0_attn_in = {k: v for k, v in _L0_attn_all.items() if k in ('a', 'W_B', 'b_B', 'W_C', 'b_C', 'W_D', 'b_D')}
    del _L0_attn_all

    def _L0_ffn_setup():
        import math
        import jax, jax.numpy as jnp
        import numpy as np
        CAPACITY_FACTOR = 1.25
        TOP_K = 2
        LN_EPS = 1e-05

        def _layer_norm(x, gamma, beta):
            mu = jnp.mean(x, axis=-1, keepdims=True)
            var = jnp.var(x, axis=-1, keepdims=True)
            return (x - mu) * jax.lax.rsqrt(var + LN_EPS) * gamma + beta
        key = jax.random.key(seed)
        ks = jax.random.split(key, 4)
        B, S, D, F, E = (8, 1024, 64, 128, 8)
        x = jax.random.normal(ks[0], (B, S, D), dtype=jnp.float32)
        Wr = jax.random.normal(ks[1], (D, E), dtype=jnp.float32) / np.sqrt(D)
        br = jnp.zeros((E,), jnp.float32)
        W1 = jax.random.normal(ks[2], (E, D, F), dtype=jnp.float32) / np.sqrt(D)
        b1 = jnp.zeros((E, F), jnp.float32)
        W2 = jax.random.normal(ks[3], (E, F, D), dtype=jnp.float32) / np.sqrt(F)
        b2 = jnp.zeros((E, D), jnp.float32)
        gamma = jnp.ones((D,), jnp.float32)
        beta = jnp.zeros((D,), jnp.float32)
        return {'x': x, 'Wr': Wr, 'br': br, 'W1': W1, 'b1': b1, 'W2': W2, 'b2': b2, 'gamma': gamma, 'beta': beta}
    _L0_ffn_all = _L0_ffn_setup()
    _L0_ffn_in = {k: v for k, v in _L0_ffn_all.items() if k in ('Wr', 'br', 'W1', 'b1', 'W2', 'b2', 'gamma', 'beta')}
    del _L0_ffn_all
    return {'x': x, 'cls_tok': cls_tok, 'L0_tok_pe_w': _L0_tok_in['pe_w'], 'L0_tok_pe_b': _L0_tok_in['pe_b'], 'L0_tok_pe_ng': _L0_tok_in['pe_ng'], 'L0_tok_pe_nb': _L0_tok_in['pe_nb'], 'L0_tok_n1g': _L0_tok_in['n1g'], 'L0_tok_n1b': _L0_tok_in['n1b'], 'L0_tok_qkv_w': _L0_tok_in['qkv_w'], 'L0_tok_qkv_b': _L0_tok_in['qkv_b'], 'L0_tok_rpb': _L0_tok_in['rpb'], 'L0_tok_proj_w': _L0_tok_in['proj_w'], 'L0_tok_proj_b': _L0_tok_in['proj_b'], 'L0_tok_n2g': _L0_tok_in['n2g'], 'L0_tok_n2b': _L0_tok_in['n2b'], 'L0_tok_w1': _L0_tok_in['w1'], 'L0_tok_b1': _L0_tok_in['b1'], 'L0_tok_w2': _L0_tok_in['w2'], 'L0_tok_b2': _L0_tok_in['b2'], 'L0_attn_a': _L0_attn_in['a'], 'L0_attn_W_B': _L0_attn_in['W_B'], 'L0_attn_b_B': _L0_attn_in['b_B'], 'L0_attn_W_C': _L0_attn_in['W_C'], 'L0_attn_b_C': _L0_attn_in['b_C'], 'L0_attn_W_D': _L0_attn_in['W_D'], 'L0_attn_b_D': _L0_attn_in['b_D'], 'L0_ffn_Wr': _L0_ffn_in['Wr'], 'L0_ffn_br': _L0_ffn_in['br'], 'L0_ffn_W1': _L0_ffn_in['W1'], 'L0_ffn_b1': _L0_ffn_in['b1'], 'L0_ffn_W2': _L0_ffn_in['W2'], 'L0_ffn_b2': _L0_ffn_in['b2'], 'L0_ffn_gamma': _L0_ffn_in['gamma'], 'L0_ffn_beta': _L0_ffn_in['beta']}

def reference(x, cls_tok, L0_tok_pe_w, L0_tok_pe_b, L0_tok_pe_ng, L0_tok_pe_nb, L0_tok_n1g, L0_tok_n1b, L0_tok_qkv_w, L0_tok_qkv_b, L0_tok_rpb, L0_tok_proj_w, L0_tok_proj_b, L0_tok_n2g, L0_tok_n2b, L0_tok_w1, L0_tok_b1, L0_tok_w2, L0_tok_b2, L0_attn_a, L0_attn_W_B, L0_attn_b_B, L0_attn_W_C, L0_attn_b_C, L0_attn_W_D, L0_attn_b_D, L0_ffn_Wr, L0_ffn_br, L0_ffn_W1, L0_ffn_b1, L0_ffn_W2, L0_ffn_b2, L0_ffn_gamma, L0_ffn_beta):
    import jax
    import jax.numpy as jnp

    def _L0_tok_ref(x, pe_w, pe_b, pe_ng, pe_nb, n1g, n1b, qkv_w, qkv_b, rpb, proj_w, proj_b, n2g, n2b, w1, b1, w2, b2):
        import jax, jax.numpy as jnp
        import numpy as np
        WS = 7
        H = W = 56
        C = 64
        NH = 8
        HD = C // NH
        SCALE = HD ** (-0.5)
        SHIFT = WS // 2
        N = WS * WS

        def _rel_pos_index():
            coords = np.stack(np.meshgrid(np.arange(WS), np.arange(WS), indexing='ij'))
            cf = coords.reshape(2, -1)
            rel = (cf[:, :, None] - cf[:, None, :]).transpose(1, 2, 0).copy()
            rel[..., 0] += WS - 1
            rel[..., 1] += WS - 1
            rel[..., 0] *= 2 * WS - 1
            return jnp.array(rel.sum(-1))

        def _attn_mask():
            img = np.zeros((H, W), np.int32)
            cnt = 0
            for h in (slice(0, -WS), slice(-WS, -SHIFT), slice(-SHIFT, None)):
                for w in (slice(0, -WS), slice(-WS, -SHIFT), slice(-SHIFT, None)):
                    cnt += 1
                    img[h, w] = cnt
            mw = img.reshape(H // WS, WS, W // WS, WS).transpose(0, 2, 1, 3).reshape(-1, N)
            diff = mw[:, None, :] - mw[:, :, None]
            return jnp.array(np.where(diff != 0, -100.0, 0.0).astype(np.float32))

        def _layernorm(x, g, b):
            m = x.mean(-1, keepdims=True)
            v = ((x - m) ** 2).mean(-1, keepdims=True)
            return (x - m) * jax.lax.rsqrt(v + 1e-05) * g + b

        def _window_partition(x):
            B = x.shape[0]
            x = x.reshape(B, H // WS, WS, W // WS, WS, C).transpose(0, 1, 3, 2, 4, 5)
            return x.reshape(-1, N, C)

        def _window_reverse(xw, B):
            x = xw.reshape(B, H // WS, W // WS, WS, WS, C).transpose(0, 1, 3, 2, 4, 5)
            return x.reshape(B, H, W, C)

        def _swin_block(x, p, shift, rpi, amask):
            B = x.shape[0]
            shortcut = x
            h = _layernorm(x, p['n1g'], p['n1b']).reshape(B, H, W, C)
            if shift > 0:
                h = jnp.roll(h, (-shift, -shift), axis=(1, 2))
            xw = _window_partition(h)
            B_ = xw.shape[0]
            qkv = (xw @ p['qkv_w'].T + p['qkv_b']).reshape(B_, N, 3, NH, HD).transpose(2, 0, 3, 1, 4)
            q, k, v = (qkv[0], qkv[1], qkv[2])
            attn = jnp.einsum('bhnd,bhmd->bhnm', q * SCALE, k)
            attn = attn + p['rpb'][rpi].transpose(2, 0, 1)[None]
            if shift > 0:
                nW = amask.shape[0]
                attn = attn.reshape(B_ // nW, nW, NH, N, N) + amask[None, :, None]
                attn = attn.reshape(B_, NH, N, N)
            attn = jax.nn.softmax(attn, axis=-1)
            o = jnp.einsum('bhnm,bhmd->bhnd', attn, v).transpose(0, 2, 1, 3).reshape(B_, N, C)
            o = o @ p['proj_w'].T + p['proj_b']
            h = _window_reverse(o, B)
            if shift > 0:
                h = jnp.roll(h, (shift, shift), axis=(1, 2))
            x = shortcut + h.reshape(B, H * W, C)
            y = _layernorm(x, p['n2g'], p['n2b'])
            y = jax.nn.gelu(y @ p['w1'].T + p['b1'], approximate=False)
            return x + y @ p['w2'].T + p['b2']
        B = x.shape[0]
        h = jax.lax.conv_general_dilated(x, pe_w, (4, 4), 'VALID', dimension_numbers=('NCHW', 'OIHW', 'NCHW'))
        h = h + pe_b[None, :, None, None]
        t = h.reshape(B, C, H * W).transpose(0, 2, 1)
        t = _layernorm(t, pe_ng, pe_nb)
        rpi = _rel_pos_index()
        amask = _attn_mask()
        for i, shift in enumerate((0, SHIFT)):
            p = {'n1g': n1g[i], 'n1b': n1b[i], 'qkv_w': qkv_w[i], 'qkv_b': qkv_b[i], 'rpb': rpb[i], 'proj_w': proj_w[i], 'proj_b': proj_b[i], 'n2g': n2g[i], 'n2b': n2b[i], 'w1': w1[i], 'b1': b1[i], 'w2': w2[i], 'b2': b2[i]}
            t = _swin_block(t, p, shift, rpi, amask)
        return t

    def _L0_attn_ref(u, a, W_B, b_B, W_C, b_C, W_D, b_D):
        import jax, jax.numpy as jnp
        import numpy as np
        from jax import lax

        def _solve_im(u, a, W_B, b_B, dt):
            s = 1.0 / (1.0 + dt * dt * a)
            Bu = jnp.einsum('bnq,pq->bnp', u, W_B) + b_B
            f_x = dt * s * Bu
            f_z = dt * dt * s * Bu
            dsa = dt * s * a
            ds = dt * s

            def step(carry, f):
                x, z = carry
                fx, fz = f
                x_new = s * x - dsa * z + fx
                z_new = ds * x + s * z + fz
                return ((x_new, z_new), z_new)
            Bsz, _, q = u.shape
            init = (jnp.zeros((Bsz, q), u.dtype), jnp.zeros((Bsz, q), u.dtype))
            _, z_t = lax.scan(step, init, (jnp.moveaxis(f_x, 1, 0), jnp.moveaxis(f_z, 1, 0)))
            return jnp.moveaxis(z_t, 0, 1)

        def _reference_tuple_inner(u, a, W_B, b_B, W_C, b_C, W_D, b_D):
            N = u.shape[1]
            dt = 1.0 / N
            y = _solve_im(u, a, W_B, b_B, dt)
            x = jnp.einsum('bnq,pq->bnp', y, W_C) + b_C + (jnp.einsum('bnq,pq->bnp', u, W_D) + b_D)
            x = jax.nn.gelu(x, approximate=False)
            out = x * jax.nn.sigmoid(x) + u
            return (out, y)
        return _reference_tuple_inner(u, a, W_B, b_B, W_C, b_C, W_D, b_D)[0]

    def _L0_ffn_ref(x, Wr, br, W1, b1, W2, b2, gamma, beta):
        import math
        import jax, jax.numpy as jnp
        import numpy as np
        CAPACITY_FACTOR = 1.25
        TOP_K = 2
        LN_EPS = 1e-05

        def _layer_norm(x, gamma, beta):
            mu = jnp.mean(x, axis=-1, keepdims=True)
            var = jnp.var(x, axis=-1, keepdims=True)
            return (x - mu) * jax.lax.rsqrt(var + LN_EPS) * gamma + beta
        B, S, D = x.shape
        E = Wr.shape[1]
        N = B * S
        K = TOP_K
        logits = jnp.mean(x, axis=1) @ Wr + br
        routing_weights = jax.nn.softmax(logits, axis=-1)
        capacity = float(math.ceil(N * CAPACITY_FACTOR / E))
        expected_loads = routing_weights.sum(axis=0) * (N / B)
        scale = jnp.where(expected_loads > capacity, capacity / expected_loads, 1.0)
        routing_weights = jax.nn.softmax(routing_weights * scale, axis=-1)
        rw_tok = jnp.broadcast_to(routing_weights[:, None, :], (B, S, E)).reshape(N, E)
        top_w, top_i = jax.lax.top_k(rw_tok, K)
        top_w = jax.nn.softmax(top_w, axis=-1)
        xf = x.reshape(N, D)
        h = jax.nn.gelu(jnp.einsum('nd,edf->enf', xf, W1) + b1[:, None, :], approximate=False)
        y = jnp.einsum('enf,efd->end', h, W2) + b2[:, None, :]
        w_dense = jnp.zeros((N, E), x.dtype).at[jnp.arange(N)[:, None], top_i].add(top_w)
        out = jnp.einsum('ne,end->nd', w_dense, y).reshape(B, S, D)
        out = _layer_norm(out + x, gamma, beta)
        return out
    h = _L0_tok_ref(x, L0_tok_pe_w, L0_tok_pe_b, L0_tok_pe_ng, L0_tok_pe_nb, L0_tok_n1g, L0_tok_n1b, L0_tok_qkv_w, L0_tok_qkv_b, L0_tok_rpb, L0_tok_proj_w, L0_tok_proj_b, L0_tok_n2g, L0_tok_n2b, L0_tok_w1, L0_tok_b1, L0_tok_w2, L0_tok_b2)
    h = jnp.concatenate([jnp.broadcast_to(cls_tok, (h.shape[0], 1, h.shape[2])), h], axis=1)
    h = h + _L0_attn_ref(_layernorm(h, axis=-1), L0_attn_a, L0_attn_W_B, L0_attn_b_B, L0_attn_W_C, L0_attn_b_C, L0_attn_W_D, L0_attn_b_D)
    h = h + _L0_ffn_ref(_layernorm(h, axis=-1), L0_ffn_Wr, L0_ffn_br, L0_ffn_W1, L0_ffn_b1, L0_ffn_W2, L0_ffn_b2, L0_ffn_gamma, L0_ffn_beta)
    return h

_drawn_inputs = setup_inputs


def setup_inputs(seed=0):
    import zlib

    import numpy as np

    out = dict(_drawn_inputs(seed))
    spreads = {'L0_tok_pe_b': (0.0, 0.1),
     'L0_tok_pe_ng': (1.0, 0.2),
     'L0_tok_pe_nb': (0.0, 0.1),
     'L0_tok_n1g': (1.0, 0.6),
     'L0_tok_n1b': (0.0, 0.8),
     'L0_tok_qkv_b': (0.0, 0.44),
     'L0_tok_proj_b': (0.0, 0.1),
     'L0_tok_n2g': (1.0, 0.6),
     'L0_tok_n2b': (0.0, 0.8),
     'L0_tok_b1': (0.0, 0.375),
     'L0_tok_b2': (0.0, 0.1),
     'L0_ffn_br': (0.0, 2.0),
     'L0_ffn_b1': (0.0, 0.521),
     'L0_ffn_b2': (0.0, 0.36),
     'L0_ffn_gamma': (1.0, 0.2),
     'L0_ffn_beta': (0.0, 0.1)}
    factors = {'cls_tok': 94.527,
     'L0_tok_rpb': 200.0,
     'L0_attn_a': 8.0,
     'L0_attn_b_B': 6.282,
     'L0_ffn_Wr': 8.0}
    for name, (base, spread) in spreads.items():
        noise = np.random.default_rng([zlib.crc32(name.encode()), seed]).standard_normal(out[name].shape)
        drawn = base * np.exp(spread * noise) if base else spread * noise
        out[name] = jnp.asarray(drawn.astype(out[name].dtype))
    for name, factor in factors.items():
        out[name] = (out[name] * factor).astype(out[name].dtype)
    return out
```

```python
from contextlib import ExitStack

import numpy as np

import concourse.bass as bass
from concourse import mybir

F32 = mybir.dt.float32
BF16 = mybir.dt.bfloat16
ALU = mybir.AluOpType
ACT = mybir.ActivationFunctionType
AX = mybir.AxisListType
ds = bass.ds

P = 128
C = 64
NH, HD = 8, 8
WS, SHIFT = 7, 3
TOK = WS * WS
NW = 8
SIDE = WS * NW
U = NW * NW
TILES = 2 * U
HID = 4 * C
EPS = 1e-5
SCALE = HD ** -0.5
PATCH = 16
ROW = C + 2
PAD = SIDE + SHIFT
N_EXP, FF = 8, 128
TIME = SIDE * SIDE
SEQ = TIME + 1
CAPACITY = float(-(-4 * SEQ * 5 // (4 * N_EXP)))
DT = 1.0 / SEQ

BLOCK_COLS = [("qBD", P), ("kBD", P), ("vBD", P), ("pBD", P), ("w1T0", HID), ("w1T1", HID), ("w2T", 2 * C),
              ("n1g", 1), ("n1b", 1), ("qb", 1), ("kb", 1), ("vb", 1), ("n2g", 1), ("n2b", 1), ("b1", 2),
              ("b2", 1), ("pb_row", C)]
COMMON_COLS = [("ident", P), ("mean_ones", P), ("head_mask", NH), ("pg_row", C), ("pbeta_row", C)]
TAIL_COLS = [("BBD", P), ("CBD", P), ("DBD", P), ("a", 1), ("bB", 1), ("bC", 1), ("bD", 1), ("cls", 1),
             ("Wr", N_EXP), ("br_row", 2 * N_EXP), ("gamma", 1), ("beta", 1), ("b2T", N_EXP), ("b1T", N_EXP),
             ("group_ones", P), ("all_ones", P), ("pick0", P), ("pick1", P), ("index_row", N_EXP)]


def columns(cols):
    at, out = 0, {}
    for name, n in cols:
        out[name] = (at, n)
        at += n
    return out, at


BLOCK_AT, BLOCK_W = columns(BLOCK_COLS)
COMMON_AT, COMMON_W = columns(COMMON_COLS)
TAIL_AT, TAIL_W = columns(TAIL_COLS)


def live(u, n=U):
    return not isinstance(u, int) or 0 <= u < n


def wait(eng, sem, value):
    if isinstance(value, int) and value <= 0:
        return
    eng.wait_ge(sem, value)


def skewed(eng, step, first, last):
    for s in range(first, NW):
        step(s, s % NW)
    with eng.Fori(1, NW - 1) as row:
        for c in range(NW):
            step(row * NW + c, c)
    for s in range(NW * (NW - 1), last + 1):
        step(s, s % NW)


def build(nc, patches, patch_w, common_in, block_in, bias_in, mask_in, tail_in, ew1_in, ew2_in, out, debug=None):
    ctx = ExitStack()
    with ctx:
        def sb(name, shape, dt=F32):
            return ctx.enter_context(nc.sbuf_tensor(name, shape, dt))

        X = sb("X", [P, TILES, ROW])
        X2 = sb("X2", [P, TILES, ROW])
        XT = sb("XT", [P, 2, PAD, PAD])
        common = sb("common", [P, COMMON_W])
        block_w = [sb(f"block_w{b}", [P, BLOCK_W]) for b in range(2)]

        def con(name):
            at, n = COMMON_AT[name]
            return common[:, at:at + n]

        def wt(b, name):
            at, n = BLOCK_AT[name]
            return block_w[b][:, at:at + n]

        load_and_embed(nc, X, X2, common, block_w, con, patches, patch_w, common_in, block_in)
        attention(nc, 0, X, con, wt, bias_in, mask_in)
        mlp(nc, 0, X, con, wt, None)
        if debug == "m0":
            return dump(nc, X, out)
        roll(nc, X, X2)
        attention(nc, 1, X2, con, wt, bias_in, mask_in)
        if debug == "a1":
            return dump(nc, X2, out)
        mlp(nc, 1, X2, con, wt, XT)
        if debug == "m1":
            return dump(nc, XT, out)
        tail(nc, ctx, X, X2, XT, con, tail_in, ew1_in, ew2_in, out, debug)


def clear_spent(nc):
    spent = sorted(nc.released_uncleared_semaphores)
    while spent:
        first = last = spent.pop(0)
        while spent and spent[0] == last + 1:
            last = spent.pop(0)
        nc.gpsimd.sem_clear(range(first, last + 1))


def dump(nc, T, out):
    with nc.semaphore("dumped") as s, nc.Block() as block:
        @block.sync
        def _(sp):
            sp.dma_start(out, T[:]).then_inc(s, 16)
            sp.wait_ge(s, 16)


def load_and_embed(nc, X, X2, common, block_w, con, patches, patch_w, common_in, block_in):
    with ExitStack() as ctx:
        sb = lambda name, shape, dt=F32: ctx.enter_context(nc.sbuf_tensor(name, shape, dt))
        pb = lambda name, shape, dt=F32: ctx.enter_context(nc.psum_tensor(name, shape, dt))
        sem = lambda name: ctx.enter_context(nc.semaphore(name))
        G4 = 4
        STEPS = TILES // G4
        pw = sb("pw", [PATCH + 1, C])
        pw_mean = sb("pw_mean", [PATCH + 1, 1])
        pw_c = sb("pw_c", [PATCH + 1, C])
        ring = [sb(f"patch_ring{i}", [PATCH + 1, G4 * P]) for i in range(2)]
        sq = [sb(f"sq{i}", [P, C]) for i in range(2)]
        var = [sb(f"pvar{i}", [P, G4]) for i in range(2)]
        ve = [sb(f"pve{i}", [P, G4]) for i in range(2)]
        rs = [sb(f"prs{i}", [P, G4]) for i in range(2)]
        half = sb("phalf", [P, G4])
        eps = sb("peps", [P, G4])
        st = [sb(f"pst{i}", [P, G4, 6]) for i in range(2)]
        mv = [sb(f"pmv{i}", [P, G4, 2]) for i in range(2)]
        gained = [sb(f"gained{i}", [P, G4, C]) for i in range(2)]
        ps = [pb(f"pe_ps{i}", [P, 512]) for i in range(2)]

        weights_in = sem("weights_in")
        pw_in = sem("pw_in")
        patch_in = [sem("patch_in0"), sem("patch_in1")]
        consts = sem("consts")
        pw_m = sem("pw_m")
        pw_ready = sem("pw_ready")
        embedded = sem("embedded")
        squared = sem("squared")
        ve_ready = sem("ve_ready")
        rs_ready = sem("rs_ready")
        scaled = sem("scaled")
        placed = sem("placed")
        stats = sem("stats")
        aggregated = sem("aggregated")
        kept = sem("kept")
        with nc.Block() as block:
            @block.sync
            def _(sp):
                sp.dma_start(pw[:], patch_w).then_inc(pw_in, 16)

                def load(i, p):
                    sp.dma_start(ring[p][:], patches[ds(i, 1), :, :].rearrange("o p n -> (o p) n")).then_inc(patch_in[p], 16)

                load(0, 0)
                load(1, 1)
                sp.dma_start(common[:], common_in).then_inc(weights_in, 16)
                for b in range(2):
                    sp.dma_start(block_w[b][:], block_in[b]).then_inc(weights_in, 16)
                with sp.Fori(1, STEPS // 2) as i:
                    for p in range(2):
                        sp.wait_ge(embedded, 2 * i + p - 1)
                        load(2 * i + p, p)
                sp.wait_ge(weights_in, 48)

            @block.tensor
            def _(pe):
                pe.wait_ge(pw_ready, 1)

                def step(s, i, p):
                    pe.wait_ge(patch_in[p], 16 * i + 16)
                    wait(pe, squared, G4 * (s - 1))
                    wait(pe, scaled, s - 1)
                    for t in range(G4):
                        last = nc.tensor.matmul(ps[p][:, t * C:(t + 1) * C], ring[p][:, t * P:(t + 1) * P], pw_c[:],
                                                start=True, stop=True)
                    last.then_inc(embedded, 1)

                step(0, 0, 0)
                step(1, 0, 1)
                with pe.Fori(1, STEPS // 2) as i:
                    for p in range(2):
                        step(2 * i + p, i, p)

            @block.scalar
            def _(act):
                def step(s, p):
                    act.wait_ge(embedded, s + 1)
                    wait(act, ve_ready, s - 1)
                    for t in range(G4):
                        wait(act, squared, G4 * s + t - 1)
                        nc.scalar.activation(sq[t % 2][:], ps[p][:, t * C:(t + 1) * C], ACT.Square, scale=C ** -0.5,
                                             accum_out=var[p][:, t:t + 1]).then_inc(squared, 1)

                step(0, 0)
                step(1, 1)
                with act.Fori(1, STEPS // 2) as i:
                    for p in range(2):
                        step(2 * i + p, p)

            @block.gpsimd
            def _(pool):
                nc.gpsimd.memset(half[:], -0.5).then_inc(consts, 1)
                nc.gpsimd.memset(eps[:], EPS).then_inc(consts, 1)
                nc.gpsimd.memset(X2[:], 0.0).then_inc(consts, 1)
                pool.wait_ge(consts, 3)
                pool.wait_ge(weights_in, 48)
                offset = con("pbeta_row").unsqueeze(1).to_broadcast([P, G4, C])

                def step(s, p):
                    pool.wait_ge(squared, G4 * s + G4)
                    nc.gpsimd.tensor_tensor(ve[p][:], var[p][:], eps[:], ALU.add).then_inc(ve_ready, 1)
                    pool.wait_ge(ve_ready, s + 1)
                    wait(pool, scaled, s - 1)
                    nc.gpsimd.tensor_tensor(rs[p][:], ve[p][:], half[:], ALU.pow).then_inc(rs_ready, 1)
                    pool.wait_ge(scaled, s + 1)
                    nc.gpsimd.tensor_tensor(X[:, ds(s * G4, G4), 0:C], gained[p][:], offset, ALU.add).then_inc(placed, 1)

                step(0, 0)
                step(1, 1)
                with pool.Fori(1, STEPS // 2) as i:
                    for p in range(2):
                        step(2 * i + p, p)

            @block.vector
            def _(dve):
                dve.wait_ge(pw_in, 16)
                nc.vector.reduce_sum(pw_mean[:], pw[:], AX.X).then_inc(pw_m, 1)
                dve.wait_ge(pw_m, 1)
                nc.vector.tensor_scalar(pw_mean[:], pw_mean[:], 1.0 / C, None, ALU.mult).then_inc(pw_m, 1)
                dve.wait_ge(pw_m, 2)
                nc.vector.tensor_scalar(pw_c[:], pw[:], pw_mean[:, 0:1], None, ALU.subtract).then_inc(pw_ready, 1)
                dve.wait_ge(weights_in, 48)
                gain = con("pg_row")

                def step(s, p):
                    if live(s, STEPS):
                        dve.wait_ge(rs_ready, s + 1)
                    wait(dve, placed, min(s, STEPS) if isinstance(s, int) else s)
                    wait(dve, stats, min(s - 1, STEPS) if isinstance(s, int) else s - 1)
                    if live(s, STEPS):
                        for t in range(G4):
                            last = nc.vector.scalar_tensor_tensor(gained[p][:, t, :], ps[p][:, t * C:(t + 1) * C],
                                                                  rs[p][:, t:t + 1], gain, ALU.mult, ALU.mult)
                        last.then_inc(scaled, 1)
                    if live(s - 3, STEPS):
                        dve.wait_ge(aggregated, s - 2)
                        wait(dve, kept, s - 3)
                        nc.vector.tensor_scalar(X[:, ds((s - 3) * G4, G4), C:ROW], mv[1 - p][:], 1.0, None, ALU.mult).then_inc(kept, 1)
                    if live(s - 1, STEPS):
                        for t in range(G4):
                            last = nc.vector.bn_stats(st[1 - p][:, t, :], X[:, ds((s - 1) * G4 + t, 1), 0:C].rearrange("p o c -> p (o c)"))
                        last.then_inc(stats, 1)
                    if live(s - 2, STEPS):
                        for t in range(G4):
                            last = nc.vector.bn_aggr(mv[p][:, t, :], st[p][:, t, :])
                        last.then_inc(aggregated, 1)

                for s in range(4):
                    step(s, s % 2)
                with dve.Fori(2, STEPS // 2) as i:
                    for p in range(2):
                        step(2 * i + p, p)
                for s in range(STEPS, STEPS + 3):
                    step(s, s % 2)


def finalize_stats(nc, ctx, prefix, T):
    sb = lambda name, shape, dt=F32: ctx.enter_context(nc.sbuf_tensor(prefix + name, shape, dt))
    sem = lambda name: ctx.enter_context(nc.semaphore(prefix + name))
    rstd, nmr, ve, half = sb("rstd", [P, TILES]), sb("nmr", [P, TILES]), sb("ve", [P, TILES]), sb("half", [P, TILES])
    half_set, ve_ready, rstd_ready, nmr_ready = sem("half_set"), sem("ve_ready"), sem("rstd_ready"), sem("nmr_ready")
    mean, var = T[:, :, C:C + 1].rearrange("p t o -> p (t o)"), T[:, :, C + 1:ROW].rearrange("p t o -> p (t o)")

    def on_pool(pool):
        nc.gpsimd.memset(half[:], -0.5).then_inc(half_set, 1)
        nc.gpsimd.tensor_scalar(ve[:], var, 1.0, EPS, ALU.mult, ALU.add).then_inc(ve_ready, 1)
        pool.wait_ge(half_set, 1)
        pool.wait_ge(ve_ready, 1)
        nc.gpsimd.tensor_tensor(rstd[:], ve[:], half[:], ALU.pow).then_inc(rstd_ready, 1)
        pool.wait_ge(nmr_ready, 1)

    def on_vector(dve):
        dve.wait_ge(rstd_ready, 1)
        nc.vector.scalar_tensor_tensor(nmr[:], mean, -1.0, rstd[:], ALU.mult, ALU.mult).then_inc(nmr_ready, 1)
        dve.wait_ge(nmr_ready, 1)

    return rstd, nmr, half_set, on_pool, on_vector


def attention(nc, b, X, con, wt, bias_in, mask_in):
    with ExitStack() as ctx:
        sb = lambda name, shape, dt=F32: ctx.enter_context(nc.sbuf_tensor(f"at{b}_{name}", shape, dt))
        pb = lambda name, shape, dt=F32: ctx.enter_context(nc.psum_tensor(f"at{b}_{name}", shape, dt))
        sem = lambda name: ctx.enter_context(nc.semaphore(f"at{b}_{name}"))
        NV = 4 if b else 1
        KH = NH * TOK

        raw_bias = sb("raw_bias", [P, KH])
        mask = sb("mask", [P, 4, TOK])
        full = sb("full", [P, KH])
        mid_all = sb("mid_all", [P, KH], BF16)
        hi_all = sb("hi_all", [P, KH], BF16)
        rest = sb("rest", [P, KH])
        rest2 = sb("rest2", [P, KH])
        t_hi_mid = sb("t_hi_mid", [P, NV, KH], BF16)
        t_lo = sb("t_lo", [P, NV, KH], BF16)
        select = sb("select", [P, P], BF16)
        qbs = sb("qbs", [P, 1])
        vb_wide = sb("vb_wide", [C, P])
        const_row = sb("const_row", [P, C])
        xn = [sb(f"xn{i}", [P, 2, C]) for i in range(2)]
        xT = [sb(f"xT{i}", [P, 2, 2, C]) for i in range(2)]
        q_bd = [sb(f"q_bd{i}", [P, 2, 2, C]) for i in range(2)]
        k_sb = sb("k_sb", [P, 2, TOK])
        k_bd = [sb(f"k_bd{i}", [P, 2, NH, TOK]) for i in range(2)]
        v_bd = [sb(f"v_bd{i}", [P, 2, 2, NH // 2, 2, HD + 1]) for i in range(2)]
        prob = [sb(f"prob{w}", [P, NH, C]) for w in range(2)]
        mx = [sb(f"mx{w}", [P, NH]) for w in range(2)]
        probT = [sb(f"probT{w}", [P, NH // 2, P]) for w in range(2)]
        rsum = sb("rsum", [P, 2 * NH // 2, 2])
        o = sb("o", [P, 2, C])
        oT = sb("oT", [P, P])
        st = [sb(f"st{i}", [P, 2, 6]) for i in range(2)]
        mv = [sb(f"mv{i}", [P, 2, 2]) for i in range(2)]

        ps_xt = pb("ps_xt", [P, 512])
        ps_qkv = pb("ps_qkv", [P, 512])
        ps_s = [pb(f"ps_s{w}", [P, 512]) for w in range(2)]
        ps_pt = [pb(f"ps_pt{w}", [P, 512]) for w in range(2)]
        ps_o = pb("ps_o", [P, 512])
        ps_misc = pb("ps_misc", [P, 512])
        PS_Q, PS_K, PS_V = 0, 2 * TOK, 4 * TOK
        PS_V = 256

        bias_loaded = sem("bias_loaded")
        zeroed = sem("zeroed")
        table_step = sem("table_step")
        tables = sem("tables")
        const_ps = sem("const_ps")
        const_ready = sem("const_ready")
        xn_ready = sem("xn_ready")
        offset_added = sem("offset_added")
        xt_ps = sem("xt_ps")
        xt_ready = sem("xt_ready")
        qkv_ps = sem("qkv_ps")
        k_ready = sem("k_ready")
        q_ready = sem("q_ready")
        kbd_ready = sem("kbd_ready")
        v_ready = sem("v_ready")
        s_ps = sem("s_ps")
        max_ready = sem("max_ready")
        shifted = sem("shifted")
        exp_ready = sem("exp_ready")
        pt_ps = sem("pt_ps")
        pt_ready = sem("pt_ready")
        pv_ps = sem("pv_ps")
        rsum_ready = sem("rsum_ready")
        o_ready = sem("o_ready")
        ot_ps = sem("ot_ps")
        ot_ready = sem("ot_ready")
        pr_ps = sem("pr_ps")
        x_ready = sem("x_ready")
        stats = sem("stats")
        aggr = sem("aggr")
        kept = sem("kept")
        rstd, nmr, half_set, stats_on_pool, stats_on_vector = finalize_stats(nc, ctx, f"at{b}_", X)

        with nc.Block() as block:
            @block.sync
            def _(sp):
                sp.dma_start(raw_bias[:], bias_in[b]).then_inc(bias_loaded, 16)
                sp.dma_start(mask[:], mask_in).then_inc(bias_loaded, 16)

            @block.gpsimd
            def _(pool):
                stats_on_pool(pool)
                mask_h = con("head_mask").unsqueeze(2).to_broadcast([P, NH, TOK])
                pool.wait_ge(const_ready, 1)
                row = const_row[:].unsqueeze(1).to_broadcast([P, 2, C])

                def step(s, c):
                    p = c % 2
                    if live(s + 1):
                        pool.wait_ge(k_ready, s + 2)
                        wait(pool, s_ps, 2 * s)
                        for w in range(2):
                            nc.gpsimd.tensor_tensor(k_bd[1 - p][:, w, :, :],
                                                    k_sb[:, w, :].unsqueeze(1).to_broadcast([P, NH, TOK]), mask_h,
                                                    ALU.mult).then_inc(kbd_ready, 1)
                    if live(s + 3):
                        pool.wait_ge(xn_ready, s + 4)
                        pool.wait_ge(const_ready, 1)
                        xs = X[:, ds((s + 3) * 2, 2), 0:C]
                        nc.gpsimd.tensor_tensor(xs, xs, row, ALU.add).then_inc(offset_added, 1)

                skewed(pool, step, -3, U + 1)

            @block.tensor
            def _(pe):
                pe.wait_ge(zeroed, 1)
                nc.tensor.matmul(ps_misc[:, 0:C], vb_wide[:], wt(b, "pBD")[0:C, 0:C], start=True, stop=True).then_inc(const_ps, 1)
                pe.wait_ge(const_ready, 1)
                pe.wait_ge(tables, NV)

                def scores(s, c, w):
                    p = c % 2
                    pe.wait_ge(kbd_ready, 2 * s + w + 1)
                    if w == 0:
                        pe.wait_ge(q_ready, s + 1)
                    wait(pe, shifted, 2 * s + w - 1)
                    v = 0
                    if b:
                        v = (1 if c == NW - 1 else 0) + (2 if isinstance(s, int) and s >= U - NW else 0)
                    nc.tensor.matmul(ps_s[w][:, 0:KH], select[:], t_hi_mid[:, v, :], start=True, stop=False)
                    nc.tensor.matmul(ps_s[w][:, 0:KH], select[:], t_lo[:, v, :], start=False, stop=False)
                    nc.tensor.matmul(ps_s[w][:, 0:KH], q_bd[p][:, w, :, :].rearrange("p g q -> p (g q)"),
                                     k_bd[p][:, w, :, :].rearrange("p h k -> p (h k)"),
                                     start=False, stop=True).then_inc(s_ps, 1)

                def transpose_probs(u, w):
                    pe.wait_ge(exp_ready, 2 * u + w + 1)
                    wait(pe, pt_ready, 2 * u + w - 1)
                    for hp in range(NH // 2):
                        last = nc.tensor.transpose(ps_pt[w][:, hp * P:(hp + 1) * P],
                                                   prob[w][:, 2 * hp:2 * hp + 2, :].rearrange("p h k -> p (h k)"), con("ident"))
                    last.then_inc(pt_ps, 1)

                def attend(u, p, w):
                    pe.wait_ge(pt_ready, 2 * u + w + 1)
                    if w == 0:
                        pe.wait_ge(v_ready, u + 1)
                        wait(pe, o_ready, u)
                    for hp in range(NH // 2):
                        at = (w * 4 + hp) * 4 * (HD + 1)
                        last = nc.tensor.matmul(ps_o[:, at:at + 4 * (HD + 1)].rearrange("p (g e) -> p g e", g=2),
                                                probT[w][:, hp, :],
                                                v_bd[p][:, w, :, hp, :, :].rearrange("p g h e -> p g (h e)"),
                                                start=True, stop=True)
                    last.then_inc(pv_ps, 1)

                def step(s, c):
                    p = c % 2
                    if live(s):
                        scores(s, c, 0)
                    if live(s - 2):
                        pe.wait_ge(o_ready, s - 1)
                        wait(pe, x_ready, s - 2)
                        nc.tensor.transpose(ps_misc[:, 0:P], o[:].rearrange("p w c -> p (w c)"), con("ident")).then_inc(ot_ps, 1)
                    if live(s - 1):
                        transpose_probs(s - 1, 1)
                    if live(s + 1):
                        pe.wait_ge(xt_ready, s + 2)
                        wait(pe, v_ready, s + 1)
                        wait(pe, q_ready, s + 1)
                        tokens = xT[1 - p][:, :, 0, 0:TOK]
                        for at, name in ((PS_Q, "qBD"), (PS_K, "kBD")):
                            nc.tensor.matmul(ps_qkv[:, at:at + 2 * TOK].rearrange("p (w t) -> p w t", w=2), wt(b, name), tokens,
                                             start=True, stop=True)
                        for w in range(2):
                            twice = xT[1 - p][:, w, :, :].rearrange("p a t -> p (a t)")
                            last = nc.tensor.matmul(ps_qkv[:, PS_V + w * P:PS_V + (w + 1) * P], twice,
                                                    wt(b, "vBD"), start=True, stop=True)
                        last.then_inc(qkv_ps, 1)
                    if live(s - 1):
                        attend(s - 1, 1 - p, 0)
                    if live(s - 2):
                        pe.wait_ge(ot_ready, s - 1)
                        for w in range(2):
                            r = slice(C * w, C * w + C)
                            for g in range(2):
                                last = nc.tensor.matmul(ps_misc[r, P + g * C:P + (g + 1) * C], oT[:, C * g:C * g + C],
                                                        wt(b, "pBD")[:, r], start=True, stop=True)
                        last.then_inc(pr_ps, 1)
                    if live(s):
                        scores(s, c, 1)
                    if live(s + 2):
                        pe.wait_ge(xn_ready, s + 3)
                        wait(pe, xt_ready, s + 2)
                        nc.tensor.transpose(ps_xt[:, 0:P], xn[p][:].rearrange("p g c -> p (g c)"), con("ident")).then_inc(xt_ps, 1)
                    if live(s - 1):
                        attend(s - 1, 1 - p, 1)
                    if live(s):
                        transpose_probs(s, 0)

                skewed(pe, step, -2, U + 1)

            @block.scalar
            def _(act):
                def copy_probs(u, w):
                    act.wait_ge(pt_ps, 2 * u + w + 1)
                    wait(act, pv_ps, 2 * u + w - 1)
                    nc.scalar.activation(probT[w][:], ps_pt[w][:].rearrange("p (h q) -> p h q", q=P), ACT.Copy).then_inc(pt_ready, 1)

                def exponential(u, w):
                    act.wait_ge(shifted, 2 * u + w + 1)
                    e = prob[w][:, :, 0:TOK]
                    nc.scalar.activation(e, e, ACT.Exp).then_inc(exp_ready, 1)

                def step(s, c):
                    p = c % 2
                    if live(s - 2):
                        act.wait_ge(ot_ps, s - 1)
                        wait(act, pr_ps, s - 2)
                        nc.scalar.activation(oT[:], ps_misc[:, 0:P], ACT.Copy).then_inc(ot_ready, 1)
                    if live(s - 1):
                        copy_probs(s - 1, 1)
                    if live(s + 1):
                        act.wait_ge(qkv_ps, s + 2)
                        wait(act, kbd_ready, 2 * s + 2)
                        nc.scalar.activation(k_sb[:], ps_qkv[:, PS_K:PS_K + 2 * TOK].rearrange("p (w t) -> p w t", w=2),
                                             ACT.Identity, bias=wt(b, "kb")).then_inc(k_ready, 1)
                        wait(act, s_ps, 2 * s)
                        for g in range(2):
                            r = slice(C * g, C * g + C)
                            last = nc.scalar.activation(q_bd[1 - p][r, :, g, 0:TOK],
                                                        ps_qkv[r, PS_Q:PS_Q + 2 * TOK].rearrange("p (w t) -> p w t", w=2),
                                                        ACT.Identity, bias=qbs[r, :], scale=SCALE)
                        last.then_inc(q_ready, 1)
                    if live(s):
                        exponential(s, 0)
                    if live(s + 2):
                        act.wait_ge(xt_ps, s + 3)
                        wait(act, qkv_ps, s + 1)
                        nc.scalar.activation(xT[p][:], ps_xt[:, 0:P].rearrange("p (w t) -> p w t", w=2).unsqueeze(2)
                                             .to_broadcast([P, 2, 2, C]), ACT.Identity,
                                             bias=wt(b, "n1b"), scale=wt(b, "n1g")).then_inc(xt_ready, 1)
                    if live(s):
                        copy_probs(s, 0)
                        exponential(s, 1)
                    if live(s + 1):
                        wait(act, pv_ps, 2 * s)
                        for h in range(2):
                            r = slice(C * h, C * h + C)
                            src = ps_qkv[r, PS_V:PS_V + 4 * C].rearrange("p (x a h d) -> p x a h d", a=NH // 2, h=2, d=HD)[:, :, :, h, :]
                            last = nc.scalar.activation(v_bd[1 - p][r, :, :, :, h, 0:HD].rearrange("p w g a d -> p (w g) a d"), src, ACT.Copy)
                        last.then_inc(v_ready, 1)

                act.wait_ge(zeroed, 1)
                skewed(act, step, -2, U + 1)

            @block.vector
            def _(dve):
                for i in range(2):
                    nc.vector.memset(q_bd[i][:], 0.0)
                    nc.vector.memset(v_bd[i][:], 0.0)
                    nc.vector.memset(prob[i][:], 0.0)
                nc.vector.tensor_scalar(qbs[:], wt(b, "qb"), SCALE, None, ALU.mult)
                nc.vector.tensor_copy(vb_wide[:], wt(b, "vb")[0:C, :].to_broadcast([C, P]))
                nc.vector.tensor_copy(select[:].rearrange("p (g q) -> p g q", g=2)[0:C],
                                      con("ident")[0:C, 0:C].unsqueeze(1).to_broadcast([C, 2, C]))
                nc.vector.tensor_copy(select[:].rearrange("p (g q) -> p g q", g=2)[C:P],
                                      con("ident")[C:P, C:P].unsqueeze(1).to_broadcast([C, 2, C]))
                nc.vector.memset(t_lo[:], 0.0).then_inc(table_step, 1)
                dve.wait_ge(table_step, 1)
                for i in range(2):
                    for h in range(2):
                        last = nc.vector.memset(v_bd[i][C * h:C * h + C, :, :, :, h, HD:HD + 1], 1.0)
                last.then_inc(zeroed, 1)
                dve.wait_ge(const_ps, 1)
                nc.vector.tensor_tensor(const_row[:], ps_misc[:, 0:C], wt(b, "pb_row"), ALU.add).then_inc(const_ready, 1)
                dve.wait_ge(bias_loaded, 32)
                chain = [1]

                def link(ins):
                    chain[0] += 1
                    ins.then_inc(table_step, 1)
                    dve.wait_ge(table_step, chain[0])

                for v in range(NV):
                    link(nc.vector.tensor_tensor(full[:].rearrange("p (h k) -> p h k", h=NH), raw_bias[:].rearrange("p (h k) -> p h k", h=NH),
                                                 mask[:, v, :].unsqueeze(1).to_broadcast([P, NH, TOK]), ALU.add))
                    link(nc.vector.tensor_copy(hi_all[:], full[:]))
                    link(nc.vector.tensor_tensor(rest[:], full[:], hi_all[:], ALU.subtract))
                    link(nc.vector.tensor_copy(mid_all[:], rest[:]))
                    link(nc.vector.tensor_tensor(rest2[:], rest[:], mid_all[:], ALU.subtract))
                    nc.vector.tensor_copy(t_hi_mid[0:C, v, :], hi_all[0:C, :])
                    nc.vector.tensor_copy(t_hi_mid[C:P, v, :], mid_all[C:P, :])
                    nc.vector.tensor_copy(t_lo[0:C, v, :], rest2[0:C, :]).then_inc(tables, 1)
                stats_on_vector(dve)

                def normalize(dve, u, p):
                    wait(dve, xt_ps, u - 1)
                    for g in range(2):
                        last = nc.vector.tensor_scalar(xn[p][:, g, :], X[:, ds(2 * u + g, 1), 0:C].rearrange("p o c -> p (o c)"),
                                                       rstd[:, ds(2 * u + g, 1)], nmr[:, ds(2 * u + g, 1)], ALU.mult, ALU.add)
                    last.then_inc(xn_ready, 1)

                def statistics(u, p):
                    for g in range(2):
                        last = nc.vector.bn_stats(st[p][:, g, :], X[:, ds(2 * u + g, 1), 0:C].rearrange("p o c -> p (o c)"))
                    last.then_inc(stats, 1)

                def aggregate(u, p):
                    for g in range(2):
                        last = nc.vector.bn_aggr(mv[p][:, g, :], st[p][:, g, :])
                    last.then_inc(aggr, 1)

                def keep(u, p):
                    dve.wait_ge(aggr, u + 1)
                    wait(dve, kept, u)
                    nc.vector.tensor_scalar(X[:, ds(2 * u, 2), C:ROW], mv[p][:], 1.0, None, ALU.mult).then_inc(kept, 1)

                def shift(s, w, more=()):
                    dve.wait_ge(s_ps, 2 * s + w + 1)
                    sc = ps_s[w][:, 0:KH].rearrange("p (h k) -> p h k", h=NH)
                    nc.vector.reduce_max(mx[w][:], sc, AX.X).then_inc(max_ready, 1)
                    for sem_, value in more:
                        wait(dve, sem_, value)
                    dve.wait_ge(max_ready, 2 * s + w + 1)
                    wait(dve, pt_ps, 2 * s + w - 1)
                    nc.vector.tensor_tensor(prob[w][:, :, 0:TOK], sc, mx[w][:].unsqueeze(2).to_broadcast([P, NH, TOK]),
                                            ALU.subtract).then_inc(shifted, 1)

                def step(s, c):
                    p = c % 2
                    settled = ((x_ready, s - 2), (stats, s - 3))
                    if live(s):
                        shift(s, 0, settled)
                    else:
                        for sem_, value in settled:
                            wait(dve, sem_, min(value, U))
                    if live(s + 3):
                        normalize(dve, s + 3, 1 - p)
                    if live(s - 5):
                        keep(s - 5, 1 - p)
                    if live(s - 3):
                        statistics(s - 3, 1 - p)
                    if live(s - 4):
                        aggregate(s - 4, p)
                    if live(s):
                        shift(s, 1)
                    if live(s - 2):
                        u = s - 2
                        dve.wait_ge(pr_ps, u + 1)
                        dve.wait_ge(offset_added, u + 1)
                        xs = X[:, ds(2 * u, 2), 0:C]
                        nc.vector.tensor_tensor(xs, xs, ps_misc[:, P:2 * P].rearrange("p (g c) -> p g c", g=2), ALU.add).then_inc(x_ready, 1)
                    if live(s - 1):
                        u = s - 1
                        dve.wait_ge(pv_ps, 2 * u + 2)
                        wait(dve, o_ready, u)
                        for g in range(2):
                            r = slice(C * g, C * g + C)
                            mine = ps_o[r, 0:32 * (HD + 1)].rearrange("p (x g h e) -> p x g h e", g=2, h=2, e=HD + 1)[:, :, g, :, :]
                            last = nc.vector.reciprocal(rsum[r, :, :].unsqueeze(3), mine[:, :, :, HD:HD + 1])
                        last.then_inc(rsum_ready, 1)
                        dve.wait_ge(rsum_ready, u + 1)
                        wait(dve, ot_ps, u)
                        for g in range(2):
                            r = slice(C * g, C * g + C)
                            mine = ps_o[r, 0:32 * (HD + 1)].rearrange("p (x g h e) -> p x g h e", g=2, h=2, e=HD + 1)[:, :, g, :, 0:HD]
                            last = nc.vector.tensor_tensor(o[r, :, :].rearrange("p w (a h d) -> p (w a) h d", h=2, d=HD), mine,
                                                           rsum[r, :, :].unsqueeze(3).to_broadcast([C, NH, 2, HD]), ALU.mult)
                        last.then_inc(o_ready, 1)

                skewed(dve, step, -3, U + 4)


def paired(eng, step, first, last, loop_from, loop_to):
    for k in range(first, loop_from):
        step(k, k % 2, k // 2)
    with eng.Fori(loop_from // 2, (loop_to + 1) // 2) as i:
        for p in range(2):
            step(2 * i + p, p, i)
    for k in range(loop_to + 1, last + 1):
        step(k, k % 2, k // 2)


def mlp(nc, b, X, con, wt, XT):
    with ExitStack() as ctx:
        sb = lambda name, shape, dt=F32: ctx.enter_context(nc.sbuf_tensor(f"ml{b}_{name}", shape, dt))
        pb = lambda name, shape, dt=F32: ctx.enter_context(nc.psum_tensor(f"ml{b}_{name}", shape, dt))
        sem = lambda name: ctx.enter_context(nc.semaphore(f"ml{b}_{name}"))
        GU = 4
        K = U // GU
        GT = 2 * GU
        COL = GT * TOK
        xn = [sb(f"xn{i}", [P, GT, C]) for i in range(2)]
        xT = [sb(f"xT{i}", [P, GT, TOK]) for i in range(2)]
        hid = [sb(f"hid{i}", [P, 2, 2, COL]) for i in range(2)]
        turn = [sb(f"turn{i}", [P, GT, C]) for i in range(2)]
        y_sb = [sb(f"y_sb{i}", [P, GT, TOK]) for i in range(2)]
        st = [sb(f"st{i}", [P, GT, 6]) for i in range(2)]
        mv = [sb(f"mv{i}", [P, GT, 2]) for i in range(2)]
        ps_xt = pb("ps_xt", [P, 512])
        ps_h = [[pb(f"ps_h{f}{g}", [P, 512]) for g in range(2)] for f in range(2)]
        ps_y = [pb(f"ps_y{i}", [P, 512]) for i in range(2)]
        ps_t = pb("ps_t", [P, 512])
        zeroed = sem("zeroed")
        scaled = sem("scaled")
        xn_ready = sem("xn_ready")
        xt_ps = sem("xt_ps")
        xt_ready = sem("xt_ready")
        h_ps = sem("h_ps")
        h_ready = sem("h_ready")
        y_ps = sem("y_ps")
        turn_ready = sem("turn_ready")
        y_ready = sem("y_ready")
        t_ps = sem("t_ps")
        x_ready = sem("x_ready")
        stats = sem("stats")
        aggr = sem("aggr")
        kept = sem("kept")
        rstd, nmr, half_set, stats_on_pool, stats_on_vector = finalize_stats(nc, ctx, f"ml{b}_", X)
        is_live = lambda k: live(k, K)
        first_block = XT is None
        with nc.Block() as block:
            @block.gpsimd
            def _(pool):
                stats_on_pool(pool)

            @block.tensor
            def _(pe):
                def transpose_units(bank, src):
                    for u in range(GU):
                        last = nc.tensor.transpose(bank[:, u * P:(u + 1) * P],
                                                   src[:, 2 * u:2 * u + 2, :].rearrange("p t c -> p (t c)"), con("ident"))
                    return last

                def step(k, p, half):
                    if is_live(k):
                        pe.wait_ge(xt_ready, k + 1)
                        for f in range(2):
                            for g in range(2):
                                wait(pe, h_ready, 4 * (k - 1) + 2 * f + g + 1)
                                nc.tensor.matmul(ps_h[f][g][:, 0:COL], wt(b, f"w1T{g}")[:, f * P:(f + 1) * P],
                                                 xT[p][:].rearrange("p t c -> p (t c)"), start=True, stop=True).then_inc(h_ps, 1)
                    if is_live(k - 2):
                        pe.wait_ge(turn_ready, k - 1)
                        wait(pe, x_ready, k - 2)
                        transpose_units(ps_t, turn[p]).then_inc(t_ps, 1)
                    if is_live(k + 1):
                        pe.wait_ge(xn_ready, k + 2)
                        wait(pe, xt_ready, k + 1)
                        transpose_units(ps_xt, xn[1 - p]).then_inc(xt_ps, 1)
                    if is_live(k - 1):
                        wait(pe, turn_ready if first_block else y_ready, k - 2)
                        for f in range(2):
                            for g in range(2):
                                pe.wait_ge(h_ready, 4 * (k - 1) + 2 * f + g + 1)
                                last = nc.tensor.matmul(ps_y[1 - p][g * C:(g + 1) * C, 0:COL], wt(b, "w2T")[:, f * C:(f + 1) * C],
                                                        hid[1 - p][:, f, g, :], start=(f == 0), stop=(f == 1))
                        last.then_inc(y_ps, 1)

                paired(pe, step, -1, K + 1, 6, 13)

            @block.scalar
            def _(act):
                act.wait_ge(zeroed, 1)

                def step(k, p, half):
                    if is_live(k):
                        wait(act, y_ps, k - 1)
                        for f in range(2):
                            for g in range(2):
                                act.wait_ge(h_ps, 4 * k + 2 * f + g + 1)
                                nc.scalar.activation(hid[p][:, f, g, :], ps_h[f][g][:, 0:COL], ACT.Gelu,
                                                     bias=wt(b, "b1")[:, f:f + 1]).then_inc(h_ready, 1)
                    if is_live(k - 1):
                        wait(act, t_ps, k - 2)
                        if first_block:
                            act.wait_ge(y_ps, k)
                            nc.scalar.activation(turn[1 - p][:, :, 0:TOK], ps_y[1 - p][:, 0:COL].rearrange("p (t c) -> p t c", c=TOK),
                                                 ACT.Identity, bias=wt(b, "b2")).then_inc(turn_ready, 1)
                        else:
                            nc.scalar.activation(turn[1 - p][:], X[:, ds((k - 1) * GT, GT), 0:C], ACT.Copy).then_inc(turn_ready, 1)
                            act.wait_ge(y_ps, k)
                            wait(act, x_ready, k - 2)
                            nc.scalar.activation(y_sb[1 - p][:], ps_y[1 - p][:, 0:COL].rearrange("p (t c) -> p t c", c=TOK),
                                                 ACT.Identity, bias=wt(b, "b2")).then_inc(y_ready, 1)

                paired(act, step, 0, K, 6, 13)

            @block.vector
            def _(dve):
                for i in range(2):
                    last = nc.vector.memset(turn[i][:], 0.0)
                last.then_inc(zeroed, 1)
                stats_on_vector(dve)

                def columns_of(t, k):
                    return t[:, ds(k * GT, GT)].unsqueeze(2).to_broadcast([P, GT, C])

                def finish(k, p, half):
                    dve.wait_ge(t_ps, k + 1)
                    if not first_block:
                        dve.wait_ge(y_ready, k + 1)
                    if first_block:
                        xs = X[:, ds(k * GT, GT), 0:C]
                        nc.vector.tensor_tensor(xs, xs, ps_t[:].rearrange("p (u g c) -> p (u g) c", g=2, c=C), ALU.add).then_inc(x_ready, 1)
                        return
                    for u in range(GU):
                        wcol = GU * p + u
                        for w in range(2):
                            last = nc.vector.tensor_tensor(
                                XT[:, w, ds(half * WS + SHIFT, WS), wcol * WS + SHIFT:wcol * WS + SHIFT + WS],
                                y_sb[p][:, 2 * u + w, :].rearrange("p (i j) -> p i j", j=WS),
                                ps_t[:, u * P + w * C:u * P + w * C + TOK].rearrange("p (i j) -> p i j", j=WS), ALU.add)
                    last.then_inc(x_ready, 1)

                def step(k, p, half):
                    if first_block:
                        wait(dve, x_ready, min(k - 2, K) if isinstance(k, int) else k - 2)
                        wait(dve, stats, min(k - 3, K) if isinstance(k, int) else k - 3)
                    if is_live(k + 2):
                        wait(dve, xt_ps, k + 1)
                        nc.vector.tensor_tensor(xn[p][:], X[:, ds((k + 2) * GT, GT), 0:C], columns_of(rstd, k + 2), ALU.mult).then_inc(scaled, 1)
                    if first_block:
                        if is_live(k - 5):
                            dve.wait_ge(aggr, k - 4)
                            nc.vector.tensor_scalar(X[:, ds((k - 5) * GT, GT), C:ROW], mv[1 - p][:], 1.0, None, ALU.mult).then_inc(kept, 1)
                        if is_live(k - 3):
                            for t in range(GT):
                                last = nc.vector.bn_stats(st[1 - p][:, t, :], X[:, ds((k - 3) * GT + t, 1), 0:C].rearrange("p o c -> p (o c)"))
                            last.then_inc(stats, 1)
                    if first_block:
                        wait(dve, kept, k - 5)
                    if is_live(k + 2):
                        dve.wait_ge(scaled, k + 3)
                        nc.vector.tensor_tensor(xn[p][:], xn[p][:], columns_of(nmr, k + 2), ALU.add).then_inc(xn_ready, 1)
                    if first_block and is_live(k - 4):
                        for t in range(GT):
                            last = nc.vector.bn_aggr(mv[p][:, t, :], st[p][:, t, :])
                        last.then_inc(aggr, 1)
                    if is_live(k + 1):
                        dve.wait_ge(xt_ps, k + 2)
                        wait(dve, h_ps, 4 * k)
                        nc.vector.tensor_scalar(xT[1 - p][:], ps_xt[:].rearrange("p (t c) -> p t c", c=C)[:, :, 0:TOK],
                                                wt(b, "n2g"), wt(b, "n2b"), ALU.mult, ALU.add).then_inc(xt_ready, 1)
                    if is_live(k - 2):
                        finish(k - 2, p, half - 1)

                paired(dve, step, -2, K + 4 if first_block else K + 1, 6, 13)


def roll(nc, X, X2):
    with nc.semaphore("rolled") as rolled, nc.Block() as block:
        src = X[:].rearrange("p (a b g) r -> p a b (g r)", a=NW, b=NW)
        dst = X2[:].rearrange("p (a b g) r -> p a b (g r)", a=NW, b=NW)

        def moves():
            for w in range(2):
                for i in range(WS):
                    for j0, j1 in ((0, SHIFT), (SHIFT, WS)):
                        up, left = i < SHIFT, j0 < SHIFT
                        frm = C * w + WS * i + j0
                        to = C * w + WS * ((i - SHIFT) % WS) + (j0 - SHIFT) % WS
                        rows = [(0, NW, 0)] if not up else [(1, NW, 0), (0, 1, NW - 1)]
                        cols = [(0, NW, 0)] if not left else [(1, NW, 0), (0, 1, NW - 1)]
                        for a0, a1, a2 in rows:
                            for b0, b1, b2 in cols:
                                yield frm, to, j1 - j0, a0, a1, a2, b0, b1, b2
        every = list(moves())

        def run(eng, mine):
            for frm, to, n, a0, a1, a2, b0, b1, b2 in mine:
                eng.dma_start(dst[to:to + n, a2:a2 + a1 - a0, b2:b2 + b1 - b0, :],
                              src[frm:frm + n, a0:a1, b0:b1, :]).then_inc(rolled, 16)

        @block.sync
        def _(sp):
            run(sp, every[0::2])
            sp.wait_ge(rolled, 16 * len(every))

        @block.scalar
        def _(act):
            run(act, every[1::2])

        @block.gpsimd
        def _(pool):
            clear_spent(nc)


CH = 448
NCH = 2 * TIME // CH
CLS = 2 * TIME
COLS = 2 * SEQ
LN_EXP_SET = 6
N1, N2, N3 = 14, 14, 16
LANES = 2 * TIME // N1


def chunked(eng, step):
    for k in range(4):
        step(k, k % 2, k * CH, CH)
    with eng.Fori(2, NCH // 2) as i:
        for p in range(2):
            step(2 * i + p, p, (2 * i + p) * CH, CH)
    step(NCH, NCH % 2, CLS, 2)


def chunked_lagging(eng, step, behind):
    def both(k, p, at, n):
        step(k, p, at, n)
        if not (isinstance(k, int) and k == 0):
            behind(k - 1, 1 - p, (k - 1) * CH, CH)
    chunked(eng, both)
    behind(NCH, NCH % 2, CLS, 2)


def unroll_raster(nc, XT, H0, tail_w, ew1, ew2, tail_in, ew1_in, ew2_in):
    with nc.semaphore("tail_loaded") as tail_loaded, nc.Block() as block:
        def copy(engine, w):
            img = H0[:, w * TIME:(w + 1) * TIME].rearrange("p (y x) -> p y x", x=SIDE)
            for y, ny, fy in ((SHIFT, SIDE - SHIFT, SHIFT), (0, SHIFT, SIDE)):
                for x, nx, fx in ((SHIFT, SIDE - SHIFT, SHIFT), (0, SHIFT, SIDE)):
                    engine.tensor_copy(img[:, y:y + ny, x:x + nx], XT[:, w, fy:fy + ny, fx:fx + nx])

        @block.sync
        def _(sp):
            sp.dma_start(tail_w[:], tail_in).then_inc(tail_loaded, 16)
            sp.dma_start(ew1[:], ew1_in).then_inc(tail_loaded, 16)
            sp.dma_start(ew2[:], ew2_in).then_inc(tail_loaded, 16)
            sp.wait_ge(tail_loaded, 48)

        @block.vector
        def _(dve):
            copy(nc.vector, 0)
            dve.wait_ge(tail_loaded, 48)
            at = TAIL_AT["cls"][0]
            nc.vector.tensor_copy(H0[:, CLS:COLS], tail_w[:, at:at + 1].to_broadcast([P, 2]))

        @block.gpsimd
        def _(pool):
            clear_spent(nc)
            copy(nc.gpsimd, 1)


def channel_norm(nc, name, src, con, finish, n_finish, on_tensor=None, on_pool=None, out_dma=None, setup=None):
    with ExitStack() as ctx:
        sb = lambda nm, shape, dt=F32: ctx.enter_context(nc.sbuf_tensor(f"{name}_{nm}", shape, dt))
        pb = lambda nm, shape, dt=F32: ctx.enter_context(nc.psum_tensor(f"{name}_{nm}", shape, dt))
        sem = lambda nm: ctx.enter_context(nc.semaphore(f"{name}_{nm}"))
        centred = [sb(f"centred{i}", [P, CH]) for i in range(2)]
        square = [sb(f"square{i}", [P, CH]) for i in range(2)]
        lnv = sb("lnv", [P, CH])
        rstd = [sb(f"rstd{i}", [P, CH]) for i in range(2)]
        eps = sb("eps", [P, 1])
        ps_mean = [pb(f"ps_mean{i}", [P, 512]) for i in range(2)]
        ps_var = [pb(f"ps_var{i}", [P, 512]) for i in range(2)]
        ps_x = [pb(f"ps_x{i}", [P, 512]) for i in range(2)]
        eps_set = sem("eps_set")
        mean_ps = sem("mean_ps")
        centred_ready = sem("centred_ready")
        square_ready = sem("square_ready")
        var_ps = sem("var_ps")
        ln_ready = sem("ln_ready")
        rstd_ready = sem("rstd_ready")
        done = sem("done")
        extra_ps = sem("extra_ps")
        extra_done = sem("extra_done")
        inner = sem("inner")
        stored = [sem("stored0"), sem("stored1")]
        ones = con("mean_ones")
        with nc.Block() as block:
            @block.tensor
            def _(pe):
                def mean(k, p, at, n):
                    wait(pe, centred_ready, k - 1)
                    nc.tensor.matmul(ps_mean[p][:, 0:n], ones, src[:, ds(at, n)], start=True, stop=True).then_inc(mean_ps, 1)

                def variance(k, p, at, n):
                    pe.wait_ge(square_ready, k + 1)
                    wait(pe, ln_ready, k - 1)
                    nc.tensor.matmul(ps_var[p][:, 0:n], ones, square[p][:, 0:n], start=True, stop=True).then_inc(var_ps, 1)
                    if on_tensor is not None and not (isinstance(k, int) and k == 0):
                        on_tensor(pe, k - 1, 1 - p, (k - 1) * CH, CH, ps_x[1 - p], done, extra_ps, extra_done)

                chunked_lagging(pe, mean, variance)
                if on_tensor is not None:
                    on_tensor(pe, NCH, NCH % 2, CLS, 2, ps_x[NCH % 2], done, extra_ps, extra_done)

            @block.scalar
            def _(act):
                nc.scalar.add_instruction(mybir.InstLoadActFuncSet(name=nc.get_next_instruction_name(), engine=mybir.EngineType.Activation,
                                                                   act_func_set_id=LN_EXP_SET, ins=[], outs=[]))
                act.wait_ge(eps_set, 1)

                def squares(k, p, at, n):
                    act.wait_ge(centred_ready, k + 1)
                    wait(act, var_ps, k - 1)
                    nc.scalar.activation(square[p][:, 0:n], centred[p][:, 0:n], ACT.Square).then_inc(square_ready, 1)

                def inverse(k, p, at, n):
                    act.wait_ge(var_ps, k + 1)
                    wait(act, rstd_ready, k)
                    nc.scalar.activation(lnv[:, 0:n], ps_var[p][:, 0:n], ACT.Ln, bias=eps[:]).then_inc(ln_ready, 1)
                    act.wait_ge(ln_ready, k + 1)
                    wait(act, done, k - 1)
                    nc.scalar.activation(rstd[p][:, 0:n], lnv[:, 0:n], ACT.Exp, scale=-0.5).then_inc(rstd_ready, 1)

                chunked_lagging(act, squares, inverse)

            @block.vector
            def _(dve):
                nc.vector.memset(eps[:], EPS).then_inc(eps_set, 1)
                if setup is not None:
                    setup(dve)

                def centre(k, p, at, n):
                    dve.wait_ge(mean_ps, k + 1)
                    wait(dve, done, k - 1)
                    nc.vector.tensor_tensor(centred[p][:, 0:n], src[:, ds(at, n)], ps_mean[p][:, 0:n], ALU.subtract).then_inc(centred_ready, 1)

                def last(k, p, at, n):
                    dve.wait_ge(rstd_ready, k + 1)
                    finish(dve, k, p, at, n, centred[p], rstd[p], done, inner, ps_x, extra_ps, extra_done, stored)

                chunked_lagging(dve, centre, last)
                if n_finish is not None:
                    n_finish(dve, ps_x, done, extra_ps, extra_done)

            if on_pool is not None:
                @block.gpsimd
                def _(pool):
                    chunked(pool, lambda k, p, at, n: on_pool(pool, k, p, at, n, done))

            if out_dma is not None:
                @block.sync
                def _(sp):
                    chunked(sp, lambda k, p, at, n: out_dma(sp, k, p, at, n, done, stored))
                    for p in range(2):
                        sp.wait_ge(stored[p], 16 * ((NCH + 2 - p) // 2))


def recurrence(nc, F, Z, tw):
    with ExitStack() as ctx:
        sb = lambda nm, shape, dt=F32: ctx.enter_context(nc.sbuf_tensor(f"rec_{nm}", shape, dt))
        sem = lambda nm: ctx.enter_context(nc.semaphore(f"rec_{nm}"))
        NL, NS = LANES + 2, 2 * N3
        xs, z_start, ts = sb("xs", [P, NL]), sb("z_start", [P, NL]), sb("ts", [P, NL])
        fcls = sb("fcls", [P, 2])
        end_x, end_z = sb("end_x", [P, NS + 2, N2]), sb("end_z", [P, NS + 2, N2])
        vx, vz = sb("vx", [P, N2 + 1, NS + 2]), sb("vz", [P, N2 + 1, NS + 2])
        tx, tz = sb("tx", [P, NS + 2]), sb("tz", [P, NS + 2])
        wx, wz = sb("wx", [P, 2, N3]), sb("wz", [P, 2, N3])
        cx, cz = sb("cx", [P, LANES]), sb("cz", [P, LANES])
        made = sem("made")
        stt = nc.vector.scalar_tensor_tensor
        with nc.Block() as block:
            @block.vector
            def _(dve):
                count = [0]

                def link(ins):
                    count[0] += 1
                    ins.then_inc(made, 1)
                    dve.wait_ge(made, count[0])

                s, neg_dsa = tw("s"), tw("neg_dsa")
                link(nc.vector.tensor_copy(fcls[:], F[:, CLS:COLS]))
                nc.vector.memset(xs[:], 0.0)
                nc.vector.memset(z_start[:], 0.0)
                nc.vector.memset(end_x[:], 0.0)
                nc.vector.memset(end_z[:], 0.0)
                nc.vector.memset(vx[:, 0, :], 0.0)
                nc.vector.memset(vz[:, 0, :], 0.0)
                nc.vector.tensor_copy(wx[:, :, 0], fcls[:])
                nc.vector.tensor_scalar(wz[:, :, 0], fcls[:], DT, None, ALU.mult)
                link(nc.vector.memset(F[:, CLS:NL * N1], 0.0))
                nc.vector.memset(xs[:, LANES:LANES + 1], 1.0)
                nc.vector.memset(vx[:, 0, NS:NS + 1], 1.0)
                nc.vector.memset(vz[:, 0, NS + 1:NS + 2], 1.0)
                link(nc.vector.memset(z_start[:, LANES + 1:NL], 1.0))
                f_at = F[:, 0:NL * N1].rearrange("p (l n) -> p l n", n=N1)
                z_at = Z[:, 0:NL * N1].rearrange("p (l n) -> p l n", n=N1)
                halves = [slice(0, LANES // 2), slice(LANES // 2, NL)]

                def at(t, h, n):
                    return t[:, h, ds(n, 1)].rearrange("p l o -> p (l o)")

                base = count[0]

                def local(n):
                    before = lambda h: z_start[:, h] if isinstance(n, int) and n == 0 else at(z_at, h, n - 1)
                    done = base + 6 * n
                    for q, h in enumerate(halves):
                        wait(dve, made, done - 1 + q)
                        stt(ts[:, h], before(h), neg_dsa, at(f_at, h, n), ALU.mult, ALU.add).then_inc(made, 1)
                    for q, h in enumerate(halves):
                        dve.wait_ge(made, done + 1 + q)
                        stt(xs[:, h], xs[:, h], s, ts[:, h], ALU.mult, ALU.add).then_inc(made, 1)
                    for q, h in enumerate(halves):
                        dve.wait_ge(made, done + 3 + q)
                        stt(at(z_at, h, n), xs[:, h], DT, before(h), ALU.mult, ALU.add).then_inc(made, 1)

                local(0)
                local(1)
                with dve.Fori(0, (N1 - 2) // 4) as i:
                    for j in range(4):
                        local(4 * i + 2 + j)
                count[0] += 6 * N1
                dve.wait_ge(made, count[0])

                last = z_at[:, :, N1 - 1]
                a11, a12 = xs[:, LANES:LANES + 1], xs[:, LANES + 1:NL]
                a21, a22 = last[:, LANES:LANES + 1], last[:, LANES + 1:NL]
                nc.vector.tensor_copy(end_x[:, 0:NS, :].rearrange("p s c -> p (s c)"), xs[:, 0:LANES])
                link(nc.vector.tensor_copy(end_z[:, 0:NS, :].rearrange("p s c -> p (s c)"), last[:, 0:LANES]))

                base = count[0]
                with dve.Fori(0, 2) as i:
                    for j in range(N2 // 2):
                        k = (N2 // 2) * i + j
                        x, z = (v[:, ds(k, 1), :].rearrange("p o l -> p (o l)") for v in (vx, vz))
                        x1, z1 = (v[:, ds(k + 1, 1), :].rearrange("p o l -> p (o l)") for v in (vx, vz))
                        every = slice(0, NS + 2)
                        stt(tx[:], x, a11, at(end_x, every, k), ALU.mult, ALU.add).then_inc(made, 1)
                        stt(tz[:], x, a21, at(end_z, every, k), ALU.mult, ALU.add).then_inc(made, 1)
                        dve.wait_ge(made, base + 4 * k + 1)
                        stt(x1, z, a12, tx[:], ALU.mult, ALU.add).then_inc(made, 1)
                        dve.wait_ge(made, base + 4 * k + 2)
                        stt(z1, z, a22, tz[:], ALU.mult, ALU.add).then_inc(made, 1)
                        dve.wait_ge(made, base + 4 * k + 4)
                count[0] += 4 * N2

                b11, b12 = vx[:, N2, NS:NS + 1], vx[:, N2, NS + 1:NS + 2]
                b21, b22 = vz[:, N2, NS:NS + 1], vz[:, N2, NS + 1:NS + 2]
                span_x = vx[:, N2, 0:NS].rearrange("p (w c) -> p w c", w=2)
                span_z = vz[:, N2, 0:NS].rearrange("p (w c) -> p w c", w=2)
                both = slice(0, 2)
                base = count[0]
                with dve.Fori(0, 3) as i:
                    for j in range((N3 - 1) // 3):
                        k = (N3 - 1) // 3 * i + j
                        stt(tx[:, 0:2], at(wx, both, k), b11, at(span_x, both, k), ALU.mult, ALU.add).then_inc(made, 1)
                        stt(tz[:, 0:2], at(wx, both, k), b21, at(span_z, both, k), ALU.mult, ALU.add).then_inc(made, 1)
                        dve.wait_ge(made, base + 4 * k + 1)
                        stt(at(wx, both, k + 1), at(wz, both, k), b12, tx[:, 0:2], ALU.mult, ALU.add).then_inc(made, 1)
                        dve.wait_ge(made, base + 4 * k + 2)
                        stt(at(wz, both, k + 1), at(wz, both, k), b22, tz[:, 0:2], ALU.mult, ALU.add).then_inc(made, 1)
                        dve.wait_ge(made, base + 4 * k + 4)
                count[0] += 4 * (N3 - 1)

                start_x, start_z = wx[:].rearrange("p w c -> p (w c)"), wz[:].rearrange("p w c -> p (w c)")
                cx_at, cz_at = (t[:].rearrange("p (s c) -> p s c", c=N2) for t in (cx, cz))
                spans = slice(0, NS)
                for part, start in ((0, start_x), (1, start_z)):
                    base = count[0]
                    with dve.Fori(0, 2) as i:
                        for j in range(N2 // 2):
                            k = (N2 // 2) * i + j
                            for v, c_at in ((vx, cx_at), (vz, cz_at)):
                                coef = v[:, ds(k, 1), NS + part:NS + part + 1].rearrange("p o l -> p (o l)")
                                own = v[:, ds(k, 1), 0:NS].rearrange("p o l -> p (o l)") if part == 0 else at(c_at, spans, k)
                                stt(at(c_at, spans, k), start, coef, own, ALU.mult, ALU.add).then_inc(made, 1)
                    count[0] += 2 * N2
                    dve.wait_ge(made, count[0])

                real = slice(0, LANES)
                for part, start in ((0, cx), (1, cz)):
                    with dve.Fori(0, 2) as i:
                        for j in range(N1 // 2):
                            n = (N1 // 2) * i + j
                            coef = z_at[:, LANES + part:LANES + part + 1, ds(n, 1)].rearrange("p l o -> p (l o)")
                            stt(at(z_at, real, n), start[:], coef, at(z_at, real, n), ALU.mult, ALU.add).then_inc(made, 1)
                    count[0] += N1
                    dve.wait_ge(made, count[0])
                link(nc.vector.tensor_scalar(Z[:, CLS:COLS], fcls[:], DT, None, ALU.mult))


def mixer_gelu(nc, U_, Z, G, tw):
    with ExitStack() as ctx:
        pb = lambda nm, shape, dt=F32: ctx.enter_context(nc.psum_tensor(f"mix_{nm}", shape, dt))
        ps = [pb(f"ps{i}", [P, 512]) for i in range(4)]
        v_ps, g_ready = ctx.enter_context(nc.semaphore("mix_v_ps")), ctx.enter_context(nc.semaphore("mix_g_ready"))
        with nc.Block() as block:
            @block.tensor
            def _(pe):
                def step(k, p, at, n):
                    wait(pe, g_ready, k - 1)
                    nc.tensor.matmul(ps[p][:, 0:n], tw("CBD"), Z[:, ds(at, n)], start=True, stop=False)
                    nc.tensor.matmul(ps[p][:, 0:n], tw("DBD"), U_[:, ds(at, n)], start=False, stop=True).then_inc(v_ps, 1)
                chunked(pe, step)

            @block.scalar
            def _(act):
                def step(k, p, at, n):
                    act.wait_ge(v_ps, k + 1)
                    nc.scalar.activation(G[:, ds(at, n)], ps[p][:, 0:n], ACT.Gelu, bias=tw("bCD")).then_inc(g_ready, 1)
                chunked(act, step)


def mixer_gate(nc, G, HU, H1):
    with ExitStack() as ctx:
        sb = lambda nm, shape, dt=F32: ctx.enter_context(nc.sbuf_tensor(f"gate_{nm}", shape, dt))
        sem = lambda nm: ctx.enter_context(nc.semaphore(f"gate_{nm}"))
        sg = [sb(f"sg{i}", [P, CH]) for i in range(2)]
        pr = [sb(f"pr{i}", [P, CH]) for i in range(2)]
        sg_ready, product, added = sem("sg_ready"), sem("product"), sem("added")
        with nc.Block() as block:
            @block.scalar
            def _(act):
                def step(k, p, at, n):
                    wait(act, product, k - 1)
                    nc.scalar.activation(sg[p][:, 0:n], G[:, ds(at, n)], ACT.Sigmoid).then_inc(sg_ready, 1)
                chunked(act, step)

            @block.vector
            def _(dve):
                def multiply(k, p, at, n):
                    dve.wait_ge(sg_ready, k + 1)
                    wait(dve, added, k - 1)
                    nc.vector.tensor_tensor(pr[p][:, 0:n], G[:, ds(at, n)], sg[p][:, 0:n], ALU.mult).then_inc(product, 1)

                def add(k, p, at, n):
                    dve.wait_ge(product, k + 1)
                    nc.vector.tensor_tensor(H1[:, ds(at, n)], pr[p][:, 0:n], HU[:, ds(at, n)], ALU.add).then_inc(added, 1)
                chunked_lagging(dve, multiply, add)


def router(nc, X3, tw, ew1, ew2, w1_sel, w2_sel, b1_sel, b2_mix):
    with ExitStack() as ctx:
        sb = lambda nm, shape, dt=F32: ctx.enter_context(nc.sbuf_tensor(f"route_{nm}", shape, dt))
        sem = lambda nm: ctx.enter_context(nc.semaphore(f"route_{nm}"))
        E = N_EXP
        sums, wr = sb("sums", [P, 2]), sb("wr", [P, 2, E])
        r, r2 = sb("r", [P, 2, E]), sb("r2", [P, 2, E])
        m = sb("m", [P, 2])
        tot, inv = sb("tot", [P, 2]), sb("inv", [P, 2])
        load, scale = sb("load", [P, E]), sb("scale", [P, E])
        cand, hot = sb("cand", [P, 2, E]), sb("hot", [P, 2, 2, E])
        top, gates, gated = sb("top", [P, 2, 2]), sb("gates", [P, 2, 2]), sb("gated", [P, 2, 2, E])
        e2, den = sb("e2", [P, 2]), sb("den", [P, 2])
        spread = sb("spread", [P, 2, 2, 2, 2, E])
        prod1, prod2 = sb("prod1", [P, 8, E]), sb("prod2", [P, 2, 2 * E])
        both = sb("both", [P, 2, 2 * 2 * E])
        ps = ctx.enter_context(nc.psum_tensor("route_ps", [P, 512], F32))
        made, by_pe, by_act, by_pool = sem("made"), sem("by_pe"), sem("by_act"), sem("by_pool")
        spread_ready = sem("spread_ready")
        with nc.Block() as block:
            @block.tensor
            def _(pe):
                pe.wait_ge(made, 4)
                nc.tensor.matmul(ps[:, 0:2 * E], tw("group_ones"), wr[:].rearrange("p w e -> p (w e)"), start=True, stop=True).then_inc(by_pe, 1)
                pe.wait_ge(made, 10)
                nc.tensor.matmul(ps[:, 0:2 * E], tw("all_ones"), r[:].rearrange("p w e -> p (w e)"), start=True, stop=True).then_inc(by_pe, 1)
                pe.wait_ge(spread_ready, 1)
                for g in range(2):
                    last = nc.tensor.matmul(ps[:, g * 64:(g + 1) * 64], tw(f"pick{g}"), both[:].rearrange("p a b -> p (a b)"), start=True, stop=True)
                last.then_inc(by_pe, 1)

            @block.scalar
            def _(act):
                act.wait_ge(made, 7)
                nc.scalar.activation(r[:], r[:], ACT.Exp).then_inc(by_act, 1)
                act.wait_ge(made, 17)
                nc.scalar.activation(r2[:], r2[:], ACT.Exp).then_inc(by_act, 1)
                act.wait_ge(made, 32)
                nc.scalar.activation(e2[:], e2[:], ACT.Exp).then_inc(by_act, 1)

            @block.vector
            def _(dve):
                count = [0]

                def link(ins):
                    count[0] += 1
                    ins.then_inc(made, 1)
                    dve.wait_ge(made, count[0])

                wide = lambda t: t[:].unsqueeze(2).to_broadcast([P, 2, E])
                link(nc.vector.reduce_sum(sums[:], X3[:, 0:CLS].rearrange("p (w t) -> p w t", w=2), AX.X))
                link(nc.vector.tensor_tensor(sums[:], sums[:], X3[:, CLS:COLS], ALU.add))
                for w in range(2):
                    link(nc.vector.tensor_scalar(wr[:, w, :], tw("Wr"), sums[:, w:w + 1], 1.0 / SEQ, ALU.mult, ALU.mult))
                dve.wait_ge(by_pe, 1)
                link(nc.vector.tensor_tensor(r[:].rearrange("p w e -> p (w e)"), ps[:, 0:2 * E], tw("br_row"), ALU.add))

                def softmax(t, n_act):
                    link(nc.vector.reduce_max(m[:], t[:], AX.X))
                    link(nc.vector.tensor_tensor(t[:], t[:], wide(m), ALU.subtract))
                    dve.wait_ge(by_act, n_act)
                    link(nc.vector.reduce_sum(tot[:], t[:], AX.X))
                    link(nc.vector.reciprocal(inv[:], tot[:]))
                    link(nc.vector.tensor_tensor(t[:], t[:], wide(inv), ALU.mult))

                softmax(r, 1)
                dve.wait_ge(by_pe, 2)
                link(nc.vector.reduce_sum(load[:], ps[:, 0:2 * E].rearrange("p (w e) -> p e w", w=2), AX.X))
                link(nc.vector.tensor_scalar(load[:], load[:], 1.0 / C, float(SEQ), ALU.mult, ALU.mult))
                link(nc.vector.reciprocal(scale[:], load[:]))
                link(nc.vector.tensor_scalar(scale[:], scale[:], CAPACITY, 1.0, ALU.mult, ALU.min))
                link(nc.vector.tensor_tensor(r2[:], r[:], scale[:].unsqueeze(1).to_broadcast([P, 2, E]), ALU.mult))
                softmax(r2, 2)
                index = tw("index_row").unsqueeze(1).to_broadcast([P, 2, E])
                for c in range(2):
                    link(nc.vector.reduce_max(top[:, :, c], r2[:], AX.X))
                    link(nc.vector.tensor_tensor(cand[:], r2[:], top[:, :, c].unsqueeze(2).to_broadcast([P, 2, E]), ALU.is_equal))
                    link(nc.vector.tensor_tensor(cand[:], cand[:], index, ALU.mult))
                    link(nc.vector.reduce_max(m[:], cand[:], AX.X))
                    if c == 0:
                        link(nc.vector.tensor_tensor(hot[:, :, c, :], cand[:], wide(m), ALU.is_equal))
                        for w in range(2):
                            link(nc.vector.scalar_tensor_tensor(r2[:, w, :], hot[:, w, c, :], -2.0, r2[:, w, :], ALU.mult, ALU.add))
                    else:
                        link(nc.vector.tensor_tensor(e2[:], top[:, :, 1], top[:, :, 0], ALU.subtract))
                        hot_at = count[0]
                        link(nc.vector.tensor_tensor(hot[:, :, c, :], cand[:], wide(m), ALU.is_equal))
                assert count[0] == 33, count[0]
                dve.wait_ge(by_act, 3)
                link(nc.vector.tensor_scalar(den[:], e2[:], 1.0, None, ALU.add))
                link(nc.vector.reciprocal(gates[:, :, 0], den[:]))
                link(nc.vector.tensor_tensor(gates[:, :, 1], gates[:, :, 0], e2[:], ALU.mult))
                link(nc.vector.tensor_tensor(gated[:].rearrange("p w c e -> p (w c) e"), hot[:].rearrange("p w c e -> p (w c) e"),
                                             gates[:].rearrange("p w c -> p (w c)").unsqueeze(2).to_broadcast([P, 4, E]), ALU.mult))
                nc.vector.tensor_copy(both[:, 0, :], hot[:].rearrange("p w c e -> p (w c e)"))
                nc.vector.tensor_copy(both[:, 1, :], gated[:].rearrange("p w c e -> p (w c e)")).then_inc(spread_ready, 1)
                for w in range(2):
                    for c in range(2):
                        dst = w1_sel[:, (2 * w + c) * FF:(2 * w + c + 1) * FF]
                        link(nc.vector.tensor_scalar(dst, ew1[:, 0:FF], hot[:, w, c, 0:1], None, ALU.mult))
                        for e in range(1, E):
                            link(nc.vector.scalar_tensor_tensor(dst, ew1[:, e * FF:(e + 1) * FF], hot[:, w, c, e:e + 1], dst, ALU.mult, ALU.add))
                for w in range(2):
                    link(nc.vector.tensor_tensor(prod2[:, w, :].rearrange("p (c e) -> p c e", c=2), gated[:, w, :, :],
                                                 tw("b2T").unsqueeze(1).to_broadcast([P, 2, E]), ALU.mult))
                link(nc.vector.reduce_sum(b2_mix[:], prod2[:], AX.X))
                dve.wait_ge(by_pe, 3)
                link(nc.vector.tensor_copy(spread[:].rearrange("p g a w c e -> p (g a w c e)"), ps[:, 0:2 * 64]))
                for g in range(2):
                    link(nc.vector.tensor_tensor(prod1[:, 4 * g:4 * g + 4, :], spread[:, g, 0, :, :, :].rearrange("p w c e -> p (w c) e"),
                                                 tw("b1T").unsqueeze(1).to_broadcast([P, 4, E]), ALU.mult))
                link(nc.vector.reduce_sum(b1_sel[:], prod1[:], AX.X))
                for g in range(2):
                    for w in range(2):
                        for c in range(2):
                            i = 4 * g + 2 * w + c
                            dst = w2_sel[:, i * C:(i + 1) * C]
                            link(nc.vector.tensor_scalar(dst, ew2[:, 0:C], spread[:, g, 1, w, c, 0:1], None, ALU.mult))
                            for e in range(1, E):
                                link(nc.vector.scalar_tensor_tensor(dst, ew2[:, e * C:(e + 1) * C], spread[:, g, 1, w, c, e:e + 1], dst, ALU.mult, ALU.add))


def experts(nc, X3, Y, w1_sel, w2_sel, b1_sel, b2_mix):
    with ExitStack() as ctx:
        sb = lambda nm, shape, dt=F32: ctx.enter_context(nc.sbuf_tensor(f"ex_{nm}", shape, dt))
        pb = lambda nm, shape, dt=F32: ctx.enter_context(nc.psum_tensor(f"ex_{nm}", shape, dt))
        sem = lambda nm: ctx.enter_context(nc.semaphore(f"ex_{nm}"))
        xin = [sb(f"xin{i}", [P, CH]) for i in range(2)]
        hid = [[sb(f"hid{i}_{j}", [P, CH]) for j in range(4)] for i in range(2)]
        ps_h = [pb(f"ps_h{j}", [P, 512]) for j in range(4)]
        ps_y = [pb(f"ps_y{i}", [P, 512]) for i in range(2)]
        x_in = sem("x_in")
        h_ps = sem("h_ps")
        h_ready = sem("h_ready")
        y_ps = sem("y_ps")
        y_ready = sem("y_ready")
        PER = NCH // 2
        assert PER % 2 == 1

        def pairs(eng, w, body):
            first = w * PER + 1
            if w == 0:
                for k in (1, 2):
                    body(k, k % 2, k * CH)
            with eng.Fori(1 - w, PER // 2) as i:
                for q in range(2):
                    k = 2 * i + first + q
                    body(k, (first + q) % 2, k * CH)

        def order(eng, step):
            for w in range(2):
                step(w * PER, w, w * PER % 2, w * PER * CH, CH)
                pairs(eng, w, lambda k, p, at: step(k, w, p, at, CH))
            for w in range(2):
                step(NCH + w, w, (NCH + w) % 2, CLS + w, 1)

        def lagging(eng, step, behind):
            for w in range(2):
                first = w * PER
                step(first, w, first % 2, first * CH, CH)
                if w:
                    behind(first - 1, 0, (first - 1) % 2, (first - 1) * CH, CH)

                def both(k, p, at):
                    step(k, w, p, at, CH)
                    behind(k - 1, w, 1 - p, (k - 1) * CH, CH)
                pairs(eng, w, both)
            step(NCH, 0, NCH % 2, CLS, 1)
            behind(NCH - 1, 1, (NCH - 1) % 2, (NCH - 1) * CH, CH)
            step(NCH + 1, 1, (NCH + 1) % 2, CLS + 1, 1)
            behind(NCH, 0, NCH % 2, CLS, 1)
            behind(NCH + 1, 1, (NCH + 1) % 2, CLS + 1, 1)

        with nc.Block() as block:
            @block.gpsimd
            def _(pool):
                def step(k, w, p, at, n):
                    wait(pool, h_ps, 4 * k - 4)
                    nc.gpsimd.tensor_copy(xin[p][:, 0:n], X3[:, ds(at, n)]).then_inc(x_in, 1)
                order(pool, step)

            @block.tensor
            def _(pe):
                def up(k, w, p, at, n):
                    pe.wait_ge(x_in, k + 1)
                    for c in range(2):
                        for g in range(2):
                            j, r = 2 * c + g, slice(C * g, C * g + C)
                            wait(pe, h_ready, 4 * k - 4 + j + 1)
                            nc.tensor.matmul(ps_h[j][:, 0:n], w1_sel[r, (2 * w + c) * FF:(2 * w + c + 1) * FF], xin[p][r, 0:n],
                                             start=True, stop=True).then_inc(h_ps, 1)

                def down(k, w, p, at, n):
                    wait(pe, y_ready, k - 1)
                    for c in range(2):
                        for g in range(2):
                            j, i = 2 * c + g, 4 * g + 2 * w + c
                            pe.wait_ge(h_ready, 4 * k + j + 1)
                            last = nc.tensor.matmul(ps_y[p][C * g:C * g + C, 0:n], w2_sel[:, i * C:(i + 1) * C], hid[p][j][:, 0:n],
                                                    start=(c == 0), stop=(c == 1), skip_group_check=True)
                    last.then_inc(y_ps, 1)
                lagging(pe, up, down)

            @block.scalar
            def _(act):
                def step(k, w, p, at, n):
                    wait(act, y_ps, k - 1)
                    for j in range(4):
                        c, g = j // 2, j % 2
                        act.wait_ge(h_ps, 4 * k + j + 1)
                        i = 4 * g + 2 * w + c
                        nc.scalar.activation(hid[p][j][:, 0:n], ps_h[j][:, 0:n], ACT.Gelu, bias=b1_sel[:, i:i + 1]).then_inc(h_ready, 1)
                order(act, step)

            @block.vector
            def _(dve):
                def step(k, w, p, at, n):
                    dve.wait_ge(y_ps, k + 1)
                    nc.vector.scalar_tensor_tensor(Y[:, ds(at, n)], ps_y[p][:, 0:n], b2_mix[:, w:w + 1], X3[:, ds(at, n)],
                                                   ALU.add, ALU.add).then_inc(y_ready, 1)
                order(dve, step)


def tail(nc, ctx, X, X2, XT, con, tail_in, ew1_in, ew2_in, out, debug):
    sb = lambda name, shape, dt=F32: ctx.enter_context(nc.sbuf_tensor(name, shape, dt))
    u_cols = X[:].rearrange("p t r -> p (t r)")
    f_cols = X2[:].rearrange("p t r -> p (t r)")
    H0 = sb("H0", [P, COLS])
    Z = sb("Z", [P, (LANES + 2) * N1])
    tail_w = sb("tail_w", [P, TAIL_W])
    ew1 = sb("ew1", [P, N_EXP * FF])
    ew2 = sb("ew2", [FF, N_EXP * C])
    w1_sel = sb("w1_sel", [P, 4 * FF])
    w2_sel = sb("w2_sel", [P, 8 * C])
    b1_sel = sb("b1_sel", [P, 8])
    b2_mix = sb("b2_mix", [P, 2])
    derived = sb("derived", [P, 6])
    extra = {"s": 0, "neg_dsa": 1, "ds": 2, "bCD": 3, "tmp": 4, "f_bias": 5}

    def tw(name):
        if name in extra:
            return derived[:, extra[name]:extra[name] + 1]
        at, n = TAIL_AT[name]
        return tail_w[:, at:at + n]

    unroll_raster(nc, XT, H0, tail_w, ew1, ew2, tail_in, ew1_in, ew2_in)

    with nc.semaphore("coef") as coef:
        def coefficients(dve):
            count = [0]

            def link(ins):
                count[0] += 1
                ins.then_inc(coef, 1)
                dve.wait_ge(coef, count[0])

            link(nc.vector.tensor_scalar(tw("tmp"), tw("a"), DT * DT, 1.0, ALU.mult, ALU.add))
            link(nc.vector.reciprocal(tw("s"), tw("tmp")))
            link(nc.vector.tensor_scalar(tw("ds"), tw("s"), DT, None, ALU.mult))
            link(nc.vector.scalar_tensor_tensor(tw("neg_dsa"), tw("ds"), -1.0, tw("a"), ALU.mult, ALU.mult))
            link(nc.vector.tensor_tensor(tw("bCD"), tw("bC"), tw("bD"), ALU.add))

        def b_product(pe, k, p, at, n, ps, done, extra_ps, extra_done):
            pe.wait_ge(done, k + 1)
            wait(pe, extra_done, k - 1)
            nc.tensor.matmul(ps[:, 0:n], tw("BBD"), u_cols[:, ds(at, n)], start=True, stop=True).then_inc(extra_ps, 1)

        def forcing(dve, k, p, at, n, ps_x, extra_ps, extra_done):
            dve.wait_ge(extra_ps, k + 1)
            nc.vector.tensor_scalar(f_cols[:, ds(at, n)], ps_x[p][:, 0:n], tw("bB"), tw("ds"), ALU.add, ALU.mult).then_inc(extra_done, 1)

        def mixer_in(dve, k, p, at, n, centred, rstd, done, inner, ps_x, extra_ps, extra_done, stored):
            nc.vector.tensor_tensor(u_cols[:, ds(at, n)], centred[:, 0:n], rstd[:, 0:n], ALU.mult).then_inc(done, 1)
            if isinstance(k, int) and k == 0:
                return
            forcing(dve, k - 1, 1 - p, (k - 1) * CH, CH, ps_x, extra_ps, extra_done)

        def last_forcing(dve, ps_x, done, extra_ps, extra_done):
            forcing(dve, NCH, NCH % 2, CLS, 2, ps_x, extra_ps, extra_done)

        def add_u(pool, k, p, at, n, done):
            pool.wait_ge(done, k + 1)
            nc.gpsimd.tensor_tensor(H0[:, ds(at, n)], H0[:, ds(at, n)], u_cols[:, ds(at, n)], ALU.add)

        channel_norm(nc, "cn0", H0, con, mixer_in, last_forcing, on_tensor=b_product, on_pool=add_u, setup=coefficients)
    recurrence(nc, f_cols, Z, tw)
    G = f_cols
    mixer_gelu(nc, u_cols, Z, G, tw)
    H1 = Z
    mixer_gate(nc, G, H0, H1)
    if debug == "h1":
        return dump(nc, H1, out)
    X3 = u_cols

    def ffn_in(dve, k, p, at, n, centred, rstd, done, inner, ps_x, extra_ps, extra_done, stored):
        nc.vector.tensor_tensor(X3[:, ds(at, n)], centred[:, 0:n], rstd[:, 0:n], ALU.mult).then_inc(done, 1)

    channel_norm(nc, "cn1", H1, con, ffn_in, None)
    router(nc, X3, tw, ew1, ew2, w1_sel, w2_sel, b1_sel, b2_mix)
    Y = f_cols
    experts(nc, X3, Y, w1_sel, w2_sel, b1_sel, b2_mix)
    res = [sb(f"res{i}", [P, CH]) for i in range(2)]
    scaled = [sb(f"scaled{i}", [P, CH]) for i in range(2)]

    def final(dve, k, p, at, n, centred, rstd, done, inner, ps_x, extra_ps, extra_done, stored):
        nc.vector.scalar_tensor_tensor(scaled[p][:, 0:n], centred[:, 0:n], tw("gamma"), rstd[:, 0:n], ALU.mult, ALU.mult).then_inc(inner, 1)
        dve.wait_ge(inner, k + 1)
        wait(dve, stored[p], 8 * k - 8 * p)
        nc.vector.scalar_tensor_tensor(res[p][:, 0:n], scaled[p][:, 0:n], tw("beta"), H1[:, ds(at, n)], ALU.add, ALU.add).then_inc(done, 1)

    def store(sp, k, p, at, n, done, stored):
        sp.wait_ge(done, k + 1)
        sp.dma_start(out[:, ds(at, n)], res[p][:, 0:n]).then_inc(stored[p], 16)

    channel_norm(nc, "cn2", Y, con, final, None, out_dma=store)


def _dup(a):
    return np.concatenate([a, a], axis=0)


def _col(v):
    return _dup(v.reshape(-1, 1))


def _blockdiag(a):
    z = np.zeros((2 * C, 2 * C), np.float32)
    z[:C, :C] = a
    z[C:, C:] = a
    return z


def _rows(v, n=P):
    return np.broadcast_to(v.reshape(1, -1), (n, v.size))


def _pack(order, parts):
    return np.ascontiguousarray(np.concatenate([parts[n] for n, _ in order], axis=1), dtype=np.float32)


def kernel(_debug=None, **inputs):
    import concourse.bacc as _bacc
    from concourse.bass_utils import run_bass_kernel_spmd as _run

    a = {k: np.asarray(v) for k, v in inputs.items()}
    x = a["x"].reshape(2, 2, NW, WS, 4, NW, WS, 4)
    x = x.transpose(4, 7, 2, 5, 0, 1, 3, 6).reshape(PATCH, U, 2, 2, TOK)
    pat = np.zeros((PATCH + 1, U, 2, 2, C), np.float32)
    pat[:PATCH, ..., :TOK] = x
    pat[PATCH, ..., :TOK] = 1.0
    pat = np.ascontiguousarray(pat.reshape(PATCH + 1, TILES // 4, 4 * P).transpose(1, 0, 2))
    patch_w = np.concatenate([a["L0_tok_pe_w"].reshape(C, PATCH).T, a["L0_tok_pe_b"].reshape(1, C)], axis=0)

    p = np.arange(P)
    same_half = (p[:, None] // C == p[None, :] // C)
    common = _pack(COMMON_COLS, {
        "ident": np.eye(P, dtype=np.float32),
        "mean_ones": same_half.astype(np.float32) / C,
        "head_mask": ((p[:, None] % C) // HD == np.arange(NH)[None, :]).astype(np.float32),
        "pg_row": _rows(a["L0_tok_pe_ng"]), "pbeta_row": _rows(a["L0_tok_pe_nb"])})
    blocks, biases = [], []
    coords = np.stack(np.meshgrid(np.arange(WS), np.arange(WS), indexing="ij")).reshape(2, -1)
    rel = coords[:, :, None] - coords[:, None, :] + WS - 1
    rpi = rel[0] * (2 * WS - 1) + rel[1]
    for b in range(2):
        w = a["L0_tok_qkv_w"][b]
        qb = a["L0_tok_qkv_b"][b]
        w1T = a["L0_tok_w1"][b].T
        w2 = a["L0_tok_w2"][b].T.reshape(2, P, C).transpose(1, 0, 2).reshape(P, 2 * C)
        blocks.append(_pack(BLOCK_COLS, {
            "qBD": _blockdiag(w[:C].T), "kBD": _blockdiag(w[C:2 * C].T), "vBD": _blockdiag(w[2 * C:].T),
            "pBD": _blockdiag(a["L0_tok_proj_w"][b].T), "w2T": w2,
            "w1T0": np.concatenate([w1T, np.zeros_like(w1T)]), "w1T1": np.concatenate([np.zeros_like(w1T), w1T]),
            "n1g": _col(a["L0_tok_n1g"][b]), "n1b": _col(a["L0_tok_n1b"][b]),
            "qb": _col(qb[:C]), "kb": _col(qb[C:2 * C]), "vb": _col(qb[2 * C:]),
            "n2g": _col(a["L0_tok_n2g"][b]), "n2b": _col(a["L0_tok_n2b"][b]),
            "b1": a["L0_tok_b1"][b].reshape(2, P).T,
            "pb_row": _rows(a["L0_tok_proj_b"][b]), "b2": _col(a["L0_tok_b2"][b])}))
        t = a["L0_tok_rpb"][b][rpi].transpose(0, 2, 1).reshape(TOK, NH * TOK)
        z = np.zeros((2, C, NH * TOK), np.float32)
        z[:, :TOK] = t
        biases.append(z.reshape(P, NH * TOK))
    part = np.arange(WS) >= WS - SHIFT
    row_part, col_part = np.repeat(part, WS), np.tile(part, WS)
    masks = np.zeros((2, C, 4, TOK), np.float32)
    for v in range(4):
        label = row_part * (v >> 1) * 2 + col_part * (v & 1)
        masks[:, :TOK, v] = np.where(label[:, None] != label[None, :], -100.0, 0.0)
    masks = masks.reshape(P, 4, TOK)
    pick = np.zeros((2, P, P), np.float32)
    pick[0, 0, :] = 1.0
    pick[1, C, :] = 1.0
    tail_w = _pack(TAIL_COLS, {
        "BBD": _blockdiag(a["L0_attn_W_B"].T), "CBD": _blockdiag(a["L0_attn_W_C"].T), "DBD": _blockdiag(a["L0_attn_W_D"].T),
        "a": _col(a["L0_attn_a"]), "bB": _col(a["L0_attn_b_B"]), "bC": _col(a["L0_attn_b_C"]), "bD": _col(a["L0_attn_b_D"]),
        "cls": _col(a["cls_tok"].reshape(C)), "Wr": _dup(a["L0_ffn_Wr"]),
        "br_row": np.concatenate([_rows(a["L0_ffn_br"])] * 2, axis=1),
        "gamma": _col(a["L0_ffn_gamma"]), "beta": _col(a["L0_ffn_beta"]), "b2T": _dup(a["L0_ffn_b2"].T), "b1T": a["L0_ffn_b1"].T,
        "group_ones": same_half.astype(np.float32), "all_ones": np.ones((P, P), np.float32),
        "pick0": pick[0], "pick1": pick[1],
        "index_row": _rows(np.arange(N_EXP, 0, -1).astype(np.float32))})
    ew1 = _dup(a["L0_ffn_W1"].transpose(1, 0, 2).reshape(C, N_EXP * FF))
    ew2 = np.ascontiguousarray(a["L0_ffn_W2"].transpose(1, 0, 2).reshape(FF, N_EXP * C))

    nc = _bacc.Bacc("TRN2", target_bir_lowering=False, num_devices=1)
    arrays, args = {}, []
    for name, v in (("patches", pat), ("patch_w", patch_w), ("common", common), ("blocks", np.stack(blocks)),
                    ("biases", np.stack(biases)), ("masks", masks), ("tail_w", tail_w), ("ew1", ew1), ("ew2", ew2)):
        v = np.ascontiguousarray(v)
        arrays[f"in_{name}"] = v
        args.append(nc.dram_tensor(f"in_{name}", v.shape, mybir.dt.from_np(v.dtype), kind="ExternalInput").ap())
    shape = {None: (P, 2 * SEQ), "m0": (P, TILES, ROW), "a1": (P, TILES, ROW), "m1": (P, 2, PAD, PAD), "h1": (P, COLS)}[_debug]
    out = nc.dram_tensor("out", shape, F32, kind="ExternalOutput").ap()
    build(nc, *args, out, debug=_debug)
    r = _run(nc, [arrays], core_ids=[0])
    got = r.results[0]["out"]
    got = got.reshape(2, C, 2 * SEQ)
    image = got[:, :, :2 * TIME].reshape(2, C, 2, TIME).transpose(0, 2, 3, 1).reshape(4, TIME, C)
    first = got[:, :, 2 * TIME:].transpose(0, 2, 1).reshape(4, 1, C)
    return np.ascontiguousarray(np.concatenate([first, image], axis=1))
```

```python
from contextlib import ExitStack

import numpy as np

import concourse.bass as bass
from concourse import mybir

F32 = mybir.dt.float32
BF16 = mybir.dt.bfloat16
ALU = mybir.AluOpType
ACT = mybir.ActivationFunctionType
AX = mybir.AxisListType
ds = bass.ds

P = 128
C = 64
NH, HD = 8, 8
WS, SHIFT = 7, 3
TOK = WS * WS
NW = 8
SIDE = WS * NW
U = NW * NW
TILES = 2 * U
HID = 4 * C
EPS = 1e-5
SCALE = HD ** -0.5
PATCH = 16
NMR, RSTD = C, C + 1
ROW = C + 2
PAD = SIDE + SHIFT
N_EXP, FF = 8, 128
TIME = SIDE * SIDE
SEQ = TIME + 1
CAPACITY = float(-(-4 * SEQ * 5 // (4 * N_EXP)))
DT = 1.0 / SEQ

BLOCK_COLS = [("qBD", P), ("kBD", P), ("vBD", P), ("pBD", P), ("w1T0", HID), ("w1T1", HID), ("w2T", 2 * C),
              ("n1g", 1), ("n1b", 1), ("qb", 1), ("kb", 1), ("vb", 1), ("n2g", 1), ("n2b", 1), ("b1", 2),
              ("b2", 1), ("pb_row", C)]
COMMON_COLS = [("ident", P), ("mean_ones", P), ("head_mask", NH), ("pg_row", C), ("pbeta_row", C)]
TAIL_COLS = [("BBD", P), ("CBD", P), ("DBD", P), ("a", 1), ("bB", 1), ("bC", 1), ("bD", 1), ("cls", 1),
             ("Wr", N_EXP), ("br_row", 2 * N_EXP), ("gamma", 1), ("beta", 1), ("b2T", N_EXP), ("b1T", N_EXP),
             ("group_ones", P), ("all_ones", P), ("pick0", P), ("pick1", P), ("index_row", N_EXP)]


def columns(cols):
    at, out = 0, {}
    for name, n in cols:
        out[name] = (at, n)
        at += n
    return out, at


BLOCK_AT, BLOCK_W = columns(BLOCK_COLS)
COMMON_AT, COMMON_W = columns(COMMON_COLS)
TAIL_AT, TAIL_W = columns(TAIL_COLS)


def live(u, n=U):
    return not isinstance(u, int) or 0 <= u < n


def wait(eng, sem, value):
    if isinstance(value, int) and value <= 0:
        return
    eng.wait_ge(sem, value)


def skewed(eng, step, first, last):
    for s in range(first, NW):
        step(s, s % NW)
    with eng.Fori(1, NW - 1) as row:
        for c in range(NW):
            step(row * NW + c, c)
    for s in range(NW * (NW - 1), last + 1):
        step(s, s % NW)


def build(nc, patches, patch_w, common_in, block_in, bias_in, mask_in, tail_in, ew1_in, ew2_in, out, debug=None):
    ctx = ExitStack()
    with ctx:
        def sb(name, shape, dt=F32):
            return ctx.enter_context(nc.sbuf_tensor(name, shape, dt))

        X = sb("X", [P, TILES, ROW])
        X2 = sb("X2", [P, TILES, ROW])
        XT = sb("XT", [P, 2, PAD, PAD])
        common = sb("common", [P, COMMON_W])
        block_w = [sb(f"block_w{b}", [P, BLOCK_W]) for b in range(2)]

        def con(name):
            at, n = COMMON_AT[name]
            return common[:, at:at + n]

        def wt(b, name):
            at, n = BLOCK_AT[name]
            return block_w[b][:, at:at + n]

        tables = [BiasTables(nc, ctx, b) for b in range(2)]
        load_and_embed(nc, X, X2, common, block_w, con, tables[0], patches, patch_w, common_in, block_in, bias_in, mask_in)
        attention(nc, 0, X, con, wt, tables[0], None)
        mlp(nc, 0, X, con, wt, None, Roll(nc, X, X2), tables[1], bias_in, mask_in)
        if debug == "m0":
            return dump(nc, X, out)
        recycle(nc)
        with nc.semaphore("rolled") as rolled:
            attention(nc, 1, X2, con, wt, tables[1], (Roll(nc, X, X2), rolled))
        if debug == "a1":
            return dump(nc, X2, out)
        mlp(nc, 1, X2, con, wt, XT, None, None, bias_in, mask_in)
        if debug == "m1":
            return dump(nc, XT, out)
        tail(nc, ctx, X, X2, XT, con, tail_in, ew1_in, ew2_in, out, debug)


def clear_spent(nc):
    spent = sorted(nc.released_uncleared_semaphores)
    while spent:
        first = last = spent.pop(0)
        while spent and spent[0] == last + 1:
            last = spent.pop(0)
        nc.gpsimd.sem_clear(range(first, last + 1))


def dump(nc, T, out):
    with nc.semaphore("dumped") as s, nc.Block() as block:
        @block.sync
        def _(sp):
            sp.dma_start(out, T[:]).then_inc(s, 16)
            sp.wait_ge(s, 16)


def paired(eng, step, first, last, loop_from, loop_to, per=2):
    assert loop_from % per == 0 and (loop_to + 1) % per == 0
    for k in range(first, loop_from):
        step(k, k % per, k // per)
    with eng.Fori(loop_from // per, (loop_to + 1) // per) as i:
        for p in range(per):
            step(per * i + p, p, i)
    for k in range(loop_to + 1, last + 1):
        step(k, k % per, k // per)


def at_most(value, n):
    return min(value, n) if isinstance(value, int) else value


class BiasTables:

    def __init__(self, nc, ctx, b):
        self.nc, self.b = nc, b
        self.NV = 4 if b else 1
        sb = lambda name, shape: ctx.enter_context(nc.sbuf_tensor(f"bias{b}_{name}", shape, BF16))
        self.hi_mid = sb("hi_mid", [P, NH * TOK])
        self.lo = sb("lo", [P, self.NV, NH * TOK])

    def scratch(self, ctx):
        sb = lambda name, shape, dt=F32: ctx.enter_context(self.nc.sbuf_tensor(f"bias{self.b}_{name}", shape, dt))
        self.raw, self.mask = sb("raw", [P, NH * TOK]), sb("mask", [P, 4, TOK])
        self.rest, self.rest2 = (sb(name, [P, NH * TOK]) for name in ("rest", "rest2"))
        self.hi_all, self.mid_all = (sb(name, [P, NH * TOK], BF16) for name in ("hi_all", "mid_all"))
        self.loaded = ctx.enter_context(self.nc.semaphore(f"bias{self.b}_loaded"))
        self.made = ctx.enter_context(self.nc.semaphore(f"bias{self.b}_made"))

    def load(self, sp, bias_in, mask_in):
        sp.dma_start(self.raw[:], bias_in[self.b]).then_inc(self.loaded, 16)
        sp.dma_start(self.mask[:], mask_in).then_inc(self.loaded, 16)

    def make(self, eng, api):
        count = [0]

        def link(ins):
            count[0] += 1
            ins.then_inc(self.made, 1)
            eng.wait_ge(self.made, count[0])

        eng.wait_ge(self.loaded, 32)
        link(api.tensor_copy(self.hi_all[:], self.raw[:]))
        link(api.tensor_tensor(self.rest[:], self.raw[:], self.hi_all[:], ALU.subtract))
        link(api.tensor_copy(self.mid_all[:], self.rest[:]))
        link(api.tensor_tensor(self.rest2[:], self.rest[:], self.mid_all[:], ALU.subtract))
        api.tensor_copy(self.hi_mid[0:C, :], self.hi_all[0:C, :])
        link(api.tensor_copy(self.hi_mid[C:P, :], self.mid_all[C:P, :]))
        for v in range(self.NV):
            api.tensor_copy(self.lo[0:C, v, :], self.rest2[0:C, :])
            link(api.tensor_copy(self.lo[C:P, v, :].rearrange("p (h k) -> p h k", h=NH),
                                 self.mask[C:P, v, :].unsqueeze(1).to_broadcast([C, NH, TOK])))


class NormScalars:

    def __init__(self, nc, ctx, prefix, X, n):
        sb = lambda name, shape, dt=F32: ctx.enter_context(nc.sbuf_tensor(prefix + name, shape, dt))
        sem = lambda name: ctx.enter_context(nc.semaphore(prefix + name))
        self.nc, self.X, self.n = nc, X, n
        self.st = [sb(f"st{i}", [P, n, 6]) for i in range(2)]
        self.mv = [sb(f"mv{i}", [P, n, 2]) for i in range(2)]
        self.ve = sb("ve", [P, n])
        self.rs = [sb(f"rs{i}", [P, n]) for i in range(2)]
        self.eps, self.half = sb("eps", [P, n]), sb("half", [P, n])
        self.stats = sem("stats")
        self.aggr = sem("aggr")
        self.ve_set = sem("ve_set")
        self.rs_ready = sem("rs_ready")
        self.kept = sem("kept")
        self.set_up = sem("set_up")

    def prepare(self, pool):
        self.nc.gpsimd.memset(self.eps[:], EPS).then_inc(self.set_up, 1)
        self.nc.gpsimd.memset(self.half[:], -0.5).then_inc(self.set_up, 1)
        pool.wait_ge(self.set_up, 2)

    def statistics(self, k, p):
        for t in range(self.n):
            last = self.nc.vector.bn_stats(self.st[p][:, t, :], self.X[:, ds(k * self.n + t, 1), 0:C].rearrange("p o c -> p (o c)"))
        last.then_inc(self.stats, 1)

    def aggregate(self, k, p):
        for t in range(self.n):
            last = self.nc.vector.bn_aggr(self.mv[p][:, t, :], self.st[p][:, t, :])
        last.then_inc(self.aggr, 1)

    def invert(self, pool, k, p):
        var = self.mv[p][:, :, 1]
        wait(pool, self.rs_ready, k)
        pool.wait_ge(self.aggr, k + 1)
        self.nc.gpsimd.tensor_tensor(self.ve[:], var, self.eps[:], ALU.add).then_inc(self.ve_set, 1)
        wait(pool, self.kept, 2 * (k - 1))
        pool.wait_ge(self.ve_set, k + 1)
        self.nc.gpsimd.tensor_tensor(self.rs[p][:], self.ve[:], self.half[:], ALU.pow).then_inc(self.rs_ready, 1)

    def keep(self, dve, k, p):
        tiles = ds(k * self.n, self.n)
        dve.wait_ge(self.rs_ready, k + 1)
        rs, mean = self.rs[p][:].unsqueeze(2), self.mv[p][:, :, 0:1]
        self.nc.vector.tensor_scalar(self.X[:, tiles, RSTD:ROW], rs, 1.0, None, ALU.mult).then_inc(self.kept, 1)
        self.nc.vector.scalar_tensor_tensor(self.X[:, tiles, NMR:RSTD], mean, -1.0, rs, ALU.mult, ALU.mult).then_inc(self.kept, 1)


def load_and_embed(nc, X, X2, common, block_w, con, tables, patches, patch_w, common_in, block_in, bias_in, mask_in):
    with ExitStack() as ctx:
        sb = lambda name, shape, dt=F32: ctx.enter_context(nc.sbuf_tensor(name, shape, dt))
        pb = lambda name, shape, dt=F32: ctx.enter_context(nc.psum_tensor(name, shape, dt))
        sem = lambda name: ctx.enter_context(nc.semaphore(name))
        GT = 8
        K = TILES // GT
        pw = sb("pw", [PATCH + 1, C])
        pw_mean = sb("pw_mean", [PATCH + 1, 1])
        pw_c = sb("pw_c", [PATCH + 1, C])
        DEEP = 4
        ring = [sb(f"patch_ring{i}", [PATCH + 1, GT * P]) for i in range(DEEP)]
        sq = [sb(f"sq{i}", [P, C]) for i in range(2)]
        var = [sb(f"pvar{i}", [P, GT]) for i in range(DEEP)]
        ve = sb("pve", [P, GT])
        rs = [sb(f"prs{i}", [P, GT]) for i in range(2)]
        gained = [sb(f"gained{i}", [P, GT, C]) for i in range(2)]
        ps = [pb(f"pe_ps{i}", [P, 512]) for i in range(DEEP)]

        weights_in = sem("weights_in")
        pw_in = sem("pw_in")
        patch_in = [sem(f"patch_in{i}") for i in range(DEEP)]
        cleared = sem("cleared")
        pw_m = sem("pw_m")
        pw_ready = sem("pw_ready")
        embedded = sem("embedded")
        squared = sem("squared")
        ve_ready = sem("ve_ready")
        rs_ready = sem("rs_ready")
        scaled = sem("scaled")
        placed = sem("placed")
        norm = NormScalars(nc, ctx, "em_", X, GT)
        tables.scratch(ctx)
        is_live = lambda k: live(k, K)
        with nc.Block() as block:
            @block.sync
            def _(sp):
                sp.dma_start(pw[:], patch_w).then_inc(pw_in, 16)

                def load(k, q, turn):
                    wait(sp, embedded, k - DEEP + 1)
                    sp.dma_start(ring[q][:], patches[ds(k, 1), :, :].rearrange("o p n -> (o p) n")).then_inc(patch_in[q], 16)

                load(0, 0, 0)
                tables.load(sp, bias_in, mask_in)
                for k in range(1, DEEP):
                    load(k, k, 0)
                sp.dma_start(common[:], common_in).then_inc(weights_in, 16)
                for b in range(2):
                    sp.dma_start(block_w[b][:], block_in[b]).then_inc(weights_in, 16)
                paired(sp, load, DEEP, K - 1, 2 * DEEP, K - 1, DEEP)
                sp.wait_ge(weights_in, 48)

            @block.tensor
            def _(pe):
                pe.wait_ge(pw_ready, 1)

                def step(k, q, turn):
                    pe.wait_ge(patch_in[q], 16 * turn + 16)
                    wait(pe, squared, GT * (k - DEEP + 1))
                    wait(pe, scaled, k - DEEP + 1)
                    for t in range(GT):
                        last = nc.tensor.matmul(ps[q][:, t * C:(t + 1) * C], ring[q][:, t * P:(t + 1) * P], pw_c[:],
                                                start=True, stop=True)
                    last.then_inc(embedded, 1)

                paired(pe, step, 0, K - 1, DEEP, K - 1, DEEP)

            @block.scalar
            def _(act):
                def step(k, q, turn):
                    act.wait_ge(embedded, k + 1)
                    wait(act, ve_ready, k - DEEP + 1)
                    for t in range(GT):
                        wait(act, squared, GT * k + t - 1)
                        nc.scalar.activation(sq[t % 2][:], ps[q][:, t * C:(t + 1) * C], ACT.Square, scale=C ** -0.5,
                                             accum_out=var[q][:, t:t + 1]).then_inc(squared, 1)

                paired(act, step, 0, K - 1, DEEP, K - 1, DEEP)

            @block.gpsimd
            def _(pool):
                norm.prepare(pool)
                nc.gpsimd.memset(X2[:], 0.0).then_inc(cleared, 1)
                pool.wait_ge(cleared, 1)

                def step(k, q, turn):
                    p = q % 2
                    if is_live(k):
                        wait(pool, rs_ready, k)
                        pool.wait_ge(squared, GT * k + GT)
                        nc.gpsimd.tensor_tensor(ve[:], var[q][:], norm.eps[:], ALU.add).then_inc(ve_ready, 1)
                        pool.wait_ge(ve_ready, k + 1)
                        wait(pool, scaled, k - 1)
                        nc.gpsimd.tensor_tensor(rs[p][:], ve[:], norm.half[:], ALU.pow).then_inc(rs_ready, 1)
                    if is_live(k - 4):
                        norm.invert(pool, k - 4, p)

                paired(pool, step, 0, K + 3, 2 * DEEP, K - 1, DEEP)

            @block.vector
            def _(dve):
                dve.wait_ge(pw_in, 16)
                nc.vector.reduce_sum(pw_mean[:], pw[:], AX.X).then_inc(pw_m, 1)
                dve.wait_ge(pw_m, 1)
                nc.vector.tensor_scalar(pw_mean[:], pw_mean[:], 1.0 / C, None, ALU.mult).then_inc(pw_m, 1)
                dve.wait_ge(pw_m, 2)
                nc.vector.tensor_scalar(pw_c[:], pw[:], pw_mean[:, 0:1], None, ALU.subtract).then_inc(pw_ready, 1)
                tables.make(dve, nc.vector)
                dve.wait_ge(weights_in, 48)
                gain = con("pg_row")
                offset = con("pbeta_row").unsqueeze(1).to_broadcast([P, GT, C])

                def step(k, q, turn):
                    p = q % 2
                    wait(dve, placed, at_most(k - 1, K))
                    wait(dve, norm.stats, at_most(k - 2, K))
                    wait(dve, norm.aggr, at_most(k - 3, K))
                    if is_live(k):
                        dve.wait_ge(rs_ready, k + 1)
                        for t in range(GT):
                            last = nc.vector.scalar_tensor_tensor(gained[p][:, t, :], ps[q][:, t * C:(t + 1) * C],
                                                                  rs[p][:, t:t + 1], gain, ALU.mult, ALU.mult)
                        last.then_inc(scaled, 1)
                    if is_live(k - 5):
                        norm.keep(dve, k - 5, 1 - p)
                    wait(dve, norm.kept, at_most(2 * (k - 4), 2 * K))
                    if is_live(k - 1):
                        dve.wait_ge(scaled, k)
                        nc.vector.tensor_tensor(X[:, ds((k - 1) * GT, GT), 0:C], gained[1 - p][:], offset, ALU.add).then_inc(placed, 1)
                    if is_live(k - 2):
                        norm.statistics(k - 2, p)
                    if is_live(k - 3):
                        norm.aggregate(k - 3, 1 - p)

                paired(dve, step, 0, K + 4, 2 * DEEP, K - 1, DEEP)


def attention(nc, b, X, con, wt, bias, arriving):
    with ExitStack() as ctx:
        sb = lambda name, shape, dt=F32: ctx.enter_context(nc.sbuf_tensor(f"at{b}_{name}", shape, dt))
        pb = lambda name, shape, dt=F32: ctx.enter_context(nc.psum_tensor(f"at{b}_{name}", shape, dt))
        sem = lambda name: ctx.enter_context(nc.semaphore(f"at{b}_{name}"))
        KH = NH * TOK

        select = sb("select", [P, P], BF16)
        qbs = sb("qbs", [P, 1])
        vb_wide = sb("vb_wide", [C, P])
        const_row = sb("const_row", [P, C])
        xn = [sb(f"xn{i}", [P, 2, C]) for i in range(2)]
        xT = [sb(f"xT{i}", [P, 2, 2, C]) for i in range(2)]
        q_bd = [sb(f"q_bd{i}", [P, 2, 2, C]) for i in range(2)]
        k_sb = sb("k_sb", [P, 2, TOK])
        k_bd = [sb(f"k_bd{i}", [P, 2, NH, TOK]) for i in range(2)]
        v_bd = [sb(f"v_bd{i}", [P, 2, 2, NH // 2, 2, HD + 1]) for i in range(2)]
        prob = [sb(f"prob{w}", [P, NH, C]) for w in range(2)]
        mx = [sb(f"mx{w}", [P, NH]) for w in range(2)]
        probT = [sb(f"probT{w}", [P, NH // 2, P]) for w in range(2)]
        rsum = sb("rsum", [P, 2 * NH // 2, 2])
        o = sb("o", [P, 2, C])
        oT = sb("oT", [P, P])

        ps_xt = pb("ps_xt", [P, 512])
        ps_qkv = pb("ps_qkv", [P, 512])
        ps_s = [pb(f"ps_s{w}", [P, 512]) for w in range(2)]
        ps_pt = [pb(f"ps_pt{w}", [P, 512]) for w in range(2)]
        ps_o = pb("ps_o", [P, 512])
        ps_misc = pb("ps_misc", [P, 512])
        PS_Q, PS_K, PS_V = 0, 2 * TOK, 4 * TOK
        PS_V = 256

        zeroed = sem("zeroed")
        initialised = sem("initialised")
        const_ps = sem("const_ps")
        const_ready = sem("const_ready")
        xn_ready = sem("xn_ready")
        offset_added = sem("offset_added")
        xt_ps = sem("xt_ps")
        xt_ready = sem("xt_ready")
        qkv_ps = sem("qkv_ps")
        k_ready = sem("k_ready")
        q_ready = sem("q_ready")
        kbd_ready = sem("kbd_ready")
        v_ready = sem("v_ready")
        s_ps = sem("s_ps")
        max_ready = sem("max_ready")
        shifted = sem("shifted")
        exp_ready = sem("exp_ready")
        pt_ps = sem("pt_ps")
        pt_ready = sem("pt_ready")
        pv_ps = sem("pv_ps")
        rsum_ready = sem("rsum_ready")
        o_ready = sem("o_ready")
        ot_ps = sem("ot_ps")
        ot_ready = sem("ot_ready")
        pr_ps = sem("pr_ps")
        x_ready = sem("x_ready")
        norm = NormScalars(nc, ctx, f"at{b}_", X, 2)

        with nc.Block() as block:
            if arriving is not None:
                roll, rolled = arriving

                @block.sync
                def _(sp):
                    sp.wait_ge(rolled, roll.issue(sp, rolled, 2, NW))

            @block.gpsimd
            def _(pool):
                norm.prepare(pool)
                mask_h = con("head_mask").unsqueeze(2).to_broadcast([P, NH, TOK])
                pool.wait_ge(const_ready, 1)
                row = const_row[:].unsqueeze(1).to_broadcast([P, 2, C])

                def step(s, c):
                    p = c % 2
                    if live(s + 1):
                        pool.wait_ge(k_ready, s + 2)
                        wait(pool, s_ps, 2 * s)
                        for w in range(2):
                            nc.gpsimd.tensor_tensor(k_bd[1 - p][:, w, :, :],
                                                    k_sb[:, w, :].unsqueeze(1).to_broadcast([P, NH, TOK]), mask_h,
                                                    ALU.mult).then_inc(kbd_ready, 1)
                    if live(s + 3):
                        pool.wait_ge(xn_ready, s + 4)
                        pool.wait_ge(const_ready, 1)
                        xs = X[:, ds((s + 3) * 2, 2), 0:C]
                        nc.gpsimd.tensor_tensor(xs, xs, row, ALU.add).then_inc(offset_added, 1)
                    if live(s - 5):
                        norm.invert(pool, s - 5, 1 - p)

                skewed(pool, step, -3, U + 4)

            @block.tensor
            def _(pe):
                pe.wait_ge(zeroed, 1)
                nc.tensor.matmul(ps_misc[:, 0:C], vb_wide[:], wt(b, "pBD")[0:C, 0:C], start=True, stop=True).then_inc(const_ps, 1)
                pe.wait_ge(const_ready, 1)

                def scores(s, c, w):
                    p = c % 2
                    pe.wait_ge(kbd_ready, 2 * s + w + 1)
                    if w == 0:
                        pe.wait_ge(q_ready, s + 1)
                    wait(pe, shifted, 2 * s + w - 1)
                    v = 0
                    if b:
                        v = (1 if c == NW - 1 else 0) + (2 if isinstance(s, int) and s >= U - NW else 0)
                    nc.tensor.matmul(ps_s[w][:, 0:KH], select[:], bias.hi_mid[:], start=True, stop=False)
                    nc.tensor.matmul(ps_s[w][:, 0:KH], select[:], bias.lo[:, v, :], start=False, stop=False)
                    nc.tensor.matmul(ps_s[w][:, 0:KH], q_bd[p][:, w, :, :].rearrange("p g q -> p (g q)"),
                                     k_bd[p][:, w, :, :].rearrange("p h k -> p (h k)"),
                                     start=False, stop=True).then_inc(s_ps, 1)

                def transpose_probs(u, w):
                    pe.wait_ge(exp_ready, 2 * u + w + 1)
                    wait(pe, pt_ready, 2 * u + w - 1)
                    for hp in range(NH // 2):
                        last = nc.tensor.transpose(ps_pt[w][:, hp * P:(hp + 1) * P],
                                                   prob[w][:, 2 * hp:2 * hp + 2, :].rearrange("p h k -> p (h k)"), con("ident"))
                    last.then_inc(pt_ps, 1)

                def attend(u, p, w):
                    pe.wait_ge(pt_ready, 2 * u + w + 1)
                    if w == 0:
                        pe.wait_ge(v_ready, u + 1)
                        wait(pe, o_ready, u)
                    for hp in range(NH // 2):
                        at = (w * 4 + hp) * 4 * (HD + 1)
                        last = nc.tensor.matmul(ps_o[:, at:at + 4 * (HD + 1)].rearrange("p (g e) -> p g e", g=2),
                                                probT[w][:, hp, :],
                                                v_bd[p][:, w, :, hp, :, :].rearrange("p g h e -> p g (h e)"),
                                                start=True, stop=True)
                    last.then_inc(pv_ps, 1)

                def step(s, c):
                    p = c % 2
                    if live(s):
                        scores(s, c, 0)
                    if live(s - 2):
                        pe.wait_ge(o_ready, s - 1)
                        wait(pe, x_ready, s - 2)
                        nc.tensor.transpose(ps_misc[:, 0:P], o[:].rearrange("p w c -> p (w c)"), con("ident")).then_inc(ot_ps, 1)
                    if live(s - 1):
                        transpose_probs(s - 1, 1)
                    if live(s + 1):
                        pe.wait_ge(xt_ready, s + 2)
                        wait(pe, v_ready, s + 1)
                        wait(pe, q_ready, s + 1)
                        tokens = xT[1 - p][:, :, 0, 0:TOK]
                        for at, name in ((PS_Q, "qBD"), (PS_K, "kBD")):
                            nc.tensor.matmul(ps_qkv[:, at:at + 2 * TOK].rearrange("p (w t) -> p w t", w=2), wt(b, name), tokens,
                                             start=True, stop=True)
                        for w in range(2):
                            twice = xT[1 - p][:, w, :, :].rearrange("p a t -> p (a t)")
                            last = nc.tensor.matmul(ps_qkv[:, PS_V + w * P:PS_V + (w + 1) * P], twice,
                                                    wt(b, "vBD"), start=True, stop=True)
                        last.then_inc(qkv_ps, 1)
                    if live(s - 1):
                        attend(s - 1, 1 - p, 0)
                    if live(s - 2):
                        pe.wait_ge(ot_ready, s - 1)
                        for w in range(2):
                            r = slice(C * w, C * w + C)
                            for g in range(2):
                                last = nc.tensor.matmul(ps_misc[r, P + g * C:P + (g + 1) * C], oT[:, C * g:C * g + C],
                                                        wt(b, "pBD")[:, r], start=True, stop=True)
                        last.then_inc(pr_ps, 1)
                    if live(s):
                        scores(s, c, 1)
                    if live(s + 2):
                        pe.wait_ge(xn_ready, s + 3)
                        wait(pe, xt_ready, s + 2)
                        nc.tensor.transpose(ps_xt[:, 0:P], xn[p][:].rearrange("p g c -> p (g c)"), con("ident")).then_inc(xt_ps, 1)
                    if live(s - 1):
                        attend(s - 1, 1 - p, 1)
                    if live(s):
                        transpose_probs(s, 0)

                skewed(pe, step, -2, U + 1)

            @block.scalar
            def _(act):
                def copy_probs(u, w):
                    act.wait_ge(pt_ps, 2 * u + w + 1)
                    wait(act, pv_ps, 2 * u + w - 1)
                    nc.scalar.activation(probT[w][:], ps_pt[w][:].rearrange("p (h q) -> p h q", q=P), ACT.Copy).then_inc(pt_ready, 1)

                def exponential(u, w):
                    act.wait_ge(shifted, 2 * u + w + 1)
                    e = prob[w][:, :, 0:TOK]
                    nc.scalar.activation(e, e, ACT.Exp).then_inc(exp_ready, 1)

                def step(s, c):
                    p = c % 2
                    if live(s - 2):
                        act.wait_ge(ot_ps, s - 1)
                        wait(act, pr_ps, s - 2)
                        nc.scalar.activation(oT[:], ps_misc[:, 0:P], ACT.Copy).then_inc(ot_ready, 1)
                    if live(s - 1):
                        copy_probs(s - 1, 1)
                    if live(s + 1):
                        act.wait_ge(qkv_ps, s + 2)
                        wait(act, kbd_ready, 2 * s + 2)
                        nc.scalar.activation(k_sb[:], ps_qkv[:, PS_K:PS_K + 2 * TOK].rearrange("p (w t) -> p w t", w=2),
                                             ACT.Identity, bias=wt(b, "kb")).then_inc(k_ready, 1)
                        wait(act, s_ps, 2 * s)
                        for g in range(2):
                            r = slice(C * g, C * g + C)
                            last = nc.scalar.activation(q_bd[1 - p][r, :, g, 0:TOK],
                                                        ps_qkv[r, PS_Q:PS_Q + 2 * TOK].rearrange("p (w t) -> p w t", w=2),
                                                        ACT.Identity, bias=qbs[r, :], scale=SCALE)
                        last.then_inc(q_ready, 1)
                    if live(s):
                        exponential(s, 0)
                    if live(s + 2):
                        act.wait_ge(xt_ps, s + 3)
                        wait(act, qkv_ps, s + 1)
                        nc.scalar.activation(xT[p][:], ps_xt[:, 0:P].rearrange("p (w t) -> p w t", w=2).unsqueeze(2)
                                             .to_broadcast([P, 2, 2, C]), ACT.Identity,
                                             bias=wt(b, "n1b"), scale=wt(b, "n1g")).then_inc(xt_ready, 1)
                    if live(s):
                        copy_probs(s, 0)
                        exponential(s, 1)
                    if live(s + 1):
                        wait(act, pv_ps, 2 * s)
                        for h in range(2):
                            r = slice(C * h, C * h + C)
                            src = ps_qkv[r, PS_V:PS_V + 4 * C].rearrange("p (x a h d) -> p x a h d", a=NH // 2, h=2, d=HD)[:, :, :, h, :]
                            last = nc.scalar.activation(v_bd[1 - p][r, :, :, :, h, 0:HD].rearrange("p w g a d -> p (w g) a d"), src, ACT.Copy)
                        last.then_inc(v_ready, 1)

                act.wait_ge(zeroed, 1)
                skewed(act, step, -2, U + 1)

            @block.vector
            def _(dve):
                for i in range(2):
                    nc.vector.memset(q_bd[i][:], 0.0)
                    nc.vector.memset(v_bd[i][:], 0.0)
                    nc.vector.memset(prob[i][:], 0.0)
                nc.vector.tensor_scalar(qbs[:], wt(b, "qb"), SCALE, None, ALU.mult)
                nc.vector.tensor_copy(vb_wide[:], wt(b, "vb")[0:C, :].to_broadcast([C, P]))
                nc.vector.tensor_copy(select[:].rearrange("p (g q) -> p g q", g=2)[0:C],
                                      con("ident")[0:C, 0:C].unsqueeze(1).to_broadcast([C, 2, C]))
                nc.vector.tensor_copy(select[:].rearrange("p (g q) -> p g q", g=2)[C:P],
                                      con("ident")[C:P, C:P].unsqueeze(1).to_broadcast([C, 2, C])).then_inc(initialised, 1)
                dve.wait_ge(initialised, 1)
                for i in range(2):
                    for h in range(2):
                        last = nc.vector.memset(v_bd[i][C * h:C * h + C, :, :, :, h, HD:HD + 1], 1.0)
                last.then_inc(zeroed, 1)
                dve.wait_ge(const_ps, 1)
                nc.vector.tensor_tensor(const_row[:], ps_misc[:, 0:C], wt(b, "pb_row"), ALU.add).then_inc(const_ready, 1)

                def normalize(dve, u, p):
                    wait(dve, xt_ps, u - 1)
                    for g in range(2):
                        last = nc.vector.tensor_scalar(xn[p][:, g, :], X[:, ds(2 * u + g, 1), 0:C].rearrange("p o c -> p (o c)"),
                                                       scalar(u, g, RSTD), scalar(u, g, NMR), ALU.mult, ALU.add)
                    last.then_inc(xn_ready, 1)

                def scalar(u, g, col):
                    return X[:, ds(2 * u + g, 1), col:col + 1].rearrange("p o c -> p (o c)")

                def shift(s, w, more=()):
                    dve.wait_ge(s_ps, 2 * s + w + 1)
                    sc = ps_s[w][:, 0:KH].rearrange("p (h k) -> p h k", h=NH)
                    nc.vector.reduce_max(mx[w][:], sc, AX.X).then_inc(max_ready, 1)
                    for sem_, value in more:
                        wait(dve, sem_, value)
                    dve.wait_ge(max_ready, 2 * s + w + 1)
                    wait(dve, pt_ps, 2 * s + w - 1)
                    nc.vector.tensor_tensor(prob[w][:, :, 0:TOK], sc, mx[w][:].unsqueeze(2).to_broadcast([P, NH, TOK]),
                                            ALU.subtract).then_inc(shifted, 1)

                def step(s, c):
                    p = c % 2
                    settled = ((x_ready, s - 2), (norm.stats, s - 3), (norm.aggr, s - 4))
                    if live(s):
                        shift(s, 0, settled)
                    else:
                        for sem_, value in settled:
                            wait(dve, sem_, min(value, U))
                    if live(s - 6):
                        norm.keep(dve, s - 6, p)
                    wait(dve, norm.kept, at_most(2 * (s - 5), 2 * U))
                    if arriving is not None and isinstance(s, int) and s + 3 == NW:
                        dve.wait_ge(rolled, roll.signals(2, NW))
                    if live(s + 3):
                        normalize(dve, s + 3, 1 - p)
                    if live(s - 3):
                        norm.statistics(s - 3, 1 - p)
                    if live(s - 4):
                        norm.aggregate(s - 4, p)
                    if live(s):
                        shift(s, 1)
                    if live(s - 2):
                        u = s - 2
                        dve.wait_ge(pr_ps, u + 1)
                        dve.wait_ge(offset_added, u + 1)
                        xs = X[:, ds(2 * u, 2), 0:C]
                        nc.vector.tensor_tensor(xs, xs, ps_misc[:, P:2 * P].rearrange("p (g c) -> p g c", g=2), ALU.add).then_inc(x_ready, 1)
                    if live(s - 1):
                        u = s - 1
                        dve.wait_ge(pv_ps, 2 * u + 2)
                        wait(dve, o_ready, u)
                        for g in range(2):
                            r = slice(C * g, C * g + C)
                            mine = ps_o[r, 0:32 * (HD + 1)].rearrange("p (x g h e) -> p x g h e", g=2, h=2, e=HD + 1)[:, :, g, :, :]
                            last = nc.vector.reciprocal(rsum[r, :, :].unsqueeze(3), mine[:, :, :, HD:HD + 1])
                        last.then_inc(rsum_ready, 1)
                        dve.wait_ge(rsum_ready, u + 1)
                        wait(dve, ot_ps, u)
                        for g in range(2):
                            r = slice(C * g, C * g + C)
                            mine = ps_o[r, 0:32 * (HD + 1)].rearrange("p (x g h e) -> p x g h e", g=2, h=2, e=HD + 1)[:, :, g, :, 0:HD]
                            last = nc.vector.tensor_tensor(o[r, :, :].rearrange("p w (a h d) -> p (w a) h d", h=2, d=HD), mine,
                                                           rsum[r, :, :].unsqueeze(3).to_broadcast([C, NH, 2, HD]), ALU.mult)
                        last.then_inc(o_ready, 1)

                skewed(dve, step, -3, U + 5)


def mlp(nc, b, X, con, wt, XT, roll, tables, bias_in, mask_in):
    with ExitStack() as ctx:
        sb = lambda name, shape, dt=F32: ctx.enter_context(nc.sbuf_tensor(f"ml{b}_{name}", shape, dt))
        pb = lambda name, shape, dt=F32: ctx.enter_context(nc.psum_tensor(f"ml{b}_{name}", shape, dt))
        sem = lambda name: ctx.enter_context(nc.semaphore(f"ml{b}_{name}"))
        GU = 4
        K = U // GU
        GT = 2 * GU
        COL = GT * TOK
        xn = [sb(f"xn{i}", [P, GT, C]) for i in range(2)]
        xT = [sb(f"xT{i}", [P, GT, TOK]) for i in range(2)]
        hid = [sb(f"hid{i}", [P, 2, 2, COL]) for i in range(2)]
        turn = [sb(f"turn{i}", [P, GT, C]) for i in range(2)]
        y_sb = [sb(f"y_sb{i}", [P, GT, TOK]) for i in range(2)]
        ps_xt = pb("ps_xt", [P, 512])
        ps_h = [[pb(f"ps_h{f}{g}", [P, 512]) for g in range(2)] for f in range(2)]
        ps_y = [pb(f"ps_y{i}", [P, 512]) for i in range(2)]
        ps_t = pb("ps_t", [P, 512])
        zeroed = sem("zeroed")
        scaled = sem("scaled")
        xn_ready = sem("xn_ready")
        xt_ps = sem("xt_ps")
        xt_ready = sem("xt_ready")
        h_ps = sem("h_ps")
        h_ready = sem("h_ready")
        y_ps = sem("y_ps")
        turn_ready = sem("turn_ready")
        y_ready = sem("y_ready")
        t_ps = sem("t_ps")
        x_ready = sem("x_ready")
        norm = NormScalars(nc, ctx, f"ml{b}_", X, GT)
        is_live = lambda k: live(k, K)
        first_block = XT is None
        if first_block:
            tables.scratch(ctx)
            rolled = sem("rolled")
        with nc.Block() as block:
            if first_block:
                @block.sync
                def _(sp):
                    tables.load(sp, bias_in, mask_in)
                    sp.wait_ge(norm.kept, 2 * 2 * NW // GU)
                    sp.wait_ge(rolled, roll.issue(sp, rolled, 0, 2))

            @block.gpsimd
            def _(pool):
                if first_block:
                    norm.prepare(pool)
                    tables.make(pool, nc.gpsimd)
                    paired(pool, lambda k, p, half: norm.invert(pool, k, p), 0, K - 1, 4, K - 1)

            @block.tensor
            def _(pe):
                def transpose_units(bank, src):
                    for u in range(GU):
                        last = nc.tensor.transpose(bank[:, u * P:(u + 1) * P],
                                                   src[:, 2 * u:2 * u + 2, :].rearrange("p t c -> p (t c)"), con("ident"))
                    return last

                def step(k, p, half):
                    if is_live(k):
                        pe.wait_ge(xt_ready, k + 1)
                        for f in range(2):
                            for g in range(2):
                                wait(pe, h_ready, 4 * (k - 1) + 2 * f + g + 1)
                                nc.tensor.matmul(ps_h[f][g][:, 0:COL], wt(b, f"w1T{g}")[:, f * P:(f + 1) * P],
                                                 xT[p][:].rearrange("p t c -> p (t c)"), start=True, stop=True).then_inc(h_ps, 1)
                    if is_live(k - 2):
                        pe.wait_ge(turn_ready, k - 1)
                        wait(pe, x_ready, k - 2)
                        transpose_units(ps_t, turn[p]).then_inc(t_ps, 1)
                    if is_live(k + 1):
                        pe.wait_ge(xn_ready, k + 2)
                        wait(pe, xt_ready, k + 1)
                        transpose_units(ps_xt, xn[1 - p]).then_inc(xt_ps, 1)
                    if is_live(k - 1):
                        wait(pe, turn_ready if first_block else y_ready, k - 2)
                        for f in range(2):
                            for g in range(2):
                                pe.wait_ge(h_ready, 4 * (k - 1) + 2 * f + g + 1)
                                last = nc.tensor.matmul(ps_y[1 - p][g * C:(g + 1) * C, 0:COL], wt(b, "w2T")[:, f * C:(f + 1) * C],
                                                        hid[1 - p][:, f, g, :], start=(f == 0), stop=(f == 1))
                        last.then_inc(y_ps, 1)

                paired(pe, step, -1, K + 1, 6, 13)

            @block.scalar
            def _(act):
                act.wait_ge(zeroed, 1)

                def step(k, p, half):
                    if is_live(k):
                        wait(act, y_ps, k - 1)
                        for f in range(2):
                            for g in range(2):
                                act.wait_ge(h_ps, 4 * k + 2 * f + g + 1)
                                nc.scalar.activation(hid[p][:, f, g, :], ps_h[f][g][:, 0:COL], ACT.Gelu,
                                                     bias=wt(b, "b1")[:, f:f + 1]).then_inc(h_ready, 1)
                    if is_live(k - 1):
                        wait(act, t_ps, k - 2)
                        if first_block:
                            act.wait_ge(y_ps, k)
                            nc.scalar.activation(turn[1 - p][:, :, 0:TOK], ps_y[1 - p][:, 0:COL].rearrange("p (t c) -> p t c", c=TOK),
                                                 ACT.Identity, bias=wt(b, "b2")).then_inc(turn_ready, 1)
                        else:
                            nc.scalar.activation(turn[1 - p][:], X[:, ds((k - 1) * GT, GT), 0:C], ACT.Copy).then_inc(turn_ready, 1)
                            act.wait_ge(y_ps, k)
                            wait(act, x_ready, k - 2)
                            nc.scalar.activation(y_sb[1 - p][:], ps_y[1 - p][:, 0:COL].rearrange("p (t c) -> p t c", c=TOK),
                                                 ACT.Identity, bias=wt(b, "b2")).then_inc(y_ready, 1)

                paired(act, step, 0, K, 6, 13)

            @block.vector
            def _(dve):
                for i in range(2):
                    last = nc.vector.memset(turn[i][:], 0.0)
                last.then_inc(zeroed, 1)

                def columns_of(col, k):
                    return X[:, ds(k * GT, GT), col:col + 1].to_broadcast([P, GT, C])

                def finish(k, p, half):
                    dve.wait_ge(t_ps, k + 1)
                    if not first_block:
                        dve.wait_ge(y_ready, k + 1)
                    if first_block:
                        xs = X[:, ds(k * GT, GT), 0:C]
                        nc.vector.tensor_tensor(xs, xs, ps_t[:].rearrange("p (u g c) -> p (u g) c", g=2, c=C), ALU.add).then_inc(x_ready, 1)
                        return
                    for u in range(GU):
                        wcol = GU * p + u
                        for w in range(2):
                            last = nc.vector.tensor_tensor(
                                XT[:, w, ds(half * WS + SHIFT, WS), wcol * WS + SHIFT:wcol * WS + SHIFT + WS],
                                y_sb[p][:, 2 * u + w, :].rearrange("p (i j) -> p i j", j=WS),
                                ps_t[:, u * P + w * C:u * P + w * C + TOK].rearrange("p (i j) -> p i j", j=WS), ALU.add)
                    last.then_inc(x_ready, 1)

                def step(k, p, half):
                    if first_block:
                        wait(dve, x_ready, at_most(k - 2, K))
                        wait(dve, norm.stats, at_most(k - 3, K))
                        wait(dve, norm.aggr, at_most(k - 4, K))
                    if is_live(k + 2):
                        wait(dve, xt_ps, k + 1)
                        nc.vector.tensor_tensor(xn[p][:], X[:, ds((k + 2) * GT, GT), 0:C], columns_of(RSTD, k + 2), ALU.mult).then_inc(scaled, 1)
                    if first_block:
                        if is_live(k - 5):
                            norm.keep(dve, k - 5, 1 - p)
                        if is_live(k - 3):
                            norm.statistics(k - 3, 1 - p)
                        wait(dve, norm.kept, at_most(2 * (k - 5), 2 * K))
                    if is_live(k + 2):
                        dve.wait_ge(scaled, k + 3)
                        nc.vector.tensor_tensor(xn[p][:], xn[p][:], columns_of(NMR, k + 2), ALU.add).then_inc(xn_ready, 1)
                    if first_block and is_live(k - 4):
                        norm.aggregate(k - 4, p)
                    if is_live(k + 1):
                        dve.wait_ge(xt_ps, k + 2)
                        wait(dve, h_ps, 4 * k)
                        nc.vector.tensor_scalar(xT[1 - p][:], ps_xt[:].rearrange("p (t c) -> p t c", c=C)[:, :, 0:TOK],
                                                wt(b, "n2g"), wt(b, "n2b"), ALU.mult, ALU.add).then_inc(xt_ready, 1)
                    if is_live(k - 2):
                        finish(k - 2, p, half - 1)

                paired(dve, step, -2, K + 4 if first_block else K + 1, 6, 13)


class Roll:

    def __init__(self, nc, X, X2):
        self.src = X[:].rearrange("p (a b g) r -> p a b (g r)", a=NW, b=NW)
        self.dst = X2[:].rearrange("p (a b g) r -> p a b (g r)", a=NW, b=NW)

    @staticmethod
    def moves(first, end):
        for w in range(2):
            for i in range(WS):
                for j0, j1 in ((0, SHIFT), (SHIFT, WS)):
                    up, left = i < SHIFT, j0 < SHIFT
                    frm = C * w + WS * i + j0
                    to = C * w + WS * ((i - SHIFT) % WS) + (j0 - SHIFT) % WS
                    rows = [(first, end, first)]
                    if up:
                        rows = [(max(first, 1), end, max(first, 1) - 1)] + ([(0, 1, NW - 1)] if first == 0 else [])
                    cols = [(0, NW, 0)] if not left else [(1, NW, 0), (0, 1, NW - 1)]
                    for a0, a1, a2 in rows:
                        for b0, b1, b2 in cols:
                            yield frm, to, j1 - j0, a0, a1, a2, b0, b1, b2

    def signals(self, first, end):
        return 16 * len(list(self.moves(first, end)))

    def issue(self, eng, rolled, first, end):
        for frm, to, n, a0, a1, a2, b0, b1, b2 in self.moves(first, end):
            eng.dma_start(self.dst[to:to + n, a2:a2 + a1 - a0, b2:b2 + b1 - b0, :],
                          self.src[frm:frm + n, a0:a1, b0:b1, :]).then_inc(rolled, 16)
        return self.signals(first, end)


def recycle(nc):
    with nc.Block() as block:
        @block.gpsimd
        def _(pool):
            clear_spent(nc)


CH = 448
NCH = 2 * TIME // CH
CLS = 2 * TIME
COLS = 2 * SEQ
LN_EXP_SET = 6
N1, N2, N3 = 14, 14, 16
LANES = 2 * TIME // N1


def chunked(eng, step):
    for k in range(4):
        step(k, k % 2, k * CH, CH)
    with eng.Fori(2, NCH // 2) as i:
        for p in range(2):
            step(2 * i + p, p, (2 * i + p) * CH, CH)
    step(NCH, NCH % 2, CLS, 2)


def chunked_lagging(eng, step, behind):
    def both(k, p, at, n):
        step(k, p, at, n)
        if not (isinstance(k, int) and k == 0):
            behind(k - 1, 1 - p, (k - 1) * CH, CH)
    chunked(eng, both)
    behind(NCH, NCH % 2, CLS, 2)


def unroll_raster(nc, XT, H0, tail_w, ew1, ew2, tail_in, ew1_in, ew2_in):
    with nc.semaphore("tail_loaded") as tail_loaded, nc.Block() as block:
        def copy(engine, w):
            img = H0[:, w * TIME:(w + 1) * TIME].rearrange("p (y x) -> p y x", x=SIDE)
            for y, ny, fy in ((SHIFT, SIDE - SHIFT, SHIFT), (0, SHIFT, SIDE)):
                for x, nx, fx in ((SHIFT, SIDE - SHIFT, SHIFT), (0, SHIFT, SIDE)):
                    engine.tensor_copy(img[:, y:y + ny, x:x + nx], XT[:, w, fy:fy + ny, fx:fx + nx])

        @block.sync
        def _(sp):
            sp.dma_start(tail_w[:], tail_in).then_inc(tail_loaded, 16)
            sp.dma_start(ew1[:], ew1_in).then_inc(tail_loaded, 16)
            sp.dma_start(ew2[:], ew2_in).then_inc(tail_loaded, 16)
            sp.wait_ge(tail_loaded, 48)

        @block.vector
        def _(dve):
            copy(nc.vector, 0)
            dve.wait_ge(tail_loaded, 48)
            at = TAIL_AT["cls"][0]
            nc.vector.tensor_copy(H0[:, CLS:COLS], tail_w[:, at:at + 1].to_broadcast([P, 2]))

        @block.gpsimd
        def _(pool):
            clear_spent(nc)
            copy(nc.gpsimd, 1)


def channel_norm(nc, name, src, con, finish, n_finish, on_tensor=None, on_pool=None, out_dma=None, setup=None):
    with ExitStack() as ctx:
        sb = lambda nm, shape, dt=F32: ctx.enter_context(nc.sbuf_tensor(f"{name}_{nm}", shape, dt))
        pb = lambda nm, shape, dt=F32: ctx.enter_context(nc.psum_tensor(f"{name}_{nm}", shape, dt))
        sem = lambda nm: ctx.enter_context(nc.semaphore(f"{name}_{nm}"))
        centred = [sb(f"centred{i}", [P, CH]) for i in range(2)]
        square = [sb(f"square{i}", [P, CH]) for i in range(2)]
        lnv = sb("lnv", [P, CH])
        rstd = [sb(f"rstd{i}", [P, CH]) for i in range(2)]
        eps = sb("eps", [P, 1])
        ps_mean = [pb(f"ps_mean{i}", [P, 512]) for i in range(2)]
        ps_var = [pb(f"ps_var{i}", [P, 512]) for i in range(2)]
        ps_x = [pb(f"ps_x{i}", [P, 512]) for i in range(2)]
        eps_set = sem("eps_set")
        mean_ps = sem("mean_ps")
        centred_ready = sem("centred_ready")
        square_ready = sem("square_ready")
        var_ps = sem("var_ps")
        ln_ready = sem("ln_ready")
        rstd_ready = sem("rstd_ready")
        done = sem("done")
        extra_ps = sem("extra_ps")
        extra_done = sem("extra_done")
        inner = sem("inner")
        stored = [sem("stored0"), sem("stored1")]
        ones = con("mean_ones")
        with nc.Block() as block:
            @block.tensor
            def _(pe):
                def mean(k, p, at, n):
                    wait(pe, centred_ready, k - 1)
                    nc.tensor.matmul(ps_mean[p][:, 0:n], ones, src[:, ds(at, n)], start=True, stop=True).then_inc(mean_ps, 1)

                def variance(k, p, at, n):
                    pe.wait_ge(square_ready, k + 1)
                    wait(pe, ln_ready, k - 1)
                    nc.tensor.matmul(ps_var[p][:, 0:n], ones, square[p][:, 0:n], start=True, stop=True).then_inc(var_ps, 1)
                    if on_tensor is not None and not (isinstance(k, int) and k == 0):
                        on_tensor(pe, k - 1, 1 - p, (k - 1) * CH, CH, ps_x[1 - p], done, extra_ps, extra_done)

                chunked_lagging(pe, mean, variance)
                if on_tensor is not None:
                    on_tensor(pe, NCH, NCH % 2, CLS, 2, ps_x[NCH % 2], done, extra_ps, extra_done)

            @block.scalar
            def _(act):
                nc.scalar.add_instruction(mybir.InstLoadActFuncSet(name=nc.get_next_instruction_name(), engine=mybir.EngineType.Activation,
                                                                   act_func_set_id=LN_EXP_SET, ins=[], outs=[]))
                act.wait_ge(eps_set, 1)

                def squares(k, p, at, n):
                    act.wait_ge(centred_ready, k + 1)
                    wait(act, var_ps, k - 1)
                    nc.scalar.activation(square[p][:, 0:n], centred[p][:, 0:n], ACT.Square).then_inc(square_ready, 1)

                def inverse(k, p, at, n):
                    act.wait_ge(var_ps, k + 1)
                    wait(act, rstd_ready, k)
                    nc.scalar.activation(lnv[:, 0:n], ps_var[p][:, 0:n], ACT.Ln, bias=eps[:]).then_inc(ln_ready, 1)
                    act.wait_ge(ln_ready, k + 1)
                    wait(act, done, k - 1)
                    nc.scalar.activation(rstd[p][:, 0:n], lnv[:, 0:n], ACT.Exp, scale=-0.5).then_inc(rstd_ready, 1)

                chunked_lagging(act, squares, inverse)

            @block.vector
            def _(dve):
                nc.vector.memset(eps[:], EPS).then_inc(eps_set, 1)
                if setup is not None:
                    setup(dve)

                def centre(k, p, at, n):
                    dve.wait_ge(mean_ps, k + 1)
                    wait(dve, done, k - 1)
                    nc.vector.tensor_tensor(centred[p][:, 0:n], src[:, ds(at, n)], ps_mean[p][:, 0:n], ALU.subtract).then_inc(centred_ready, 1)

                def last(k, p, at, n):
                    dve.wait_ge(rstd_ready, k + 1)
                    finish(dve, k, p, at, n, centred[p], rstd[p], done, inner, ps_x, extra_ps, extra_done, stored)

                chunked_lagging(dve, centre, last)
                if n_finish is not None:
                    n_finish(dve, ps_x, done, extra_ps, extra_done)

            if on_pool is not None:
                @block.gpsimd
                def _(pool):
                    chunked(pool, lambda k, p, at, n: on_pool(pool, k, p, at, n, done))

            if out_dma is not None:
                @block.sync
                def _(sp):
                    chunked(sp, lambda k, p, at, n: out_dma(sp, k, p, at, n, done, stored))
                    for p in range(2):
                        sp.wait_ge(stored[p], 16 * ((NCH + 2 - p) // 2))


def recurrence(nc, F, Z, tw):
    with ExitStack() as ctx:
        sb = lambda nm, shape, dt=F32: ctx.enter_context(nc.sbuf_tensor(f"rec_{nm}", shape, dt))
        sem = lambda nm: ctx.enter_context(nc.semaphore(f"rec_{nm}"))
        NL, NS = LANES + 2, 2 * N3
        xs, z_start, ts = sb("xs", [P, NL]), sb("z_start", [P, NL]), sb("ts", [P, NL])
        fcls = sb("fcls", [P, 2])
        end_x, end_z = sb("end_x", [P, NS + 2, N2]), sb("end_z", [P, NS + 2, N2])
        vx, vz = sb("vx", [P, N2 + 1, NS + 2]), sb("vz", [P, N2 + 1, NS + 2])
        tx, tz = sb("tx", [P, NS + 2]), sb("tz", [P, NS + 2])
        wx, wz = sb("wx", [P, 2, N3]), sb("wz", [P, 2, N3])
        cx, cz = sb("cx", [P, LANES]), sb("cz", [P, LANES])
        made = sem("made")
        stt = nc.vector.scalar_tensor_tensor
        with nc.Block() as block:
            @block.vector
            def _(dve):
                count = [0]

                def link(ins):
                    count[0] += 1
                    ins.then_inc(made, 1)
                    dve.wait_ge(made, count[0])

                s, neg_dsa = tw("s"), tw("neg_dsa")
                link(nc.vector.tensor_copy(fcls[:], F[:, CLS:COLS]))
                nc.vector.memset(xs[:], 0.0)
                nc.vector.memset(z_start[:], 0.0)
                nc.vector.memset(end_x[:], 0.0)
                nc.vector.memset(end_z[:], 0.0)
                nc.vector.memset(vx[:, 0, :], 0.0)
                nc.vector.memset(vz[:, 0, :], 0.0)
                nc.vector.tensor_copy(wx[:, :, 0], fcls[:])
                nc.vector.tensor_scalar(wz[:, :, 0], fcls[:], DT, None, ALU.mult)
                link(nc.vector.memset(F[:, CLS:NL * N1], 0.0))
                nc.vector.memset(xs[:, LANES:LANES + 1], 1.0)
                nc.vector.memset(vx[:, 0, NS:NS + 1], 1.0)
                nc.vector.memset(vz[:, 0, NS + 1:NS + 2], 1.0)
                link(nc.vector.memset(z_start[:, LANES + 1:NL], 1.0))
                f_at = F[:, 0:NL * N1].rearrange("p (l n) -> p l n", n=N1)
                z_at = Z[:, 0:NL * N1].rearrange("p (l n) -> p l n", n=N1)
                halves = [slice(0, LANES // 2), slice(LANES // 2, NL)]

                def at(t, h, n):
                    return t[:, h, ds(n, 1)].rearrange("p l o -> p (l o)")

                base = count[0]

                def local(n):
                    before = lambda h: z_start[:, h] if isinstance(n, int) and n == 0 else at(z_at, h, n - 1)
                    done = base + 6 * n
                    for q, h in enumerate(halves):
                        wait(dve, made, done - 1 + q)
                        stt(ts[:, h], before(h), neg_dsa, at(f_at, h, n), ALU.mult, ALU.add).then_inc(made, 1)
                    for q, h in enumerate(halves):
                        dve.wait_ge(made, done + 1 + q)
                        stt(xs[:, h], xs[:, h], s, ts[:, h], ALU.mult, ALU.add).then_inc(made, 1)
                    for q, h in enumerate(halves):
                        dve.wait_ge(made, done + 3 + q)
                        stt(at(z_at, h, n), xs[:, h], DT, before(h), ALU.mult, ALU.add).then_inc(made, 1)

                local(0)
                local(1)
                with dve.Fori(0, (N1 - 2) // 4) as i:
                    for j in range(4):
                        local(4 * i + 2 + j)
                count[0] += 6 * N1
                dve.wait_ge(made, count[0])

                last = z_at[:, :, N1 - 1]
                a11, a12 = xs[:, LANES:LANES + 1], xs[:, LANES + 1:NL]
                a21, a22 = last[:, LANES:LANES + 1], last[:, LANES + 1:NL]
                nc.vector.tensor_copy(end_x[:, 0:NS, :].rearrange("p s c -> p (s c)"), xs[:, 0:LANES])
                link(nc.vector.tensor_copy(end_z[:, 0:NS, :].rearrange("p s c -> p (s c)"), last[:, 0:LANES]))

                base = count[0]
                with dve.Fori(0, 2) as i:
                    for j in range(N2 // 2):
                        k = (N2 // 2) * i + j
                        x, z = (v[:, ds(k, 1), :].rearrange("p o l -> p (o l)") for v in (vx, vz))
                        x1, z1 = (v[:, ds(k + 1, 1), :].rearrange("p o l -> p (o l)") for v in (vx, vz))
                        every = slice(0, NS + 2)
                        stt(tx[:], x, a11, at(end_x, every, k), ALU.mult, ALU.add).then_inc(made, 1)
                        stt(tz[:], x, a21, at(end_z, every, k), ALU.mult, ALU.add).then_inc(made, 1)
                        dve.wait_ge(made, base + 4 * k + 1)
                        stt(x1, z, a12, tx[:], ALU.mult, ALU.add).then_inc(made, 1)
                        dve.wait_ge(made, base + 4 * k + 2)
                        stt(z1, z, a22, tz[:], ALU.mult, ALU.add).then_inc(made, 1)
                        dve.wait_ge(made, base + 4 * k + 4)
                count[0] += 4 * N2

                b11, b12 = vx[:, N2, NS:NS + 1], vx[:, N2, NS + 1:NS + 2]
                b21, b22 = vz[:, N2, NS:NS + 1], vz[:, N2, NS + 1:NS + 2]
                span_x = vx[:, N2, 0:NS].rearrange("p (w c) -> p w c", w=2)
                span_z = vz[:, N2, 0:NS].rearrange("p (w c) -> p w c", w=2)
                both = slice(0, 2)
                base = count[0]
                with dve.Fori(0, 3) as i:
                    for j in range((N3 - 1) // 3):
                        k = (N3 - 1) // 3 * i + j
                        stt(tx[:, 0:2], at(wx, both, k), b11, at(span_x, both, k), ALU.mult, ALU.add).then_inc(made, 1)
                        stt(tz[:, 0:2], at(wx, both, k), b21, at(span_z, both, k), ALU.mult, ALU.add).then_inc(made, 1)
                        dve.wait_ge(made, base + 4 * k + 1)
                        stt(at(wx, both, k + 1), at(wz, both, k), b12, tx[:, 0:2], ALU.mult, ALU.add).then_inc(made, 1)
                        dve.wait_ge(made, base + 4 * k + 2)
                        stt(at(wz, both, k + 1), at(wz, both, k), b22, tz[:, 0:2], ALU.mult, ALU.add).then_inc(made, 1)
                        dve.wait_ge(made, base + 4 * k + 4)
                count[0] += 4 * (N3 - 1)

                start_x, start_z = wx[:].rearrange("p w c -> p (w c)"), wz[:].rearrange("p w c -> p (w c)")
                cx_at, cz_at = (t[:].rearrange("p (s c) -> p s c", c=N2) for t in (cx, cz))
                spans = slice(0, NS)
                for part, start in ((0, start_x), (1, start_z)):
                    base = count[0]
                    with dve.Fori(0, 2) as i:
                        for j in range(N2 // 2):
                            k = (N2 // 2) * i + j
                            for v, c_at in ((vx, cx_at), (vz, cz_at)):
                                coef = v[:, ds(k, 1), NS + part:NS + part + 1].rearrange("p o l -> p (o l)")
                                own = v[:, ds(k, 1), 0:NS].rearrange("p o l -> p (o l)") if part == 0 else at(c_at, spans, k)
                                stt(at(c_at, spans, k), start, coef, own, ALU.mult, ALU.add).then_inc(made, 1)
                    count[0] += 2 * N2
                    dve.wait_ge(made, count[0])

                real = slice(0, LANES)
                for part, start in ((0, cx), (1, cz)):
                    with dve.Fori(0, 2) as i:
                        for j in range(N1 // 2):
                            n = (N1 // 2) * i + j
                            coef = z_at[:, LANES + part:LANES + part + 1, ds(n, 1)].rearrange("p l o -> p (l o)")
                            stt(at(z_at, real, n), start[:], coef, at(z_at, real, n), ALU.mult, ALU.add).then_inc(made, 1)
                    count[0] += N1
                    dve.wait_ge(made, count[0])
                link(nc.vector.tensor_scalar(Z[:, CLS:COLS], fcls[:], DT, None, ALU.mult))


def mixer_gelu(nc, U_, Z, G, tw):
    with ExitStack() as ctx:
        pb = lambda nm, shape, dt=F32: ctx.enter_context(nc.psum_tensor(f"mix_{nm}", shape, dt))
        ps = [pb(f"ps{i}", [P, 512]) for i in range(4)]
        v_ps, g_ready = ctx.enter_context(nc.semaphore("mix_v_ps")), ctx.enter_context(nc.semaphore("mix_g_ready"))
        with nc.Block() as block:
            @block.tensor
            def _(pe):
                def step(k, p, at, n):
                    wait(pe, g_ready, k - 1)
                    nc.tensor.matmul(ps[p][:, 0:n], tw("CBD"), Z[:, ds(at, n)], start=True, stop=False)
                    nc.tensor.matmul(ps[p][:, 0:n], tw("DBD"), U_[:, ds(at, n)], start=False, stop=True).then_inc(v_ps, 1)
                chunked(pe, step)

            @block.scalar
            def _(act):
                def step(k, p, at, n):
                    act.wait_ge(v_ps, k + 1)
                    nc.scalar.activation(G[:, ds(at, n)], ps[p][:, 0:n], ACT.Gelu, bias=tw("bCD")).then_inc(g_ready, 1)
                chunked(act, step)


def mixer_gate(nc, G, HU, H1):
    with ExitStack() as ctx:
        sb = lambda nm, shape, dt=F32: ctx.enter_context(nc.sbuf_tensor(f"gate_{nm}", shape, dt))
        sem = lambda nm: ctx.enter_context(nc.semaphore(f"gate_{nm}"))
        sg = [sb(f"sg{i}", [P, CH]) for i in range(2)]
        pr = [sb(f"pr{i}", [P, CH]) for i in range(2)]
        sg_ready, product, added = sem("sg_ready"), sem("product"), sem("added")
        with nc.Block() as block:
            @block.scalar
            def _(act):
                def step(k, p, at, n):
                    wait(act, product, k - 1)
                    nc.scalar.activation(sg[p][:, 0:n], G[:, ds(at, n)], ACT.Sigmoid).then_inc(sg_ready, 1)
                chunked(act, step)

            @block.vector
            def _(dve):
                def multiply(k, p, at, n):
                    dve.wait_ge(sg_ready, k + 1)
                    wait(dve, added, k - 1)
                    nc.vector.tensor_tensor(pr[p][:, 0:n], G[:, ds(at, n)], sg[p][:, 0:n], ALU.mult).then_inc(product, 1)

                def add(k, p, at, n):
                    dve.wait_ge(product, k + 1)
                    nc.vector.tensor_tensor(H1[:, ds(at, n)], pr[p][:, 0:n], HU[:, ds(at, n)], ALU.add).then_inc(added, 1)
                chunked_lagging(dve, multiply, add)


def router(nc, X3, tw, ew1, ew2, w1_sel, w2_sel, b1_sel, b2_mix):
    with ExitStack() as ctx:
        sb = lambda nm, shape, dt=F32: ctx.enter_context(nc.sbuf_tensor(f"route_{nm}", shape, dt))
        sem = lambda nm: ctx.enter_context(nc.semaphore(f"route_{nm}"))
        E = N_EXP
        sums, wr = sb("sums", [P, 2]), sb("wr", [P, 2, E])
        r, r2 = sb("r", [P, 2, E]), sb("r2", [P, 2, E])
        m = sb("m", [P, 2])
        tot, inv = sb("tot", [P, 2]), sb("inv", [P, 2])
        load, scale = sb("load", [P, E]), sb("scale", [P, E])
        cand, hot = sb("cand", [P, 2, E]), sb("hot", [P, 2, 2, E])
        top, gates, gated = sb("top", [P, 2, 2]), sb("gates", [P, 2, 2]), sb("gated", [P, 2, 2, E])
        e2, den = sb("e2", [P, 2]), sb("den", [P, 2])
        spread = sb("spread", [P, 2, 2, 2, 2, E])
        prod1, prod2 = sb("prod1", [P, 8, E]), sb("prod2", [P, 2, 2 * E])
        both = sb("both", [P, 2, 2 * 2 * E])
        ps = ctx.enter_context(nc.psum_tensor("route_ps", [P, 512], F32))
        made, by_pe, by_act, by_pool = sem("made"), sem("by_pe"), sem("by_act"), sem("by_pool")
        spread_ready = sem("spread_ready")
        with nc.Block() as block:
            @block.tensor
            def _(pe):
                pe.wait_ge(made, 4)
                nc.tensor.matmul(ps[:, 0:2 * E], tw("group_ones"), wr[:].rearrange("p w e -> p (w e)"), start=True, stop=True).then_inc(by_pe, 1)
                pe.wait_ge(made, 10)
                nc.tensor.matmul(ps[:, 0:2 * E], tw("all_ones"), r[:].rearrange("p w e -> p (w e)"), start=True, stop=True).then_inc(by_pe, 1)
                pe.wait_ge(spread_ready, 1)
                for g in range(2):
                    last = nc.tensor.matmul(ps[:, g * 64:(g + 1) * 64], tw(f"pick{g}"), both[:].rearrange("p a b -> p (a b)"), start=True, stop=True)
                last.then_inc(by_pe, 1)

            @block.scalar
            def _(act):
                act.wait_ge(made, 7)
                nc.scalar.activation(r[:], r[:], ACT.Exp).then_inc(by_act, 1)
                act.wait_ge(made, 17)
                nc.scalar.activation(r2[:], r2[:], ACT.Exp).then_inc(by_act, 1)
                act.wait_ge(made, 32)
                nc.scalar.activation(e2[:], e2[:], ACT.Exp).then_inc(by_act, 1)

            @block.vector
            def _(dve):
                count = [0]

                def link(ins):
                    count[0] += 1
                    ins.then_inc(made, 1)
                    dve.wait_ge(made, count[0])

                wide = lambda t: t[:].unsqueeze(2).to_broadcast([P, 2, E])
                link(nc.vector.reduce_sum(sums[:], X3[:, 0:CLS].rearrange("p (w t) -> p w t", w=2), AX.X))
                link(nc.vector.tensor_tensor(sums[:], sums[:], X3[:, CLS:COLS], ALU.add))
                for w in range(2):
                    link(nc.vector.tensor_scalar(wr[:, w, :], tw("Wr"), sums[:, w:w + 1], 1.0 / SEQ, ALU.mult, ALU.mult))
                dve.wait_ge(by_pe, 1)
                link(nc.vector.tensor_tensor(r[:].rearrange("p w e -> p (w e)"), ps[:, 0:2 * E], tw("br_row"), ALU.add))

                def softmax(t, n_act):
                    link(nc.vector.reduce_max(m[:], t[:], AX.X))
                    link(nc.vector.tensor_tensor(t[:], t[:], wide(m), ALU.subtract))
                    dve.wait_ge(by_act, n_act)
                    link(nc.vector.reduce_sum(tot[:], t[:], AX.X))
                    link(nc.vector.reciprocal(inv[:], tot[:]))
                    link(nc.vector.tensor_tensor(t[:], t[:], wide(inv), ALU.mult))

                softmax(r, 1)
                dve.wait_ge(by_pe, 2)
                link(nc.vector.reduce_sum(load[:], ps[:, 0:2 * E].rearrange("p (w e) -> p e w", w=2), AX.X))
                link(nc.vector.tensor_scalar(load[:], load[:], 1.0 / C, float(SEQ), ALU.mult, ALU.mult))
                link(nc.vector.reciprocal(scale[:], load[:]))
                link(nc.vector.tensor_scalar(scale[:], scale[:], CAPACITY, 1.0, ALU.mult, ALU.min))
                link(nc.vector.tensor_tensor(r2[:], r[:], scale[:].unsqueeze(1).to_broadcast([P, 2, E]), ALU.mult))
                softmax(r2, 2)
                index = tw("index_row").unsqueeze(1).to_broadcast([P, 2, E])
                for c in range(2):
                    link(nc.vector.reduce_max(top[:, :, c], r2[:], AX.X))
                    link(nc.vector.tensor_tensor(cand[:], r2[:], top[:, :, c].unsqueeze(2).to_broadcast([P, 2, E]), ALU.is_equal))
                    link(nc.vector.tensor_tensor(cand[:], cand[:], index, ALU.mult))
                    link(nc.vector.reduce_max(m[:], cand[:], AX.X))
                    if c == 0:
                        link(nc.vector.tensor_tensor(hot[:, :, c, :], cand[:], wide(m), ALU.is_equal))
                        for w in range(2):
                            link(nc.vector.scalar_tensor_tensor(r2[:, w, :], hot[:, w, c, :], -2.0, r2[:, w, :], ALU.mult, ALU.add))
                    else:
                        link(nc.vector.tensor_tensor(e2[:], top[:, :, 1], top[:, :, 0], ALU.subtract))
                        hot_at = count[0]
                        link(nc.vector.tensor_tensor(hot[:, :, c, :], cand[:], wide(m), ALU.is_equal))
                assert count[0] == 33, count[0]
                dve.wait_ge(by_act, 3)
                link(nc.vector.tensor_scalar(den[:], e2[:], 1.0, None, ALU.add))
                link(nc.vector.reciprocal(gates[:, :, 0], den[:]))
                link(nc.vector.tensor_tensor(gates[:, :, 1], gates[:, :, 0], e2[:], ALU.mult))
                link(nc.vector.tensor_tensor(gated[:].rearrange("p w c e -> p (w c) e"), hot[:].rearrange("p w c e -> p (w c) e"),
                                             gates[:].rearrange("p w c -> p (w c)").unsqueeze(2).to_broadcast([P, 4, E]), ALU.mult))
                nc.vector.tensor_copy(both[:, 0, :], hot[:].rearrange("p w c e -> p (w c e)"))
                nc.vector.tensor_copy(both[:, 1, :], gated[:].rearrange("p w c e -> p (w c e)")).then_inc(spread_ready, 1)
                for w in range(2):
                    for c in range(2):
                        dst = w1_sel[:, (2 * w + c) * FF:(2 * w + c + 1) * FF]
                        link(nc.vector.tensor_scalar(dst, ew1[:, 0:FF], hot[:, w, c, 0:1], None, ALU.mult))
                        for e in range(1, E):
                            link(nc.vector.scalar_tensor_tensor(dst, ew1[:, e * FF:(e + 1) * FF], hot[:, w, c, e:e + 1], dst, ALU.mult, ALU.add))
                for w in range(2):
                    link(nc.vector.tensor_tensor(prod2[:, w, :].rearrange("p (c e) -> p c e", c=2), gated[:, w, :, :],
                                                 tw("b2T").unsqueeze(1).to_broadcast([P, 2, E]), ALU.mult))
                link(nc.vector.reduce_sum(b2_mix[:], prod2[:], AX.X))
                dve.wait_ge(by_pe, 3)
                link(nc.vector.tensor_copy(spread[:].rearrange("p g a w c e -> p (g a w c e)"), ps[:, 0:2 * 64]))
                for g in range(2):
                    link(nc.vector.tensor_tensor(prod1[:, 4 * g:4 * g + 4, :], spread[:, g, 0, :, :, :].rearrange("p w c e -> p (w c) e"),
                                                 tw("b1T").unsqueeze(1).to_broadcast([P, 4, E]), ALU.mult))
                link(nc.vector.reduce_sum(b1_sel[:], prod1[:], AX.X))
                for g in range(2):
                    for w in range(2):
                        for c in range(2):
                            i = 4 * g + 2 * w + c
                            dst = w2_sel[:, i * C:(i + 1) * C]
                            link(nc.vector.tensor_scalar(dst, ew2[:, 0:C], spread[:, g, 1, w, c, 0:1], None, ALU.mult))
                            for e in range(1, E):
                                link(nc.vector.scalar_tensor_tensor(dst, ew2[:, e * C:(e + 1) * C], spread[:, g, 1, w, c, e:e + 1], dst, ALU.mult, ALU.add))


def experts(nc, X3, Y, w1_sel, w2_sel, b1_sel, b2_mix):
    with ExitStack() as ctx:
        sb = lambda nm, shape, dt=F32: ctx.enter_context(nc.sbuf_tensor(f"ex_{nm}", shape, dt))
        pb = lambda nm, shape, dt=F32: ctx.enter_context(nc.psum_tensor(f"ex_{nm}", shape, dt))
        sem = lambda nm: ctx.enter_context(nc.semaphore(f"ex_{nm}"))
        xin = [sb(f"xin{i}", [P, CH]) for i in range(2)]
        hid = [[sb(f"hid{i}_{j}", [P, CH]) for j in range(4)] for i in range(2)]
        ps_h = [pb(f"ps_h{j}", [P, 512]) for j in range(4)]
        ps_y = [pb(f"ps_y{i}", [P, 512]) for i in range(2)]
        x_in = sem("x_in")
        h_ps = sem("h_ps")
        h_ready = sem("h_ready")
        y_ps = sem("y_ps")
        y_ready = sem("y_ready")
        PER = NCH // 2
        assert PER % 2 == 1

        def pairs(eng, w, body):
            first = w * PER + 1
            if w == 0:
                for k in (1, 2):
                    body(k, k % 2, k * CH)
            with eng.Fori(1 - w, PER // 2) as i:
                for q in range(2):
                    k = 2 * i + first + q
                    body(k, (first + q) % 2, k * CH)

        def order(eng, step):
            for w in range(2):
                step(w * PER, w, w * PER % 2, w * PER * CH, CH)
                pairs(eng, w, lambda k, p, at: step(k, w, p, at, CH))
            for w in range(2):
                step(NCH + w, w, (NCH + w) % 2, CLS + w, 1)

        def lagging(eng, step, behind):
            for w in range(2):
                first = w * PER
                step(first, w, first % 2, first * CH, CH)
                if w:
                    behind(first - 1, 0, (first - 1) % 2, (first - 1) * CH, CH)

                def both(k, p, at):
                    step(k, w, p, at, CH)
                    behind(k - 1, w, 1 - p, (k - 1) * CH, CH)
                pairs(eng, w, both)
            step(NCH, 0, NCH % 2, CLS, 1)
            behind(NCH - 1, 1, (NCH - 1) % 2, (NCH - 1) * CH, CH)
            step(NCH + 1, 1, (NCH + 1) % 2, CLS + 1, 1)
            behind(NCH, 0, NCH % 2, CLS, 1)
            behind(NCH + 1, 1, (NCH + 1) % 2, CLS + 1, 1)

        with nc.Block() as block:
            @block.gpsimd
            def _(pool):
                def step(k, w, p, at, n):
                    wait(pool, h_ps, 4 * k - 4)
                    nc.gpsimd.tensor_copy(xin[p][:, 0:n], X3[:, ds(at, n)]).then_inc(x_in, 1)
                order(pool, step)

            @block.tensor
            def _(pe):
                def up(k, w, p, at, n):
                    pe.wait_ge(x_in, k + 1)
                    for c in range(2):
                        for g in range(2):
                            j, r = 2 * c + g, slice(C * g, C * g + C)
                            wait(pe, h_ready, 4 * k - 4 + j + 1)
                            nc.tensor.matmul(ps_h[j][:, 0:n], w1_sel[r, (2 * w + c) * FF:(2 * w + c + 1) * FF], xin[p][r, 0:n],
                                             start=True, stop=True).then_inc(h_ps, 1)

                def down(k, w, p, at, n):
                    wait(pe, y_ready, k - 1)
                    for c in range(2):
                        for g in range(2):
                            j, i = 2 * c + g, 4 * g + 2 * w + c
                            pe.wait_ge(h_ready, 4 * k + j + 1)
                            last = nc.tensor.matmul(ps_y[p][C * g:C * g + C, 0:n], w2_sel[:, i * C:(i + 1) * C], hid[p][j][:, 0:n],
                                                    start=(c == 0), stop=(c == 1), skip_group_check=True)
                    last.then_inc(y_ps, 1)
                lagging(pe, up, down)

            @block.scalar
            def _(act):
                def step(k, w, p, at, n):
                    wait(act, y_ps, k - 1)
                    for j in range(4):
                        c, g = j // 2, j % 2
                        act.wait_ge(h_ps, 4 * k + j + 1)
                        i = 4 * g + 2 * w + c
                        nc.scalar.activation(hid[p][j][:, 0:n], ps_h[j][:, 0:n], ACT.Gelu, bias=b1_sel[:, i:i + 1]).then_inc(h_ready, 1)
                order(act, step)

            @block.vector
            def _(dve):
                def step(k, w, p, at, n):
                    dve.wait_ge(y_ps, k + 1)
                    nc.vector.scalar_tensor_tensor(Y[:, ds(at, n)], ps_y[p][:, 0:n], b2_mix[:, w:w + 1], X3[:, ds(at, n)],
                                                   ALU.add, ALU.add).then_inc(y_ready, 1)
                order(dve, step)


def tail(nc, ctx, X, X2, XT, con, tail_in, ew1_in, ew2_in, out, debug):
    sb = lambda name, shape, dt=F32: ctx.enter_context(nc.sbuf_tensor(name, shape, dt))
    u_cols = X[:].rearrange("p t r -> p (t r)")
    f_cols = X2[:].rearrange("p t r -> p (t r)")
    H0 = sb("H0", [P, COLS])
    Z = sb("Z", [P, (LANES + 2) * N1])
    tail_w = sb("tail_w", [P, TAIL_W])
    ew1 = sb("ew1", [P, N_EXP * FF])
    ew2 = sb("ew2", [FF, N_EXP * C])
    w1_sel = sb("w1_sel", [P, 4 * FF])
    w2_sel = sb("w2_sel", [P, 8 * C])
    b1_sel = sb("b1_sel", [P, 8])
    b2_mix = sb("b2_mix", [P, 2])
    derived = sb("derived", [P, 6])
    extra = {"s": 0, "neg_dsa": 1, "ds": 2, "bCD": 3, "tmp": 4, "f_bias": 5}

    def tw(name):
        if name in extra:
            return derived[:, extra[name]:extra[name] + 1]
        at, n = TAIL_AT[name]
        return tail_w[:, at:at + n]

    unroll_raster(nc, XT, H0, tail_w, ew1, ew2, tail_in, ew1_in, ew2_in)

    with nc.semaphore("coef") as coef:
        def coefficients(dve):
            count = [0]

            def link(ins):
                count[0] += 1
                ins.then_inc(coef, 1)
                dve.wait_ge(coef, count[0])

            link(nc.vector.tensor_scalar(tw("tmp"), tw("a"), DT * DT, 1.0, ALU.mult, ALU.add))
            link(nc.vector.reciprocal(tw("s"), tw("tmp")))
            link(nc.vector.tensor_scalar(tw("ds"), tw("s"), DT, None, ALU.mult))
            link(nc.vector.scalar_tensor_tensor(tw("neg_dsa"), tw("ds"), -1.0, tw("a"), ALU.mult, ALU.mult))
            link(nc.vector.tensor_tensor(tw("bCD"), tw("bC"), tw("bD"), ALU.add))

        def b_product(pe, k, p, at, n, ps, done, extra_ps, extra_done):
            pe.wait_ge(done, k + 1)
            wait(pe, extra_done, k - 1)
            nc.tensor.matmul(ps[:, 0:n], tw("BBD"), u_cols[:, ds(at, n)], start=True, stop=True).then_inc(extra_ps, 1)

        def forcing(dve, k, p, at, n, ps_x, extra_ps, extra_done):
            dve.wait_ge(extra_ps, k + 1)
            nc.vector.tensor_scalar(f_cols[:, ds(at, n)], ps_x[p][:, 0:n], tw("bB"), tw("ds"), ALU.add, ALU.mult).then_inc(extra_done, 1)

        def mixer_in(dve, k, p, at, n, centred, rstd, done, inner, ps_x, extra_ps, extra_done, stored):
            nc.vector.tensor_tensor(u_cols[:, ds(at, n)], centred[:, 0:n], rstd[:, 0:n], ALU.mult).then_inc(done, 1)
            if isinstance(k, int) and k == 0:
                return
            forcing(dve, k - 1, 1 - p, (k - 1) * CH, CH, ps_x, extra_ps, extra_done)

        def last_forcing(dve, ps_x, done, extra_ps, extra_done):
            forcing(dve, NCH, NCH % 2, CLS, 2, ps_x, extra_ps, extra_done)

        def add_u(pool, k, p, at, n, done):
            pool.wait_ge(done, k + 1)
            nc.gpsimd.tensor_tensor(H0[:, ds(at, n)], H0[:, ds(at, n)], u_cols[:, ds(at, n)], ALU.add)

        channel_norm(nc, "cn0", H0, con, mixer_in, last_forcing, on_tensor=b_product, on_pool=add_u, setup=coefficients)
    recurrence(nc, f_cols, Z, tw)
    G = f_cols
    mixer_gelu(nc, u_cols, Z, G, tw)
    H1 = Z
    mixer_gate(nc, G, H0, H1)
    if debug == "h1":
        return dump(nc, H1, out)
    X3 = u_cols

    def ffn_in(dve, k, p, at, n, centred, rstd, done, inner, ps_x, extra_ps, extra_done, stored):
        nc.vector.tensor_tensor(X3[:, ds(at, n)], centred[:, 0:n], rstd[:, 0:n], ALU.mult).then_inc(done, 1)

    channel_norm(nc, "cn1", H1, con, ffn_in, None)
    router(nc, X3, tw, ew1, ew2, w1_sel, w2_sel, b1_sel, b2_mix)
    Y = f_cols
    experts(nc, X3, Y, w1_sel, w2_sel, b1_sel, b2_mix)
    res = [sb(f"res{i}", [P, CH]) for i in range(2)]
    scaled = [sb(f"scaled{i}", [P, CH]) for i in range(2)]

    def final(dve, k, p, at, n, centred, rstd, done, inner, ps_x, extra_ps, extra_done, stored):
        nc.vector.scalar_tensor_tensor(scaled[p][:, 0:n], centred[:, 0:n], tw("gamma"), rstd[:, 0:n], ALU.mult, ALU.mult).then_inc(inner, 1)
        dve.wait_ge(inner, k + 1)
        wait(dve, stored[p], 8 * k - 8 * p)
        nc.vector.scalar_tensor_tensor(res[p][:, 0:n], scaled[p][:, 0:n], tw("beta"), H1[:, ds(at, n)], ALU.add, ALU.add).then_inc(done, 1)

    def store(sp, k, p, at, n, done, stored):
        sp.wait_ge(done, k + 1)
        sp.dma_start(out[:, ds(at, n)], res[p][:, 0:n]).then_inc(stored[p], 16)

    channel_norm(nc, "cn2", Y, con, final, None, out_dma=store)


def _dup(a):
    return np.concatenate([a, a], axis=0)


def _col(v):
    return _dup(v.reshape(-1, 1))


def _blockdiag(a):
    z = np.zeros((2 * C, 2 * C), np.float32)
    z[:C, :C] = a
    z[C:, C:] = a
    return z


def _rows(v, n=P):
    return np.broadcast_to(v.reshape(1, -1), (n, v.size))


def _pack(order, parts):
    return np.ascontiguousarray(np.concatenate([parts[n] for n, _ in order], axis=1), dtype=np.float32)


def kernel(_debug=None, **inputs):
    import concourse.bacc as _bacc
    from concourse.bass_utils import run_bass_kernel_spmd as _run

    a = {k: np.asarray(v) for k, v in inputs.items()}
    x = a["x"].reshape(2, 2, NW, WS, 4, NW, WS, 4)
    x = x.transpose(4, 7, 2, 5, 0, 1, 3, 6).reshape(PATCH, U, 2, 2, TOK)
    pat = np.zeros((PATCH + 1, U, 2, 2, C), np.float32)
    pat[:PATCH, ..., :TOK] = x
    pat[PATCH, ..., :TOK] = 1.0
    pat = np.ascontiguousarray(pat.reshape(PATCH + 1, TILES // 8, 8 * P).transpose(1, 0, 2))
    patch_w = np.concatenate([a["L0_tok_pe_w"].reshape(C, PATCH).T, a["L0_tok_pe_b"].reshape(1, C)], axis=0)

    p = np.arange(P)
    same_half = (p[:, None] // C == p[None, :] // C)
    common = _pack(COMMON_COLS, {
        "ident": np.eye(P, dtype=np.float32),
        "mean_ones": same_half.astype(np.float32) / C,
        "head_mask": ((p[:, None] % C) // HD == np.arange(NH)[None, :]).astype(np.float32),
        "pg_row": _rows(a["L0_tok_pe_ng"]), "pbeta_row": _rows(a["L0_tok_pe_nb"])})
    blocks, biases = [], []
    coords = np.stack(np.meshgrid(np.arange(WS), np.arange(WS), indexing="ij")).reshape(2, -1)
    rel = coords[:, :, None] - coords[:, None, :] + WS - 1
    rpi = rel[0] * (2 * WS - 1) + rel[1]
    for b in range(2):
        w = a["L0_tok_qkv_w"][b]
        qb = a["L0_tok_qkv_b"][b]
        w1T = a["L0_tok_w1"][b].T
        w2 = a["L0_tok_w2"][b].T.reshape(2, P, C).transpose(1, 0, 2).reshape(P, 2 * C)
        blocks.append(_pack(BLOCK_COLS, {
            "qBD": _blockdiag(w[:C].T), "kBD": _blockdiag(w[C:2 * C].T), "vBD": _blockdiag(w[2 * C:].T),
            "pBD": _blockdiag(a["L0_tok_proj_w"][b].T), "w2T": w2,
            "w1T0": np.concatenate([w1T, np.zeros_like(w1T)]), "w1T1": np.concatenate([np.zeros_like(w1T), w1T]),
            "n1g": _col(a["L0_tok_n1g"][b]), "n1b": _col(a["L0_tok_n1b"][b]),
            "qb": _col(qb[:C]), "kb": _col(qb[C:2 * C]), "vb": _col(qb[2 * C:]),
            "n2g": _col(a["L0_tok_n2g"][b]), "n2b": _col(a["L0_tok_n2b"][b]),
            "b1": a["L0_tok_b1"][b].reshape(2, P).T,
            "pb_row": _rows(a["L0_tok_proj_b"][b]), "b2": _col(a["L0_tok_b2"][b])}))
        t = a["L0_tok_rpb"][b][rpi].transpose(0, 2, 1).reshape(TOK, NH * TOK)
        z = np.zeros((2, C, NH * TOK), np.float32)
        z[:, :TOK] = t
        biases.append(z.reshape(P, NH * TOK))
    part = np.arange(WS) >= WS - SHIFT
    row_part, col_part = np.repeat(part, WS), np.tile(part, WS)
    masks = np.zeros((2, C, 4, TOK), np.float32)
    for v in range(4):
        label = row_part * (v >> 1) * 2 + col_part * (v & 1)
        masks[:, :TOK, v] = np.where(label[:, None] != label[None, :], -100.0, 0.0)
    masks = masks.reshape(P, 4, TOK)
    pick = np.zeros((2, P, P), np.float32)
    pick[0, 0, :] = 1.0
    pick[1, C, :] = 1.0
    tail_w = _pack(TAIL_COLS, {
        "BBD": _blockdiag(a["L0_attn_W_B"].T), "CBD": _blockdiag(a["L0_attn_W_C"].T), "DBD": _blockdiag(a["L0_attn_W_D"].T),
        "a": _col(a["L0_attn_a"]), "bB": _col(a["L0_attn_b_B"]), "bC": _col(a["L0_attn_b_C"]), "bD": _col(a["L0_attn_b_D"]),
        "cls": _col(a["cls_tok"].reshape(C)), "Wr": _dup(a["L0_ffn_Wr"]),
        "br_row": np.concatenate([_rows(a["L0_ffn_br"])] * 2, axis=1),
        "gamma": _col(a["L0_ffn_gamma"]), "beta": _col(a["L0_ffn_beta"]), "b2T": _dup(a["L0_ffn_b2"].T), "b1T": a["L0_ffn_b1"].T,
        "group_ones": same_half.astype(np.float32), "all_ones": np.ones((P, P), np.float32),
        "pick0": pick[0], "pick1": pick[1],
        "index_row": _rows(np.arange(N_EXP, 0, -1).astype(np.float32))})
    ew1 = _dup(a["L0_ffn_W1"].transpose(1, 0, 2).reshape(C, N_EXP * FF))
    ew2 = np.ascontiguousarray(a["L0_ffn_W2"].transpose(1, 0, 2).reshape(FF, N_EXP * C))

    nc = _bacc.Bacc("TRN2", target_bir_lowering=False, num_devices=1)
    arrays, args = {}, []
    for name, v in (("patches", pat), ("patch_w", patch_w), ("common", common), ("blocks", np.stack(blocks)),
                    ("biases", np.stack(biases)), ("masks", masks), ("tail_w", tail_w), ("ew1", ew1), ("ew2", ew2)):
        v = np.ascontiguousarray(v)
        arrays[f"in_{name}"] = v
        args.append(nc.dram_tensor(f"in_{name}", v.shape, mybir.dt.from_np(v.dtype), kind="ExternalInput").ap())
    shape = {None: (P, 2 * SEQ), "m0": (P, TILES, ROW), "a1": (P, TILES, ROW), "m1": (P, 2, PAD, PAD), "h1": (P, COLS)}[_debug]
    out = nc.dram_tensor("out", shape, F32, kind="ExternalOutput").ap()
    build(nc, *args, out, debug=_debug)
    r = _run(nc, [arrays], core_ids=[0])
    got = r.results[0]["out"]
    got = got.reshape(2, C, 2 * SEQ)
    image = got[:, :, :2 * TIME].reshape(2, C, 2, TIME).transpose(0, 2, 3, 1).reshape(4, TIME, C)
    first = got[:, :, 2 * TIME:].transpose(0, 2, 1).reshape(4, 1, C)
    return np.ascontiguousarray(np.concatenate([first, image], axis=1))
```

```python
from contextlib import ExitStack

import numpy as np

import concourse.bass as bass
from concourse import mybir

F32 = mybir.dt.float32
BF16 = mybir.dt.bfloat16
ALU = mybir.AluOpType
ACT = mybir.ActivationFunctionType
AX = mybir.AxisListType
ds = bass.ds

P = 128
C = 64
NH, HD = 8, 8
WS, SHIFT = 7, 3
TOK = WS * WS
NW = 8
SIDE = WS * NW
U = NW * NW
TILES = 2 * U
HID = 4 * C
EPS = 1e-5
SCALE = HD ** -0.5
PATCH = 16
NMR, RSTD = C, C + 1
ROW = C + 2
N_EXP, FF = 8, 128
TIME = SIDE * SIDE
SEQ = TIME + 1
CAPACITY = float(-(-4 * SEQ * 5 // (4 * N_EXP)))
DT = 1.0 / SEQ

BLOCK_COLS = [("qBD", P), ("kBD", P), ("vBD", P), ("pBD", P), ("w1T0", HID), ("w1T1", HID), ("w2T", 2 * C),
              ("n1g", 1), ("n1b", 1), ("qb", 1), ("kb", 1), ("vb", 1), ("n2g", 1), ("n2b", 1), ("b1", 2),
              ("b2", 1), ("pb_row", C)]
COMMON_COLS = [("ident", P), ("mean_ones", P), ("head_mask", NH), ("pg_row", C), ("pbeta_row", C)]
TAIL_COLS = [("BBD", P), ("CBD", P), ("DBD", P), ("a", 1), ("bB", 1), ("bC", 1), ("bD", 1), ("cls", 1),
             ("Wr", N_EXP), ("br_row", 2 * N_EXP), ("gamma", 1), ("beta", 1), ("b2T", N_EXP), ("b1T", N_EXP),
             ("group_ones", P), ("all_ones", P), ("pick0", P), ("pick1", P), ("index_row", N_EXP)]


def columns(cols):
    at, out = 0, {}
    for name, n in cols:
        out[name] = (at, n)
        at += n
    return out, at


BLOCK_AT, BLOCK_W = columns(BLOCK_COLS)
COMMON_AT, COMMON_W = columns(COMMON_COLS)
TAIL_AT, TAIL_W = columns(TAIL_COLS)


def live(u, n=U):
    return not isinstance(u, int) or 0 <= u < n


def wait(eng, sem, value):
    if isinstance(value, int) and value <= 0:
        return
    eng.wait_ge(sem, value)


def skewed(eng, step, first, last):
    for s in range(first, NW):
        step(s, s % NW)
    with eng.Fori(1, NW - 1) as row:
        for c in range(NW):
            step(row * NW + c, c)
    for s in range(NW * (NW - 1), last + 1):
        step(s, s % NW)


def build(nc, patches, patch_w, common_in, block_in, bias_in, mask_in, tail_in, ew1_in, ew2_in, out, debug=None):
    ctx = ExitStack()
    with ctx:
        def sb(name, shape, dt=F32):
            return ctx.enter_context(nc.sbuf_tensor(name, shape, dt))

        X = sb("X", [P, TILES, ROW])
        X2 = sb("X2", [P, TILES, ROW])
        H0 = sb("H0", [P, COLS])
        common = sb("common", [P, COMMON_W])
        block_w = [sb(f"block_w{b}", [P, BLOCK_W]) for b in range(2)]

        def con(name):
            at, n = COMMON_AT[name]
            return common[:, at:at + n]

        def wt(b, name):
            at, n = BLOCK_AT[name]
            return block_w[b][:, at:at + n]

        tables = [BiasTables(nc, ctx, b) for b in range(2)]
        padded = Padded(nc, ctx)
        load_and_embed(nc, X, X2, common, block_w, con, tables[0], padded, patches, patch_w, common_in, block_in, bias_in, mask_in)
        attention(nc, 0, X, con, wt, tables[0], padded, None)
        mlp(nc, 0, X, con, wt, None, Roll(nc, X, X2), tables[1], bias_in, mask_in)
        if debug == "m0":
            return dump(nc, X, out)
        recycle(nc)
        with nc.semaphore("rolled") as rolled:
            attention(nc, 1, X2, con, wt, tables[1], padded, (Roll(nc, X, X2), rolled))
        if debug == "a1":
            return dump(nc, X2, out)
        tail_w, ew1, ew2 = sb("tail_w", [P, TAIL_W]), sb("ew1", [P, N_EXP * FF]), sb("ew2", [FF, N_EXP * C])
        mlp(nc, 1, X2, con, wt, H0, None, None, bias_in, mask_in, ((tail_w, tail_in), (ew1, ew1_in), (ew2, ew2_in)))
        tail(nc, ctx, X, X2, H0, con, tail_w, ew1, ew2, out, debug)


def clear_spent(nc):
    spent = sorted(nc.released_uncleared_semaphores)
    while spent:
        first = last = spent.pop(0)
        while spent and spent[0] == last + 1:
            last = spent.pop(0)
        nc.gpsimd.sem_clear(range(first, last + 1))


def dump(nc, T, out):
    with nc.semaphore("dumped") as s, nc.Block() as block:
        @block.sync
        def _(sp):
            sp.dma_start(out, T[:]).then_inc(s, 16)
            sp.wait_ge(s, 16)


def paired(eng, step, first, last, loop_from, loop_to, per=2):
    assert (loop_to + 1 - loop_from) % per == 0
    for k in range(first, loop_from):
        step(k, k % per, k // per)
    turns, past = divmod(loop_from, per)
    with eng.Fori(turns, (loop_to + 1) // per) as i:
        for p in range(past, past + per):
            step(per * i + p, p % per, i + p // per)
    for k in range(loop_to + 1, last + 1):
        step(k, k % per, k // per)


def at_most(value, n):
    return min(value, n) if isinstance(value, int) else value


class BiasTables:

    def __init__(self, nc, ctx, b):
        self.nc, self.b = nc, b
        self.NV = 4 if b else 1
        sb = lambda name, shape: ctx.enter_context(nc.sbuf_tensor(f"bias{b}_{name}", shape, BF16))
        self.hi_mid = sb("hi_mid", [P, NH * TOK])
        self.lo = sb("lo", [P, self.NV, NH * TOK])
        self.table = ctx.enter_context(nc.sbuf_tensor(f"bias{b}_table", [P, self.NV, NH * TOK], F32))

    def scratch(self, ctx):
        sb = lambda name, shape, dt=F32: ctx.enter_context(self.nc.sbuf_tensor(f"bias{self.b}_{name}", shape, dt))
        self.raw, self.mask = self.table[:, 0, :], sb("mask", [P, 4, TOK])
        self.rest, self.rest2 = (sb(name, [P, NH * TOK]) for name in ("rest", "rest2"))
        self.hi_all, self.mid_all = (sb(name, [P, NH * TOK], BF16) for name in ("hi_all", "mid_all"))
        self.loaded = ctx.enter_context(self.nc.semaphore(f"bias{self.b}_loaded"))
        self.made = ctx.enter_context(self.nc.semaphore(f"bias{self.b}_made"))

    def load(self, sp, bias_in, mask_in):
        sp.dma_start(self.raw, bias_in[self.b]).then_inc(self.loaded, 16)
        sp.dma_start(self.mask[:], mask_in).then_inc(self.loaded, 16)

    def make(self, eng, api):
        count = [0]

        def link(ins):
            count[0] += 1
            ins.then_inc(self.made, 1)
            eng.wait_ge(self.made, count[0])

        eng.wait_ge(self.loaded, 32)
        link(api.tensor_copy(self.hi_all[:], self.raw))
        link(api.tensor_tensor(self.rest[:], self.raw, self.hi_all[:], ALU.subtract))
        link(api.tensor_copy(self.mid_all[:], self.rest[:]))
        link(api.tensor_tensor(self.rest2[:], self.rest[:], self.mid_all[:], ALU.subtract))
        api.tensor_copy(self.hi_mid[0:C, :], self.hi_all[0:C, :])
        link(api.tensor_copy(self.hi_mid[C:P, :], self.mid_all[C:P, :]))
        for v in range(self.NV):
            api.tensor_copy(self.lo[0:C, v, :], self.rest2[0:C, :])
            if v:
                heads = lambda x: self.table[:, x, :].rearrange("p (h k) -> p h k", h=NH)
                link(api.tensor_tensor(heads(v), heads(0), self.mask[:, v, :].unsqueeze(1).to_broadcast([P, NH, TOK]), ALU.add))
            link(api.tensor_copy(self.lo[C:P, v, :].rearrange("p (h k) -> p h k", h=NH),
                                 self.mask[C:P, v, :].unsqueeze(1).to_broadcast([C, NH, TOK])))


class Padded:

    def __init__(self, nc, ctx):
        self.nc = nc
        sb = lambda name, shape: ctx.enter_context(nc.sbuf_tensor(name, shape, F32))
        self.q_bd = [sb(f"q_bd{i}", [P, 2, 2, C]) for i in range(2)]
        self.v_bd = [sb(f"v_bd{i}", [P, 2, 2, NH // 2, 2, HD + 1]) for i in range(2)]
        self.prob = [sb(f"prob{w}", [P, NH, C]) for w in range(2)]

    def clear(self, dve, zeroed):
        for i in range(2):
            self.nc.vector.memset(self.q_bd[i][:], 0.0)
            self.nc.vector.memset(self.prob[i][:], 0.0)
            self.nc.vector.memset(self.v_bd[i][:], 0.0).then_inc(zeroed, 1)
        dve.wait_ge(zeroed, 2)
        for i in range(2):
            for h in range(2):
                self.nc.vector.memset(self.v_bd[i][C * h:C * h + C, :, :, :, h, HD:HD + 1], 1.0)


class NormScalars:

    def __init__(self, nc, ctx, prefix, X, n):
        sb = lambda name, shape, dt=F32: ctx.enter_context(nc.sbuf_tensor(prefix + name, shape, dt))
        sem = lambda name: ctx.enter_context(nc.semaphore(prefix + name))
        self.nc, self.X, self.n = nc, X, n
        self.st = [sb(f"st{i}", [P, n, 6]) for i in range(2)]
        self.mv = [sb(f"mv{i}", [P, n, 2]) for i in range(2)]
        self.ve = sb("ve", [P, n])
        self.rs = [sb(f"rs{i}", [P, n]) for i in range(2)]
        self.eps, self.half = sb("eps", [P, n]), sb("half", [P, n])
        self.stats = sem("stats")
        self.aggr = sem("aggr")
        self.ve_set = sem("ve_set")
        self.rs_ready = sem("rs_ready")
        self.kept = sem("kept")
        self.set_up = sem("set_up")

    def prepare(self, pool):
        self.nc.gpsimd.memset(self.eps[:], EPS).then_inc(self.set_up, 1)
        self.nc.gpsimd.memset(self.half[:], -0.5).then_inc(self.set_up, 1)
        pool.wait_ge(self.set_up, 2)

    def statistics(self, k, p):
        for t in range(self.n):
            last = self.nc.vector.bn_stats(self.st[p][:, t, :], self.X[:, ds(k * self.n + t, 1), 0:C].rearrange("p o c -> p (o c)"))
        last.then_inc(self.stats, 1)

    def aggregate(self, k, p):
        for t in range(self.n):
            last = self.nc.vector.bn_aggr(self.mv[p][:, t, :], self.st[p][:, t, :])
        last.then_inc(self.aggr, 1)

    def invert(self, pool, k, p):
        var = self.mv[p][:, :, 1]
        wait(pool, self.rs_ready, k)
        pool.wait_ge(self.aggr, k + 1)
        self.nc.gpsimd.tensor_tensor(self.ve[:], var, self.eps[:], ALU.add).then_inc(self.ve_set, 1)
        wait(pool, self.kept, 2 * (k - 1))
        pool.wait_ge(self.ve_set, k + 1)
        self.nc.gpsimd.tensor_tensor(self.rs[p][:], self.ve[:], self.half[:], ALU.pow).then_inc(self.rs_ready, 1)

    def keep(self, dve, k, p):
        tiles = ds(k * self.n, self.n)
        dve.wait_ge(self.rs_ready, k + 1)
        rs, mean = self.rs[p][:].unsqueeze(2), self.mv[p][:, :, 0:1]
        self.nc.vector.tensor_scalar(self.X[:, tiles, RSTD:ROW], rs, 1.0, None, ALU.mult).then_inc(self.kept, 1)
        self.nc.vector.scalar_tensor_tensor(self.X[:, tiles, NMR:RSTD], mean, -1.0, rs, ALU.mult, ALU.mult).then_inc(self.kept, 1)


def load_and_embed(nc, X, X2, common, block_w, con, tables, padded, patches, patch_w, common_in, block_in, bias_in, mask_in):
    with ExitStack() as ctx:
        sb = lambda name, shape, dt=F32: ctx.enter_context(nc.sbuf_tensor(name, shape, dt))
        pb = lambda name, shape, dt=F32: ctx.enter_context(nc.psum_tensor(name, shape, dt))
        sem = lambda name: ctx.enter_context(nc.semaphore(name))
        GT = 8
        K = TILES // GT
        pw = sb("pw", [PATCH + 1, C])
        pw_mean = sb("pw_mean", [PATCH + 1, 1])
        pw_c = sb("pw_c", [PATCH + 1, C])
        DEEP = 4
        ring = [sb(f"patch_ring{i}", [PATCH + 1, GT * P]) for i in range(DEEP)]
        sq = [sb(f"sq{i}", [P, C]) for i in range(2)]
        var = [sb(f"pvar{i}", [P, GT]) for i in range(DEEP)]
        ve = sb("pve", [P, GT])
        rs = [sb(f"prs{i}", [P, GT]) for i in range(2)]
        gained = [sb(f"gained{i}", [P, GT, C]) for i in range(2)]
        ps = [pb(f"pe_ps{i}", [P, 512]) for i in range(DEEP)]

        weights_in = sem("weights_in")
        pw_in = sem("pw_in")
        patch_in = [sem(f"patch_in{i}") for i in range(DEEP)]
        cleared = sem("cleared")
        padding = sem("padding")
        pw_m = sem("pw_m")
        pw_ready = sem("pw_ready")
        embedded = sem("embedded")
        squared = sem("squared")
        ve_ready = sem("ve_ready")
        rs_ready = sem("rs_ready")
        scaled = sem("scaled")
        placed = sem("placed")
        norm = NormScalars(nc, ctx, "em_", X, GT)
        tables.scratch(ctx)
        is_live = lambda k: live(k, K)
        with nc.Block() as block:
            @block.sync
            def _(sp):
                sp.dma_start(pw[:], patch_w).then_inc(pw_in, 16)

                def load(k, q, turn):
                    wait(sp, embedded, k - DEEP + 1)
                    sp.dma_start(ring[q][:], patches[ds(k, 1), :, :].rearrange("o p n -> (o p) n")).then_inc(patch_in[q], 16)

                load(0, 0, 0)
                tables.load(sp, bias_in, mask_in)
                for k in range(1, DEEP):
                    load(k, k, 0)
                sp.dma_start(common[:], common_in).then_inc(weights_in, 16)
                for b in range(2):
                    sp.dma_start(block_w[b][:], block_in[b]).then_inc(weights_in, 16)
                paired(sp, load, DEEP, K - 1, 2 * DEEP, K - 1, DEEP)
                sp.wait_ge(weights_in, 48)

            @block.tensor
            def _(pe):
                pe.wait_ge(pw_ready, 1)

                def step(k, q, turn):
                    pe.wait_ge(patch_in[q], 16 * turn + 16)
                    wait(pe, squared, GT * (k - DEEP + 1))
                    wait(pe, scaled, k - DEEP + 1)
                    for t in range(GT):
                        last = nc.tensor.matmul(ps[q][:, t * C:(t + 1) * C], ring[q][:, t * P:(t + 1) * P], pw_c[:],
                                                start=True, stop=True)
                    last.then_inc(embedded, 1)

                paired(pe, step, 0, K - 1, DEEP, K - 1, DEEP)

            @block.scalar
            def _(act):
                def step(k, q, turn):
                    act.wait_ge(embedded, k + 1)
                    wait(act, ve_ready, k - DEEP + 1)
                    for t in range(GT):
                        wait(act, squared, GT * k + t - 1)
                        nc.scalar.activation(sq[t % 2][:], ps[q][:, t * C:(t + 1) * C], ACT.Square, scale=C ** -0.5,
                                             accum_out=var[q][:, t:t + 1]).then_inc(squared, 1)

                paired(act, step, 0, K - 1, DEEP, K - 1, DEEP)

            @block.gpsimd
            def _(pool):
                norm.prepare(pool)
                nc.gpsimd.memset(X2[:], 0.0).then_inc(cleared, 1)
                pool.wait_ge(cleared, 1)

                def step(k, q, turn):
                    p = q % 2
                    if is_live(k):
                        wait(pool, rs_ready, k)
                        pool.wait_ge(squared, GT * k + GT)
                        nc.gpsimd.tensor_tensor(ve[:], var[q][:], norm.eps[:], ALU.add).then_inc(ve_ready, 1)
                        pool.wait_ge(ve_ready, k + 1)
                        wait(pool, scaled, k - 1)
                        nc.gpsimd.tensor_tensor(rs[p][:], ve[:], norm.half[:], ALU.pow).then_inc(rs_ready, 1)
                    if is_live(k - 4):
                        norm.invert(pool, k - 4, p)

                paired(pool, step, 0, K + 3, 2 * DEEP, K - 1, DEEP)

            @block.vector
            def _(dve):
                dve.wait_ge(pw_in, 16)
                nc.vector.reduce_sum(pw_mean[:], pw[:], AX.X).then_inc(pw_m, 1)
                dve.wait_ge(pw_m, 1)
                nc.vector.tensor_scalar(pw_mean[:], pw_mean[:], 1.0 / C, None, ALU.mult).then_inc(pw_m, 1)
                dve.wait_ge(pw_m, 2)
                nc.vector.tensor_scalar(pw_c[:], pw[:], pw_mean[:, 0:1], None, ALU.subtract).then_inc(pw_ready, 1)
                padded.clear(dve, padding)
                tables.make(dve, nc.vector)
                dve.wait_ge(weights_in, 48)
                gain = con("pg_row")
                offset = con("pbeta_row").unsqueeze(1).to_broadcast([P, GT, C])

                def step(k, q, turn):
                    p = q % 2
                    wait(dve, placed, at_most(k - 1, K))
                    wait(dve, norm.stats, at_most(k - 2, K))
                    wait(dve, norm.aggr, at_most(k - 3, K))
                    if is_live(k):
                        dve.wait_ge(rs_ready, k + 1)
                        for t in range(GT):
                            last = nc.vector.scalar_tensor_tensor(gained[p][:, t, :], ps[q][:, t * C:(t + 1) * C],
                                                                  rs[p][:, t:t + 1], gain, ALU.mult, ALU.mult)
                        last.then_inc(scaled, 1)
                    if is_live(k - 2):
                        norm.statistics(k - 2, p)
                    if is_live(k - 5):
                        norm.keep(dve, k - 5, 1 - p)
                    wait(dve, norm.kept, at_most(2 * (k - 4), 2 * K))
                    if is_live(k - 1):
                        dve.wait_ge(scaled, k)
                        nc.vector.tensor_tensor(X[:, ds((k - 1) * GT, GT), 0:C], gained[1 - p][:], offset, ALU.add).then_inc(placed, 1)
                    if is_live(k - 3):
                        norm.aggregate(k - 3, 1 - p)

                paired(dve, step, 0, K + 4, 2 * DEEP, K - 1, DEEP)


def attention(nc, b, X, con, wt, bias, padded, arriving):
    with ExitStack() as ctx:
        sb = lambda name, shape, dt=F32: ctx.enter_context(nc.sbuf_tensor(f"at{b}_{name}", shape, dt))
        pb = lambda name, shape, dt=F32: ctx.enter_context(nc.psum_tensor(f"at{b}_{name}", shape, dt))
        sem = lambda name: ctx.enter_context(nc.semaphore(f"at{b}_{name}"))
        KH = NH * TOK

        select = sb("select", [P, P], BF16)
        qbs = sb("qbs", [P, 1])
        vb_wide = sb("vb_wide", [C, P])
        const_row = sb("const_row", [P, C])
        xn = [sb(f"xn{i}", [P, 2, C]) for i in range(2)]
        xT = [sb(f"xT{i}", [P, 2, 2, C]) for i in range(2)]
        q_bd, v_bd, prob = padded.q_bd, padded.v_bd, padded.prob
        k_sb = sb("k_sb", [P, 2, TOK])
        k_bd = [sb(f"k_bd{i}", [P, 2, NH, TOK]) for i in range(2)]
        mx = [sb(f"mx{w}", [P, NH]) for w in range(2)]
        probT = [sb(f"probT{w}", [P, NH // 2, P]) for w in range(2)]
        rsum = sb("rsum", [P, 2 * NH // 2, 2])
        o = sb("o", [P, 2, C])
        oT = sb("oT", [P, P])

        ps_xt = pb("ps_xt", [P, 512])
        ps_qkv = pb("ps_qkv", [P, 512])
        ps_s = [pb(f"ps_s{w}", [P, 512]) for w in range(2)]
        ps_pt = [pb(f"ps_pt{w}", [P, 512]) for w in range(2)]
        ps_o = pb("ps_o", [P, 512])
        ps_misc = pb("ps_misc", [P, 512])
        PS_Q, PS_K, PS_V = 0, 2 * TOK, 4 * TOK
        PS_V = 256

        operands = sem("operands")
        const_ps = sem("const_ps")
        const_ready = sem("const_ready")
        xn_ready = sem("xn_ready")
        offset_added = sem("offset_added")
        xt_ps = sem("xt_ps")
        xt_ready = sem("xt_ready")
        qkv_ps = sem("qkv_ps")
        k_ready = sem("k_ready")
        q_ready = sem("q_ready")
        kbd_ready = sem("kbd_ready")
        v_ready = sem("v_ready")
        s_ps = sem("s_ps")
        max_ready = sem("max_ready")
        shifted = sem("shifted")
        exp_ready = sem("exp_ready")
        pt_ps = sem("pt_ps")
        pt_ready = sem("pt_ready")
        pv_ps = sem("pv_ps")
        rsum_ready = sem("rsum_ready")
        o_ready = sem("o_ready")
        ot_ps = sem("ot_ps")
        ot_ready = sem("ot_ready")
        pr_ps = sem("pr_ps")
        x_ready = sem("x_ready")
        summed = sem("summed")
        norm = NormScalars(nc, ctx, f"at{b}_", X, 2)

        def variant(s, c):
            if not b:
                return 0
            return (1 if c == NW - 1 else 0) + (2 if isinstance(s, int) and s >= U - NW else 0)

        with nc.Block() as block:
            if arriving is not None:
                roll, rolled = arriving

                @block.sync
                def _(sp):
                    sp.wait_ge(rolled, roll.issue(sp, rolled, 2, NW))

            @block.gpsimd
            def _(pool):
                norm.prepare(pool)
                mask_h = con("head_mask").unsqueeze(2).to_broadcast([P, NH, TOK])
                pool.wait_ge(const_ready, 1)
                row = const_row[:].unsqueeze(1).to_broadcast([P, 2, C])

                def step(s, c):
                    p = c % 2
                    if live(s + 1):
                        pool.wait_ge(k_ready, s + 2)
                        wait(pool, s_ps, 2 * s)
                        for w in range(2):
                            nc.gpsimd.tensor_tensor(k_bd[1 - p][:, w, :, :],
                                                    k_sb[:, w, :].unsqueeze(1).to_broadcast([P, NH, TOK]), mask_h,
                                                    ALU.mult).then_inc(kbd_ready, 1)
                    if live(s + 3):
                        pool.wait_ge(xn_ready, s + 4)
                        pool.wait_ge(const_ready, 1)
                        xs = X[:, ds((s + 3) * 2, 2), 0:C]
                        nc.gpsimd.tensor_tensor(xs, xs, row, ALU.add).then_inc(offset_added, 1)
                    if live(s - 5):
                        norm.invert(pool, s - 5, 1 - p)

                skewed(pool, step, -3, U + 4)

            @block.tensor
            def _(pe):
                pe.wait_ge(operands, 1)
                nc.tensor.matmul(ps_misc[:, 0:C], vb_wide[:], wt(b, "pBD")[0:C, 0:C], start=True, stop=True).then_inc(const_ps, 1)
                pe.wait_ge(const_ready, 1)

                def scores(s, c, w):
                    p = c % 2
                    pe.wait_ge(kbd_ready, 2 * s + w + 1)
                    if w == 0:
                        pe.wait_ge(q_ready, s + 1)
                    wait(pe, shifted, 2 * s + w - 1)
                    if w == 1:
                        nc.tensor.matmul(ps_s[w][:, 0:KH], select[:], bias.hi_mid[:], start=True, stop=False)
                        nc.tensor.matmul(ps_s[w][:, 0:KH], select[:], bias.lo[:, variant(s, c), :], start=False, stop=False)
                    nc.tensor.matmul(ps_s[w][:, 0:KH], q_bd[p][:, w, :, :].rearrange("p g q -> p (g q)"),
                                     k_bd[p][:, w, :, :].rearrange("p h k -> p (h k)"),
                                     start=(w == 0), stop=True).then_inc(s_ps, 1)

                def transpose_probs(u, w):
                    pe.wait_ge(exp_ready, 2 * u + w + 1)
                    wait(pe, pt_ready, 2 * u + w - 1)
                    for hp in range(NH // 2):
                        last = nc.tensor.transpose(ps_pt[w][:, hp * P:(hp + 1) * P],
                                                   prob[w][:, 2 * hp:2 * hp + 2, :].rearrange("p h k -> p (h k)"), con("ident"))
                    last.then_inc(pt_ps, 1)

                def attend(u, p, w):
                    pe.wait_ge(pt_ready, 2 * u + w + 1)
                    if w == 0:
                        pe.wait_ge(v_ready, u + 1)
                        wait(pe, o_ready, u)
                    for hp in range(NH // 2):
                        at = (w * 4 + hp) * 4 * (HD + 1)
                        last = nc.tensor.matmul(ps_o[:, at:at + 4 * (HD + 1)].rearrange("p (g e) -> p g e", g=2),
                                                probT[w][:, hp, :],
                                                v_bd[p][:, w, :, hp, :, :].rearrange("p g h e -> p g (h e)"),
                                                start=True, stop=True)
                    last.then_inc(pv_ps, 1)

                def step(s, c):
                    p = c % 2
                    if live(s):
                        scores(s, c, 0)
                    if live(s - 1):
                        transpose_probs(s - 1, 1)
                    if live(s - 2):
                        pe.wait_ge(o_ready, s - 1)
                        wait(pe, x_ready, s - 2)
                        nc.tensor.transpose(ps_misc[:, 0:P], o[:].rearrange("p w c -> p (w c)"), con("ident")).then_inc(ot_ps, 1)
                    if live(s + 1):
                        pe.wait_ge(xt_ready, s + 2)
                        wait(pe, v_ready, s + 1)
                        wait(pe, q_ready, s + 1)
                        tokens = xT[1 - p][:, :, 0, 0:TOK]
                        for at, name in ((PS_Q, "qBD"), (PS_K, "kBD")):
                            nc.tensor.matmul(ps_qkv[:, at:at + 2 * TOK].rearrange("p (w t) -> p w t", w=2), wt(b, name), tokens,
                                             start=True, stop=True)
                        for w in range(2):
                            twice = xT[1 - p][:, w, :, :].rearrange("p a t -> p (a t)")
                            last = nc.tensor.matmul(ps_qkv[:, PS_V + w * P:PS_V + (w + 1) * P], twice,
                                                    wt(b, "vBD"), start=True, stop=True)
                        last.then_inc(qkv_ps, 1)
                    if live(s - 1):
                        attend(s - 1, 1 - p, 0)
                    if live(s - 2):
                        pe.wait_ge(ot_ready, s - 1)
                        for w in range(2):
                            r = slice(C * w, C * w + C)
                            for g in range(2):
                                last = nc.tensor.matmul(ps_misc[r, P + g * C:P + (g + 1) * C], oT[:, C * g:C * g + C],
                                                        wt(b, "pBD")[:, r], start=True, stop=True)
                        last.then_inc(pr_ps, 1)
                    if live(s):
                        scores(s, c, 1)
                    if live(s + 2):
                        pe.wait_ge(xn_ready, s + 3)
                        wait(pe, xt_ready, s + 2)
                        nc.tensor.transpose(ps_xt[:, 0:P], xn[p][:].rearrange("p g c -> p (g c)"), con("ident")).then_inc(xt_ps, 1)
                    if live(s - 1):
                        attend(s - 1, 1 - p, 1)
                    if live(s):
                        transpose_probs(s, 0)

                skewed(pe, step, -2, U + 1)

            @block.scalar
            def _(act):
                def copy_probs(u, w):
                    act.wait_ge(pt_ps, 2 * u + w + 1)
                    wait(act, pv_ps, 2 * u + w - 1)
                    nc.scalar.activation(probT[w][:], ps_pt[w][:].rearrange("p (h q) -> p h q", q=P), ACT.Copy).then_inc(pt_ready, 1)

                def exponential(u, w):
                    act.wait_ge(shifted, 2 * u + w + 1)
                    e = prob[w][:, :, 0:TOK]
                    nc.scalar.activation(e, e, ACT.Exp).then_inc(exp_ready, 1)

                def step(s, c):
                    p = c % 2
                    if live(s - 1):
                        copy_probs(s - 1, 1)
                    if live(s - 2):
                        act.wait_ge(ot_ps, s - 1)
                        wait(act, pr_ps, s - 2)
                        nc.scalar.activation(oT[:], ps_misc[:, 0:P], ACT.Copy).then_inc(ot_ready, 1)
                    if live(s + 1):
                        act.wait_ge(qkv_ps, s + 2)
                        wait(act, kbd_ready, 2 * s + 2)
                        nc.scalar.activation(k_sb[:], ps_qkv[:, PS_K:PS_K + 2 * TOK].rearrange("p (w t) -> p w t", w=2),
                                             ACT.Identity, bias=wt(b, "kb")).then_inc(k_ready, 1)
                        wait(act, s_ps, 2 * s)
                        for g in range(2):
                            r = slice(C * g, C * g + C)
                            last = nc.scalar.activation(q_bd[1 - p][r, :, g, 0:TOK],
                                                        ps_qkv[r, PS_Q:PS_Q + 2 * TOK].rearrange("p (w t) -> p w t", w=2),
                                                        ACT.Identity, bias=qbs[r, :], scale=SCALE)
                        last.then_inc(q_ready, 1)
                    if live(s):
                        exponential(s, 0)
                    if live(s + 2):
                        act.wait_ge(xt_ps, s + 3)
                        wait(act, qkv_ps, s + 1)
                        nc.scalar.activation(xT[p][:], ps_xt[:, 0:P].rearrange("p (w t) -> p w t", w=2).unsqueeze(2)
                                             .to_broadcast([P, 2, 2, C]), ACT.Identity,
                                             bias=wt(b, "n1b"), scale=wt(b, "n1g")).then_inc(xt_ready, 1)
                    if live(s + 1):
                        wait(act, pv_ps, 2 * s)
                        for h in range(2):
                            r = slice(C * h, C * h + C)
                            src = ps_qkv[r, PS_V:PS_V + 4 * C].rearrange("p (x a h d) -> p x a h d", a=NH // 2, h=2, d=HD)[:, :, :, h, :]
                            last = nc.scalar.activation(v_bd[1 - p][r, :, :, :, h, 0:HD].rearrange("p w g a d -> p (w g) a d"), src, ACT.Copy)
                        last.then_inc(v_ready, 1)
                    if live(s):
                        exponential(s, 1)
                        copy_probs(s, 0)

                act.wait_ge(operands, 1)
                skewed(act, step, -2, U + 1)

            @block.vector
            def _(dve):
                nc.vector.tensor_scalar(qbs[:], wt(b, "qb"), SCALE, None, ALU.mult)
                nc.vector.tensor_copy(vb_wide[:], wt(b, "vb")[0:C, :].to_broadcast([C, P]))
                nc.vector.tensor_copy(select[:].rearrange("p (g q) -> p g q", g=2)[0:C],
                                      con("ident")[0:C, 0:C].unsqueeze(1).to_broadcast([C, 2, C]))
                nc.vector.tensor_copy(select[:].rearrange("p (g q) -> p g q", g=2)[C:P],
                                      con("ident")[C:P, C:P].unsqueeze(1).to_broadcast([C, 2, C])).then_inc(operands, 1)
                dve.wait_ge(const_ps, 1)
                nc.vector.tensor_tensor(const_row[:], ps_misc[:, 0:C], wt(b, "pb_row"), ALU.add).then_inc(const_ready, 1)

                def normalize(dve, u, p):
                    wait(dve, xt_ps, u - 1)
                    for g in range(2):
                        last = nc.vector.tensor_scalar(xn[p][:, g, :], X[:, ds(2 * u + g, 1), 0:C].rearrange("p o c -> p (o c)"),
                                                       scalar(u, g, RSTD), scalar(u, g, NMR), ALU.mult, ALU.add)
                    last.then_inc(xn_ready, 1)

                def scalar(u, g, col):
                    return X[:, ds(2 * u + g, 1), col:col + 1].rearrange("p o c -> p (o c)")

                def shift(s, c, w, more=()):
                    sc = ps_s[w][:, 0:KH].rearrange("p (h k) -> p h k", h=NH)
                    if w == 0:
                        wait(dve, pt_ps, 2 * s - 1)
                        dve.wait_ge(s_ps, 2 * s + 1)
                        scored, sc = sc, prob[0][:, :, 0:TOK]
                        nc.vector.tensor_tensor(sc, scored, bias.table[:, variant(s, c), :].rearrange("p (h k) -> p h k", h=NH),
                                                ALU.add).then_inc(summed, 1)
                        dve.wait_ge(summed, s + 1)
                    else:
                        dve.wait_ge(s_ps, 2 * s + 2)
                    nc.vector.reduce_max(mx[w][:], sc, AX.X).then_inc(max_ready, 1)
                    for sem_, value in more:
                        wait(dve, sem_, value)
                    dve.wait_ge(max_ready, 2 * s + w + 1)
                    wait(dve, pt_ps, 2 * s + w - 1)
                    nc.vector.tensor_tensor(prob[w][:, :, 0:TOK], sc, mx[w][:].unsqueeze(2).to_broadcast([P, NH, TOK]),
                                            ALU.subtract).then_inc(shifted, 1)

                def step(s, c):
                    p = c % 2
                    settled = ((x_ready, s - 2), (norm.stats, s - 3), (norm.aggr, s - 4))
                    if live(s):
                        shift(s, c, 0, settled)
                    else:
                        for sem_, value in settled:
                            wait(dve, sem_, min(value, U))
                    if live(s - 6):
                        norm.keep(dve, s - 6, p)
                    wait(dve, norm.kept, at_most(2 * (s - 5), 2 * U))
                    if arriving is not None and isinstance(s, int) and s + 3 == NW:
                        dve.wait_ge(rolled, roll.signals(2, NW))
                    if live(s + 3):
                        normalize(dve, s + 3, 1 - p)
                    if live(s - 3):
                        norm.statistics(s - 3, 1 - p)
                    if live(s - 4):
                        norm.aggregate(s - 4, p)
                    if live(s):
                        shift(s, c, 1)
                    if live(s - 2):
                        u = s - 2
                        dve.wait_ge(pr_ps, u + 1)
                        dve.wait_ge(offset_added, u + 1)
                        xs = X[:, ds(2 * u, 2), 0:C]
                        nc.vector.tensor_tensor(xs, xs, ps_misc[:, P:2 * P].rearrange("p (g c) -> p g c", g=2), ALU.add).then_inc(x_ready, 1)
                    if live(s - 1):
                        u = s - 1
                        dve.wait_ge(pv_ps, 2 * u + 2)
                        wait(dve, o_ready, u)
                        for g in range(2):
                            r = slice(C * g, C * g + C)
                            mine = ps_o[r, 0:32 * (HD + 1)].rearrange("p (x g h e) -> p x g h e", g=2, h=2, e=HD + 1)[:, :, g, :, :]
                            last = nc.vector.reciprocal(rsum[r, :, :].unsqueeze(3), mine[:, :, :, HD:HD + 1])
                        last.then_inc(rsum_ready, 1)
                        dve.wait_ge(rsum_ready, u + 1)
                        wait(dve, ot_ps, u)
                        for g in range(2):
                            r = slice(C * g, C * g + C)
                            mine = ps_o[r, 0:32 * (HD + 1)].rearrange("p (x g h e) -> p x g h e", g=2, h=2, e=HD + 1)[:, :, g, :, 0:HD]
                            last = nc.vector.tensor_tensor(o[r, :, :].rearrange("p w (a h d) -> p (w a) h d", h=2, d=HD), mine,
                                                           rsum[r, :, :].unsqueeze(3).to_broadcast([C, NH, 2, HD]), ALU.mult)
                        last.then_inc(o_ready, 1)

                skewed(dve, step, -3, U + 5)


def mlp(nc, b, X, con, wt, H0, roll, tables, bias_in, mask_in, loads=()):
    with ExitStack() as ctx:
        sb = lambda name, shape, dt=F32: ctx.enter_context(nc.sbuf_tensor(f"ml{b}_{name}", shape, dt))
        pb = lambda name, shape, dt=F32: ctx.enter_context(nc.psum_tensor(f"ml{b}_{name}", shape, dt))
        sem = lambda name: ctx.enter_context(nc.semaphore(f"ml{b}_{name}"))
        GU = 4
        K = U // GU
        GT = 2 * GU
        COL = GT * TOK
        xn = [sb(f"xn{i}", [P, GT, C]) for i in range(2)]
        xT = [sb(f"xT{i}", [P, GT, TOK]) for i in range(2)]
        hid = [sb(f"hid{i}", [P, 2, 2, COL]) for i in range(2)]
        turn = [sb(f"turn{i}", [P, GT, C]) for i in range(2)]
        y_sb = [sb(f"y_sb{i}", [P, GT, TOK]) for i in range(2)]
        ps_xt = pb("ps_xt", [P, 512])
        ps_h = [[pb(f"ps_h{f}{g}", [P, 512]) for g in range(2)] for f in range(2)]
        ps_y = [pb(f"ps_y{i}", [P, 512]) for i in range(2)]
        ps_t = pb("ps_t", [P, 512])
        zeroed = sem("zeroed")
        scaled = sem("scaled")
        xn_ready = sem("xn_ready")
        xt_ps = sem("xt_ps")
        xt_ready = sem("xt_ready")
        h_ps = sem("h_ps")
        h_ready = sem("h_ready")
        y_ps = sem("y_ps")
        turn_ready = sem("turn_ready")
        y_ready = sem("y_ready")
        t_ps = sem("t_ps")
        x_ready = sem("x_ready")
        norm = NormScalars(nc, ctx, f"ml{b}_", X, GT)
        is_live = lambda k: live(k, K)
        first_block = H0 is None
        if first_block:
            tables.scratch(ctx)
            rolled = sem("rolled")
        loaded = sem("loaded")
        with nc.Block() as block:
            if first_block:
                @block.sync
                def _(sp):
                    tables.load(sp, bias_in, mask_in)
                    sp.wait_ge(norm.kept, 2 * 2 * NW // GU)
                    sp.wait_ge(rolled, roll.issue(sp, rolled, 0, 2))

            if loads:
                @block.sync
                def _(sp):
                    for dst, source in loads:
                        sp.dma_start(dst[:], source).then_inc(loaded, 16)
                    sp.wait_ge(loaded, 16 * len(loads))

            @block.gpsimd
            def _(pool):
                if first_block:
                    for i in range(2):
                        nc.gpsimd.memset(turn[i][:], 0.0).then_inc(zeroed, 1)
                    norm.prepare(pool)
                    tables.make(pool, nc.gpsimd)
                    paired(pool, lambda k, p, half: norm.invert(pool, k, p), 0, K - 1, 4, K - 1)

            @block.tensor
            def _(pe):
                def transpose_units(bank, src):
                    for u in range(GU):
                        last = nc.tensor.transpose(bank[:, u * P:(u + 1) * P],
                                                   src[:, 2 * u:2 * u + 2, :].rearrange("p t c -> p (t c)"), con("ident"))
                    return last

                def step(k, p, half):
                    if is_live(k):
                        pe.wait_ge(xt_ready, k + 1)
                        for f in range(2):
                            for g in range(2):
                                wait(pe, h_ready, 4 * (k - 1) + 2 * f + g + 1)
                                nc.tensor.matmul(ps_h[f][g][:, 0:COL], wt(b, f"w1T{g}")[:, f * P:(f + 1) * P],
                                                 xT[p][:].rearrange("p t c -> p (t c)"), start=True, stop=True).then_inc(h_ps, 1)
                    if is_live(k - 2):
                        pe.wait_ge(turn_ready, k - 1)
                        wait(pe, x_ready, k - 2)
                        transpose_units(ps_t, turn[p]).then_inc(t_ps, 1)
                    if is_live(k + 1):
                        pe.wait_ge(xn_ready, k + 2)
                        wait(pe, xt_ready, k + 1)
                        transpose_units(ps_xt, xn[1 - p]).then_inc(xt_ps, 1)
                    if is_live(k - 1):
                        wait(pe, turn_ready if first_block else y_ready, k - 2)
                        for f in range(2):
                            for g in range(2):
                                pe.wait_ge(h_ready, 4 * (k - 1) + 2 * f + g + 1)
                                last = nc.tensor.matmul(ps_y[1 - p][g * C:(g + 1) * C, 0:COL], wt(b, "w2T")[:, f * C:(f + 1) * C],
                                                        hid[1 - p][:, f, g, :], start=(f == 0), stop=(f == 1))
                        last.then_inc(y_ps, 1)

                paired(pe, step, -1, K + 1, 6, 13)

            @block.scalar
            def _(act):
                if first_block:
                    act.wait_ge(zeroed, 2)

                def step(k, p, half):
                    if is_live(k):
                        wait(act, y_ps, k - 1)
                        for f in range(2):
                            for g in range(2):
                                act.wait_ge(h_ps, 4 * k + 2 * f + g + 1)
                                nc.scalar.activation(hid[p][:, f, g, :], ps_h[f][g][:, 0:COL], ACT.Gelu,
                                                     bias=wt(b, "b1")[:, f:f + 1]).then_inc(h_ready, 1)
                    if is_live(k - 1):
                        wait(act, t_ps, k - 2)
                        if first_block:
                            act.wait_ge(y_ps, k)
                            nc.scalar.activation(turn[1 - p][:, :, 0:TOK], ps_y[1 - p][:, 0:COL].rearrange("p (t c) -> p t c", c=TOK),
                                                 ACT.Identity, bias=wt(b, "b2")).then_inc(turn_ready, 1)
                        else:
                            nc.scalar.activation(turn[1 - p][:], X[:, ds((k - 1) * GT, GT), 0:C], ACT.Copy).then_inc(turn_ready, 1)
                            act.wait_ge(y_ps, k)
                            wait(act, x_ready, k - 2)
                            nc.scalar.activation(y_sb[1 - p][:], ps_y[1 - p][:, 0:COL].rearrange("p (t c) -> p t c", c=TOK),
                                                 ACT.Identity, bias=wt(b, "b2")).then_inc(y_ready, 1)

                paired(act, step, 0, K, 6, 13)

            @block.vector
            def _(dve):
                def columns_of(col, k):
                    return X[:, ds(k * GT, GT), col:col + 1].to_broadcast([P, GT, C])

                def finish(k, p, half):
                    dve.wait_ge(t_ps, k + 1)
                    if not first_block:
                        dve.wait_ge(y_ready, k + 1)
                    if first_block:
                        xs = X[:, ds(k * GT, GT), 0:C]
                        nc.vector.tensor_tensor(xs, xs, ps_t[:].rearrange("p (u g c) -> p (u g) c", g=2, c=C), ALU.add).then_inc(x_ready, 1)
                        return
                    rows = [(0, WS, half * WS + SHIFT)]
                    if isinstance(half, int) and half == NW - 1:
                        rows = [(0, WS - SHIFT, SIDE - WS + SHIFT), (WS - SHIFT, WS, 0)]
                    for u in range(GU):
                        wcol = GU * p + u
                        cols = [(0, WS, wcol * WS + SHIFT)]
                        if wcol == NW - 1:
                            cols = [(0, WS - SHIFT, SIDE - WS + SHIFT), (WS - SHIFT, WS, 0)]
                        for w in range(2):
                            image = H0[:, w * TIME:(w + 1) * TIME].rearrange("p (y x) -> p y x", x=SIDE)
                            own = y_sb[p][:, 2 * u + w, :].rearrange("p (i j) -> p i j", j=WS)
                            old = ps_t[:, u * P + w * C:u * P + w * C + TOK].rearrange("p (i j) -> p i j", j=WS)
                            for i0, i1, y in rows:
                                for j0, j1, x in cols:
                                    last = nc.vector.tensor_tensor(image[:, ds(y, i1 - i0), x:x + j1 - j0], own[:, i0:i1, j0:j1],
                                                                   old[:, i0:i1, j0:j1], ALU.add)
                    last.then_inc(x_ready, 1)

                def step(k, p, half):
                    if first_block:
                        wait(dve, x_ready, at_most(k - 2, K))
                        wait(dve, norm.stats, at_most(k - 3, K))
                        wait(dve, norm.aggr, at_most(k - 4, K))
                    if is_live(k + 2):
                        wait(dve, xt_ps, k + 1)
                        nc.vector.tensor_tensor(xn[p][:], X[:, ds((k + 2) * GT, GT), 0:C], columns_of(RSTD, k + 2), ALU.mult).then_inc(scaled, 1)
                    if first_block:
                        if is_live(k - 3):
                            norm.statistics(k - 3, 1 - p)
                        if is_live(k - 5):
                            norm.keep(dve, k - 5, 1 - p)
                        wait(dve, norm.kept, at_most(2 * (k - 5), 2 * K))
                    if is_live(k + 2):
                        dve.wait_ge(scaled, k + 3)
                        nc.vector.tensor_tensor(xn[p][:], xn[p][:], columns_of(NMR, k + 2), ALU.add).then_inc(xn_ready, 1)
                    if first_block and is_live(k - 4):
                        norm.aggregate(k - 4, p)
                    if is_live(k + 1):
                        dve.wait_ge(xt_ps, k + 2)
                        wait(dve, h_ps, 4 * k)
                        nc.vector.tensor_scalar(xT[1 - p][:], ps_xt[:].rearrange("p (t c) -> p t c", c=C)[:, :, 0:TOK],
                                                wt(b, "n2g"), wt(b, "n2b"), ALU.mult, ALU.add).then_inc(xt_ready, 1)
                    if is_live(k - 2):
                        finish(k - 2, p, half - 1)

                paired(dve, step, -2, K + 4 if first_block else K + 1, 6, 13)


class Roll:

    def __init__(self, nc, X, X2):
        self.src = X[:].rearrange("p (a b g) r -> p a b (g r)", a=NW, b=NW)
        self.dst = X2[:].rearrange("p (a b g) r -> p a b (g r)", a=NW, b=NW)

    @staticmethod
    def moves(first, end):
        for w in range(2):
            for i in range(WS):
                for j0, j1 in ((0, SHIFT), (SHIFT, WS)):
                    up, left = i < SHIFT, j0 < SHIFT
                    frm = C * w + WS * i + j0
                    to = C * w + WS * ((i - SHIFT) % WS) + (j0 - SHIFT) % WS
                    rows = [(first, end, first)]
                    if up:
                        rows = [(max(first, 1), end, max(first, 1) - 1)] + ([(0, 1, NW - 1)] if first == 0 else [])
                    cols = [(0, NW, 0)] if not left else [(1, NW, 0), (0, 1, NW - 1)]
                    for a0, a1, a2 in rows:
                        for b0, b1, b2 in cols:
                            yield frm, to, j1 - j0, a0, a1, a2, b0, b1, b2

    def signals(self, first, end):
        return 16 * len(list(self.moves(first, end)))

    def issue(self, eng, rolled, first, end):
        for frm, to, n, a0, a1, a2, b0, b1, b2 in self.moves(first, end):
            eng.dma_start(self.dst[to:to + n, a2:a2 + a1 - a0, b2:b2 + b1 - b0, :],
                          self.src[frm:frm + n, a0:a1, b0:b1, :]).then_inc(rolled, 16)
        return self.signals(first, end)


def recycle(nc):
    with nc.Block() as block:
        @block.gpsimd
        def _(pool):
            clear_spent(nc)


CH = 448
NCH = 2 * TIME // CH
CLS = 2 * TIME
COLS = 2 * SEQ
LN_EXP_SET = 6
N1, N2, N3 = 14, 14, 16
LANES = 2 * TIME // N1


def chunks(eng, step, last):
    paired(eng, lambda k, q, turn: step(k, q), 0, last, 5, 12, 4)


def extent(k):
    return (CLS, 2) if isinstance(k, int) and k == NCH else (k * CH, CH)


def class_tokens(nc, H0, cls):
    with nc.Block() as block:
        @block.vector
        def _(dve):
            nc.vector.tensor_copy(H0[:, CLS:COLS], cls.to_broadcast([P, 2]))

        @block.gpsimd
        def _(pool):
            clear_spent(nc)


def channel_norm(nc, name, src, con, finish, product=None, after_product=None, on_pool=None, out_dma=None, setup=None):
    with ExitStack() as ctx:
        sb = lambda nm, shape, dt=F32: ctx.enter_context(nc.sbuf_tensor(f"{name}_{nm}", shape, dt))
        pb = lambda nm, shape, dt=F32: ctx.enter_context(nc.psum_tensor(f"{name}_{nm}", shape, dt))
        sem = lambda nm: ctx.enter_context(nc.semaphore(f"{name}_{nm}"))
        centred = [sb(f"centred{i}", [P, CH]) for i in range(4)]
        square = [sb(f"square{i}", [P, CH]) for i in range(4)]
        lnv = [sb(f"lnv{i}", [P, CH]) for i in range(2)]
        rstd = [sb(f"rstd{i}", [P, CH]) for i in range(4)]
        eps = sb("eps", [P, 1])
        ps_mean = [pb(f"ps_mean{i}", [P, 512]) for i in range(2)]
        ps_var = [pb(f"ps_var{i}", [P, 512]) for i in range(2)]
        ps_x = [pb(f"ps_x{i}", [P, 512]) for i in range(2)]
        eps_set = sem("eps_set")
        mean_ps = sem("mean_ps")
        centred_ready = sem("centred_ready")
        square_ready = sem("square_ready")
        var_ps = sem("var_ps")
        ln_ready = sem("ln_ready")
        rstd_ready = sem("rstd_ready")
        done = sem("done")
        extra_ps = sem("extra_ps")
        extra_done = sem("extra_done")
        inner = sem("inner")
        stored = [sem(f"stored{i}") for i in range(4)]
        ones = con("mean_ones")
        is_live = lambda k: live(k, NCH + 1)
        with nc.Block() as block:
            @block.tensor
            def _(pe):
                def step(k, q):
                    if is_live(k):
                        at, n = extent(k)
                        wait(pe, centred_ready, k - 1)
                        nc.tensor.matmul(ps_mean[q % 2][:, 0:n], ones, src[:, ds(at, n)], start=True, stop=True).then_inc(mean_ps, 1)
                    if is_live(k - 1):
                        at, n = extent(k - 1)
                        v = (q - 1) % 4
                        pe.wait_ge(square_ready, k)
                        wait(pe, ln_ready, k - 2)
                        nc.tensor.matmul(ps_var[v % 2][:, 0:n], ones, square[v][:, 0:n], start=True, stop=True).then_inc(var_ps, 1)
                    if product is not None and is_live(k - 3):
                        at, n = extent(k - 3)
                        pe.wait_ge(done, k - 2)
                        wait(pe, extra_done, k - 4)
                        product(at, n, ps_x[(q - 3) % 2]).then_inc(extra_ps, 1)

                chunks(pe, step, NCH + (1 if product is None else 3))

            @block.scalar
            def _(act):
                nc.scalar.add_instruction(mybir.InstLoadActFuncSet(name=nc.get_next_instruction_name(), engine=mybir.EngineType.Activation,
                                                                   act_func_set_id=LN_EXP_SET, ins=[], outs=[]))
                act.wait_ge(eps_set, 1)

                def step(k, q):
                    if is_live(k):
                        at, n = extent(k)
                        act.wait_ge(centred_ready, k + 1)
                        wait(act, var_ps, k - 3)
                        nc.scalar.activation(square[q][:, 0:n], centred[q][:, 0:n], ACT.Square).then_inc(square_ready, 1)
                    if is_live(k - 1):
                        at, n = extent(k - 1)
                        v = (q - 1) % 4
                        act.wait_ge(var_ps, k)
                        wait(act, rstd_ready, k - 2)
                        nc.scalar.activation(lnv[v % 2][:, 0:n], ps_var[v % 2][:, 0:n], ACT.Ln, bias=eps[:]).then_inc(ln_ready, 1)
                        act.wait_ge(ln_ready, k)
                        wait(act, done, k - 4)
                        nc.scalar.activation(rstd[v][:, 0:n], lnv[v % 2][:, 0:n], ACT.Exp, scale=-0.5).then_inc(rstd_ready, 1)

                chunks(act, step, NCH + 1)

            @block.vector
            def _(dve):
                nc.vector.memset(eps[:], EPS).then_inc(eps_set, 1)
                if setup is not None:
                    setup(dve)

                def step(k, q):
                    if is_live(k):
                        at, n = extent(k)
                        dve.wait_ge(mean_ps, k + 1)
                        wait(dve, done, k - 3)
                        nc.vector.tensor_tensor(centred[q][:, 0:n], src[:, ds(at, n)], ps_mean[q % 2][:, 0:n], ALU.subtract).then_inc(centred_ready, 1)
                    if is_live(k - 2):
                        at, n = extent(k - 2)
                        v = (q - 2) % 4
                        dve.wait_ge(rstd_ready, k - 1)
                        finish(dve, k - 2, v, at, n, centred[v], rstd[v], done, inner, stored)
                    if after_product is not None and is_live(k - 4):
                        at, n = extent(k - 4)
                        dve.wait_ge(extra_ps, k - 3)
                        after_product(at, n, ps_x[q % 2]).then_inc(extra_done, 1)

                chunks(dve, step, NCH + (2 if product is None else 4))

            if on_pool is not None:
                @block.gpsimd
                def _(pool):
                    def step(k, q):
                        pool.wait_ge(done, k + 1)
                        on_pool(*extent(k))
                    chunks(pool, step, NCH)

            if out_dma is not None:
                @block.sync
                def _(sp):
                    def step(k, q):
                        sp.wait_ge(done, k + 1)
                        out_dma(sp, q, *extent(k)).then_inc(stored[q], 16)
                    chunks(sp, step, NCH)
                    for q in range(4):
                        sp.wait_ge(stored[q], 16 * ((NCH + 4 - q) // 4))


def mixer(nc, F, Z, U_, G, HU, H1, tw):
    with ExitStack() as ctx:
        sb = lambda nm, shape, dt=F32: ctx.enter_context(nc.sbuf_tensor(f"rec_{nm}", shape, dt))
        sem = lambda nm: ctx.enter_context(nc.semaphore(f"rec_{nm}"))
        NL, NS = LANES + 2, 2 * N3
        xs, z_start, ts = sb("xs", [P, NL]), sb("z_start", [P, NL]), sb("ts", [P, NL])
        fcls = sb("fcls", [P, 2])
        end_x, end_z = sb("end_x", [P, NS + 2, N2]), sb("end_z", [P, NS + 2, N2])
        vx, vz = sb("vx", [P, N2 + 1, NS + 2]), sb("vz", [P, N2 + 1, NS + 2])
        tx, tz = sb("tx", [P, NS + 2]), sb("tz", [P, NS + 2])
        wx, wz = sb("wx", [P, 2, N3]), sb("wz", [P, 2, N3])
        cx, cz = sb("cx", [P, LANES]), sb("cz", [P, LANES])
        made = sem("made")
        stt = nc.vector.scalar_tensor_tensor
        pb = lambda nm, shape, dt=F32: ctx.enter_context(nc.psum_tensor(f"mix_{nm}", shape, dt))
        ps = [pb(f"ps{i}", [P, 512]) for i in range(8)]
        sg = [sb(f"sg{i}", [P, CH]) for i in range(4)]
        pr = {name: [sb(f"pr_{name}{i}", [P, CH]) for i in range(2)] for name in ("dve", "pool")}
        z_there = sem("z_there")
        v_ps = sem("v_ps")
        g_ready = sem("g_ready")
        sg_ready = sem("sg_ready")
        gated = {"dve": sem("gated_dve"), "pool": sem("gated_pool")}
        on_pool = [2, 5, 8, 11]
        side = ["pool" if k in on_pool else "dve" for k in range(NCH + 1)]
        nth = [side[:k].count(side[k]) for k in range(NCH + 1)]

        def gate(eng, api, name):
            for k in (k for k in range(NCH + 1) if side[k] == name):
                at, n = extent(k)
                eng.wait_ge(sg_ready, k + 1)
                product = pr[name][nth[k] % 2]
                wait(eng, gated[name], 2 * (nth[k] - 1))
                api.tensor_tensor(product[:, 0:n], G[:, at:at + n], sg[k % 4][:, 0:n], ALU.mult).then_inc(gated[name], 1)
                eng.wait_ge(gated[name], 2 * nth[k] + 1)
                api.tensor_tensor(H1[:, at:at + n], product[:, 0:n], HU[:, at:at + n], ALU.add).then_inc(gated[name], 1)

        with nc.Block() as block:
            @block.tensor
            def _(pe):
                def direct(k):
                    at, n = extent(k)
                    nc.tensor.matmul(ps[k % 8][:, 0:n], tw("DBD"), U_[:, at:at + n], start=True, stop=False)

                for k in range(8):
                    direct(k)
                for k in range(NCH + 1):
                    at, n = extent(k)
                    if k >= 8:
                        pe.wait_ge(g_ready, k - 7)
                        direct(k)
                    pe.wait_ge(z_there, k + 1)
                    nc.tensor.matmul(ps[k % 8][:, 0:n], tw("CBD"), Z[:, at:at + n], start=False, stop=True).then_inc(v_ps, 1)

            @block.scalar
            def _(act):
                for k in range(NCH + 1):
                    at, n = extent(k)
                    act.wait_ge(v_ps, k + 1)
                    nc.scalar.activation(G[:, at:at + n], ps[k % 8][:, 0:n], ACT.Gelu, bias=tw("bCD")).then_inc(g_ready, 1)
                for k in range(NCH + 1):
                    at, n = extent(k)
                    act.wait_ge(g_ready, k + 1)
                    if k >= 4:
                        act.wait_ge(gated[side[k - 4]], 2 * nth[k - 4] + 1)
                    nc.scalar.activation(sg[k % 4][:, 0:n], G[:, at:at + n], ACT.Sigmoid).then_inc(sg_ready, 1)

            @block.gpsimd
            def _(pool):
                gate(pool, nc.gpsimd, "pool")

            @block.vector
            def _(dve):
                count = [0]

                def link(ins):
                    count[0] += 1
                    ins.then_inc(made, 1)
                    dve.wait_ge(made, count[0])

                s, neg_dsa = tw("s"), tw("neg_dsa")
                link(nc.vector.tensor_copy(fcls[:], F[:, CLS:COLS]))
                nc.vector.memset(xs[:], 0.0)
                nc.vector.memset(z_start[:], 0.0)
                nc.vector.memset(end_x[:], 0.0)
                nc.vector.memset(end_z[:], 0.0)
                nc.vector.memset(vx[:, 0, :], 0.0)
                nc.vector.memset(vz[:, 0, :], 0.0)
                nc.vector.tensor_copy(wx[:, :, 0], fcls[:])
                nc.vector.tensor_scalar(wz[:, :, 0], fcls[:], DT, None, ALU.mult)
                link(nc.vector.memset(F[:, CLS:NL * N1], 0.0))
                nc.vector.memset(xs[:, LANES:LANES + 1], 1.0)
                nc.vector.memset(vx[:, 0, NS:NS + 1], 1.0)
                nc.vector.memset(vz[:, 0, NS + 1:NS + 2], 1.0)
                link(nc.vector.memset(z_start[:, LANES + 1:NL], 1.0))
                f_at = F[:, 0:NL * N1].rearrange("p (l n) -> p l n", n=N1)
                z_at = Z[:, 0:NL * N1].rearrange("p (l n) -> p l n", n=N1)
                halves = [slice(0, LANES // 2), slice(LANES // 2, NL)]

                def at(t, h, n):
                    return t[:, h, ds(n, 1)].rearrange("p l o -> p (l o)")

                base = count[0]

                def local(n):
                    before = lambda h: z_start[:, h] if isinstance(n, int) and n == 0 else at(z_at, h, n - 1)
                    done = base + 6 * n
                    for q, h in enumerate(halves):
                        wait(dve, made, done - 1 + q)
                        stt(ts[:, h], before(h), neg_dsa, at(f_at, h, n), ALU.mult, ALU.add).then_inc(made, 1)
                    for q, h in enumerate(halves):
                        dve.wait_ge(made, done + 1 + q)
                        stt(xs[:, h], xs[:, h], s, ts[:, h], ALU.mult, ALU.add).then_inc(made, 1)
                    for q, h in enumerate(halves):
                        dve.wait_ge(made, done + 3 + q)
                        stt(at(z_at, h, n), xs[:, h], DT, before(h), ALU.mult, ALU.add).then_inc(made, 1)

                local(0)
                local(1)
                with dve.Fori(0, (N1 - 2) // 4) as i:
                    for j in range(4):
                        local(4 * i + 2 + j)
                count[0] += 6 * N1
                dve.wait_ge(made, count[0])

                last = z_at[:, :, N1 - 1]
                a11, a12 = xs[:, LANES:LANES + 1], xs[:, LANES + 1:NL]
                a21, a22 = last[:, LANES:LANES + 1], last[:, LANES + 1:NL]
                nc.vector.tensor_copy(end_x[:, 0:NS, :].rearrange("p s c -> p (s c)"), xs[:, 0:LANES])
                link(nc.vector.tensor_copy(end_z[:, 0:NS, :].rearrange("p s c -> p (s c)"), last[:, 0:LANES]))

                base = count[0]
                for k in range(N2):
                    x, z = (v[:, ds(k, 1), :].rearrange("p o l -> p (o l)") for v in (vx, vz))
                    x1, z1 = (v[:, ds(k + 1, 1), :].rearrange("p o l -> p (o l)") for v in (vx, vz))
                    every = slice(0, NS + 2)
                    stt(tx[:], x, a11, at(end_x, every, k), ALU.mult, ALU.add).then_inc(made, 1)
                    stt(tz[:], x, a21, at(end_z, every, k), ALU.mult, ALU.add).then_inc(made, 1)
                    dve.wait_ge(made, base + 4 * k + 1)
                    stt(x1, z, a12, tx[:], ALU.mult, ALU.add).then_inc(made, 1)
                    dve.wait_ge(made, base + 4 * k + 2)
                    stt(z1, z, a22, tz[:], ALU.mult, ALU.add).then_inc(made, 1)
                    dve.wait_ge(made, base + 4 * k + 4)
                count[0] += 4 * N2

                b11, b12 = vx[:, N2, NS:NS + 1], vx[:, N2, NS + 1:NS + 2]
                b21, b22 = vz[:, N2, NS:NS + 1], vz[:, N2, NS + 1:NS + 2]
                span_x = vx[:, N2, 0:NS].rearrange("p (w c) -> p w c", w=2)
                span_z = vz[:, N2, 0:NS].rearrange("p (w c) -> p w c", w=2)
                both = slice(0, 2)
                base = count[0]
                for k in range(N3 - 1):
                    stt(tx[:, 0:2], at(wx, both, k), b11, at(span_x, both, k), ALU.mult, ALU.add).then_inc(made, 1)
                    stt(tz[:, 0:2], at(wx, both, k), b21, at(span_z, both, k), ALU.mult, ALU.add).then_inc(made, 1)
                    dve.wait_ge(made, base + 4 * k + 1)
                    stt(at(wx, both, k + 1), at(wz, both, k), b12, tx[:, 0:2], ALU.mult, ALU.add).then_inc(made, 1)
                    dve.wait_ge(made, base + 4 * k + 2)
                    stt(at(wz, both, k + 1), at(wz, both, k), b22, tz[:, 0:2], ALU.mult, ALU.add).then_inc(made, 1)
                    dve.wait_ge(made, base + 4 * k + 4)
                count[0] += 4 * (N3 - 1)

                start_x, start_z = wx[:].rearrange("p w c -> p (w c)"), wz[:].rearrange("p w c -> p (w c)")
                cx_at, cz_at = (t[:].rearrange("p (s c) -> p s c", c=N2) for t in (cx, cz))
                spans = slice(0, NS)
                for part, start in ((0, start_x), (1, start_z)):
                    base = count[0]
                    for k in range(N2):
                        for v, c_at in ((vx, cx_at), (vz, cz_at)):
                            coef = v[:, ds(k, 1), NS + part:NS + part + 1].rearrange("p o l -> p (o l)")
                            own = v[:, ds(k, 1), 0:NS].rearrange("p o l -> p (o l)") if part == 0 else at(c_at, spans, k)
                            stt(at(c_at, spans, k), start, coef, own, ALU.mult, ALU.add).then_inc(made, 1)
                    count[0] += 2 * N2
                    dve.wait_ge(made, count[0])

                for w in range(2):
                    lanes = slice(w * LANES // 2, (w + 1) * LANES // 2)
                    for part, start in ((0, cx), (1, cz)):
                        with dve.Fori(0, 2) as i:
                            for j in range(N1 // 2):
                                n = (N1 // 2) * i + j
                                coef = z_at[:, LANES + part:LANES + part + 1, ds(n, 1)].rearrange("p l o -> p (l o)")
                                stt(at(z_at, lanes, n), start[:, lanes], coef, at(z_at, lanes, n), ALU.mult, ALU.add).then_inc(made, 1)
                        count[0] += N1
                        dve.wait_ge(made, count[0])
                    if w == 0:
                        nc.vector.sem_inc(z_there, NCH // 2)
                nc.vector.tensor_scalar(Z[:, CLS:COLS], fcls[:], DT, None, ALU.mult).then_inc(z_there, NCH + 1 - NCH // 2)
                gate(dve, nc.vector, "dve")


def router(nc, X3, scratch, tw, ew1, w1_sel, b1_sel, b2_mix, spread):
    with ExitStack() as ctx:
        sb = lambda nm, shape, dt=F32: ctx.enter_context(nc.sbuf_tensor(f"route_{nm}", shape, dt))
        sem = lambda nm: ctx.enter_context(nc.semaphore(f"route_{nm}"))
        E = N_EXP
        sums, wr = sb("sums", [P, 2]), sb("wr", [P, 2, E])
        r, r2 = sb("r", [P, 2, E]), sb("r2", [P, 2, E])
        m = sb("m", [P, 2])
        tot, inv = sb("tot", [P, 2]), sb("inv", [P, 2])
        load, scale = sb("load", [P, E]), sb("scale", [P, E])
        cand, hot = sb("cand", [P, 2, E]), sb("hot", [P, 2, 2, E])
        top, gates, gated = sb("top", [P, 2, 2]), sb("gates", [P, 2, 2]), sb("gated", [P, 2, 2, E])
        e2, den = sb("e2", [P, 2]), sb("den", [P, 2])
        prod1, prod2 = sb("prod1", [P, 8, E]), sb("prod2", [P, 2, 2 * E])
        both = sb("both", [P, 2, 2 * 2 * E])
        ps = ctx.enter_context(nc.psum_tensor("route_ps", [P, 512], F32))
        made, by_pe, by_act, by_pool = sem("made"), sem("by_pe"), sem("by_act"), sem("by_pool")
        spread_ready = sem("spread_ready")
        summed = sem("summed")
        with nc.Block() as block:
            @block.tensor
            def _(pe):
                pe.wait_ge(made, 4)
                nc.tensor.matmul(ps[:, 0:2 * E], tw("group_ones"), wr[:].rearrange("p w e -> p (w e)"), start=True, stop=True).then_inc(by_pe, 1)
                pe.wait_ge(made, 10)
                nc.tensor.matmul(ps[:, 0:2 * E], tw("all_ones"), r[:].rearrange("p w e -> p (w e)"), start=True, stop=True).then_inc(by_pe, 1)
                pe.wait_ge(spread_ready, 1)
                for g in range(2):
                    last = nc.tensor.matmul(ps[:, g * 64:(g + 1) * 64], tw(f"pick{g}"), both[:].rearrange("p a b -> p (a b)"), start=True, stop=True)
                last.then_inc(by_pe, 1)

            @block.scalar
            def _(act):
                nc.scalar.activation(scratch[:, 0:TIME], X3[:, TIME:CLS], ACT.Copy, accum_out=sums[:, 1:2]).then_inc(summed, 1)
                act.wait_ge(made, 7)
                nc.scalar.activation(r[:], r[:], ACT.Exp).then_inc(by_act, 1)
                act.wait_ge(made, 17)
                nc.scalar.activation(r2[:], r2[:], ACT.Exp).then_inc(by_act, 1)
                act.wait_ge(made, 32)
                nc.scalar.activation(e2[:], e2[:], ACT.Exp).then_inc(by_act, 1)

            @block.vector
            def _(dve):
                count = [0]

                def link(ins):
                    count[0] += 1
                    ins.then_inc(made, 1)
                    dve.wait_ge(made, count[0])

                wide = lambda t: t[:].unsqueeze(2).to_broadcast([P, 2, E])
                link(nc.vector.reduce_sum(sums[:, 0:1], X3[:, 0:TIME], AX.X))
                dve.wait_ge(summed, 1)
                link(nc.vector.tensor_tensor(sums[:], sums[:], X3[:, CLS:COLS], ALU.add))
                for w in range(2):
                    link(nc.vector.tensor_scalar(wr[:, w, :], tw("Wr"), sums[:, w:w + 1], 1.0 / SEQ, ALU.mult, ALU.mult))
                dve.wait_ge(by_pe, 1)
                link(nc.vector.tensor_tensor(r[:].rearrange("p w e -> p (w e)"), ps[:, 0:2 * E], tw("br_row"), ALU.add))

                def softmax(t, n_act):
                    link(nc.vector.reduce_max(m[:], t[:], AX.X))
                    link(nc.vector.tensor_tensor(t[:], t[:], wide(m), ALU.subtract))
                    dve.wait_ge(by_act, n_act)
                    link(nc.vector.reduce_sum(tot[:], t[:], AX.X))
                    link(nc.vector.reciprocal(inv[:], tot[:]))
                    link(nc.vector.tensor_tensor(t[:], t[:], wide(inv), ALU.mult))

                softmax(r, 1)
                dve.wait_ge(by_pe, 2)
                link(nc.vector.reduce_sum(load[:], ps[:, 0:2 * E].rearrange("p (w e) -> p e w", w=2), AX.X))
                link(nc.vector.tensor_scalar(load[:], load[:], 1.0 / C, float(SEQ), ALU.mult, ALU.mult))
                link(nc.vector.reciprocal(scale[:], load[:]))
                link(nc.vector.tensor_scalar(scale[:], scale[:], CAPACITY, 1.0, ALU.mult, ALU.min))
                link(nc.vector.tensor_tensor(r2[:], r[:], scale[:].unsqueeze(1).to_broadcast([P, 2, E]), ALU.mult))
                softmax(r2, 2)
                index = tw("index_row").unsqueeze(1).to_broadcast([P, 2, E])
                for c in range(2):
                    link(nc.vector.reduce_max(top[:, :, c], r2[:], AX.X))
                    link(nc.vector.tensor_tensor(cand[:], r2[:], top[:, :, c].unsqueeze(2).to_broadcast([P, 2, E]), ALU.is_equal))
                    link(nc.vector.tensor_tensor(cand[:], cand[:], index, ALU.mult))
                    link(nc.vector.reduce_max(m[:], cand[:], AX.X))
                    if c == 0:
                        link(nc.vector.tensor_tensor(hot[:, :, c, :], cand[:], wide(m), ALU.is_equal))
                        for w in range(2):
                            link(nc.vector.scalar_tensor_tensor(r2[:, w, :], hot[:, w, c, :], -2.0, r2[:, w, :], ALU.mult, ALU.add))
                    else:
                        link(nc.vector.tensor_tensor(e2[:], top[:, :, 1], top[:, :, 0], ALU.subtract))
                        hot_at = count[0]
                        link(nc.vector.tensor_tensor(hot[:, :, c, :], cand[:], wide(m), ALU.is_equal))
                assert count[0] == 33, count[0]
                dve.wait_ge(by_act, 3)
                link(nc.vector.tensor_scalar(den[:], e2[:], 1.0, None, ALU.add))
                link(nc.vector.reciprocal(gates[:, :, 0], den[:]))
                link(nc.vector.tensor_tensor(gates[:, :, 1], gates[:, :, 0], e2[:], ALU.mult))
                link(nc.vector.tensor_tensor(gated[:].rearrange("p w c e -> p (w c) e"), hot[:].rearrange("p w c e -> p (w c) e"),
                                             gates[:].rearrange("p w c -> p (w c)").unsqueeze(2).to_broadcast([P, 4, E]), ALU.mult))
                nc.vector.tensor_copy(both[:, 0, :], hot[:].rearrange("p w c e -> p (w c e)"))
                nc.vector.tensor_copy(both[:, 1, :], gated[:].rearrange("p w c e -> p (w c e)")).then_inc(spread_ready, 1)
                sums_at = count[0]
                for e in range(E):
                    for i, (w, c) in enumerate(((0, 0), (0, 1), (1, 0), (1, 1))):
                        dst, own = w1_sel[:, i * FF:(i + 1) * FF], ew1[:, e * FF:(e + 1) * FF]
                        if e == 0:
                            ins = nc.vector.tensor_scalar(dst, own, hot[:, w, c, 0:1], None, ALU.mult)
                        else:
                            dve.wait_ge(made, sums_at + 4 * (e - 1) + i + 1)
                            ins = nc.vector.scalar_tensor_tensor(dst, own, hot[:, w, c, e:e + 1], dst, ALU.mult, ALU.add)
                        ins.then_inc(made, 1)
                count[0] += 4 * E
                for w in range(2):
                    link(nc.vector.tensor_tensor(prod2[:, w, :].rearrange("p (c e) -> p c e", c=2), gated[:, w, :, :],
                                                 tw("b2T").unsqueeze(1).to_broadcast([P, 2, E]), ALU.mult))
                link(nc.vector.reduce_sum(b2_mix[:], prod2[:], AX.X))
                dve.wait_ge(by_pe, 3)
                link(nc.vector.tensor_copy(spread[:].rearrange("p g a w c e -> p (g a w c e)"), ps[:, 0:2 * 64]))
                for g in range(2):
                    link(nc.vector.tensor_tensor(prod1[:, 4 * g:4 * g + 4, :], spread[:, g, 0, :, :, :].rearrange("p w c e -> p (w c) e"),
                                                 tw("b1T").unsqueeze(1).to_broadcast([P, 4, E]), ALU.mult))
                link(nc.vector.reduce_sum(b1_sel[:], prod1[:], AX.X))


def experts(nc, X3, Y, ew2, w1_sel, w2_sel, b1_sel, b2_mix, spread):
    with ExitStack() as ctx:
        sb = lambda nm, shape, dt=F32: ctx.enter_context(nc.sbuf_tensor(f"ex_{nm}", shape, dt))
        pb = lambda nm, shape, dt=F32: ctx.enter_context(nc.psum_tensor(f"ex_{nm}", shape, dt))
        sem = lambda nm: ctx.enter_context(nc.semaphore(f"ex_{nm}"))
        xin = [sb(f"xin{i}", [P, CH]) for i in range(2)]
        hid = [[sb(f"hid{i}_{j}", [P, CH]) for j in range(4)] for i in range(2)]
        ps_h = [pb(f"ps_h{j}", [P, 512]) for j in range(4)]
        ps_y = [pb(f"ps_y{i}", [P, 512]) for i in range(2)]
        x_in = sem("x_in")
        h_ps = sem("h_ps")
        h_ready = sem("h_ready")
        y_ps = sem("y_ps")
        y_ready = sem("y_ready")
        w2_ready = sem("w2_ready")
        PER = NCH // 2
        assert PER % 2 == 1

        def pairs(eng, w, body):
            first = w * PER + 1
            if w == 0:
                for k in (1, 2):
                    body(k, k % 2, k * CH)
            with eng.Fori(1 - w, PER // 2) as i:
                for q in range(2):
                    k = 2 * i + first + q
                    body(k, (first + q) % 2, k * CH)

        def order(eng, step):
            for w in range(2):
                step(w * PER, w, w * PER % 2, w * PER * CH, CH)
                pairs(eng, w, lambda k, p, at: step(k, w, p, at, CH))
            for w in range(2):
                step(NCH + w, w, (NCH + w) % 2, CLS + w, 1)

        def lagging(eng, step, behind):
            for w in range(2):
                first = w * PER
                step(first, w, first % 2, first * CH, CH)
                if w:
                    behind(first - 1, 0, (first - 1) % 2, (first - 1) * CH, CH)

                def both(k, p, at):
                    step(k, w, p, at, CH)
                    behind(k - 1, w, 1 - p, (k - 1) * CH, CH)
                pairs(eng, w, both)
            step(NCH, 0, NCH % 2, CLS, 1)
            behind(NCH - 1, 1, (NCH - 1) % 2, (NCH - 1) * CH, CH)
            step(NCH + 1, 1, (NCH + 1) % 2, CLS + 1, 1)
            behind(NCH, 0, NCH % 2, CLS, 1)
            behind(NCH + 1, 1, (NCH + 1) % 2, CLS + 1, 1)

        with nc.Block() as block:
            @block.gpsimd
            def _(pool):
                def step(k, w, p, at, n):
                    wait(pool, h_ps, 4 * k - 4)
                    nc.gpsimd.tensor_copy(xin[p][:, 0:n], X3[:, ds(at, n)]).then_inc(x_in, 1)
                order(pool, step)

            @block.tensor
            def _(pe):
                def up(k, w, p, at, n):
                    pe.wait_ge(x_in, k + 1)
                    for c in range(2):
                        for g in range(2):
                            j, r = 2 * c + g, slice(C * g, C * g + C)
                            wait(pe, h_ready, 4 * k - 4 + j + 1)
                            nc.tensor.matmul(ps_h[j][:, 0:n], w1_sel[r, (2 * w + c) * FF:(2 * w + c + 1) * FF], xin[p][r, 0:n],
                                             start=True, stop=True).then_inc(h_ps, 1)

                def down(k, w, p, at, n):
                    if isinstance(k, int) and k == 0:
                        pe.wait_ge(w2_ready, 8 * N_EXP)
                    wait(pe, y_ready, k - 1)
                    for c in range(2):
                        for g in range(2):
                            j, i = 2 * c + g, 4 * g + 2 * w + c
                            pe.wait_ge(h_ready, 4 * k + j + 1)
                            last = nc.tensor.matmul(ps_y[p][C * g:C * g + C, 0:n], w2_sel[:, i * C:(i + 1) * C], hid[p][j][:, 0:n],
                                                    start=(c == 0), stop=(c == 1), skip_group_check=True)
                    last.then_inc(y_ps, 1)
                lagging(pe, up, down)

            @block.scalar
            def _(act):
                def step(k, w, p, at, n):
                    wait(act, y_ps, k - 1)
                    for j in range(4):
                        c, g = j // 2, j % 2
                        act.wait_ge(h_ps, 4 * k + j + 1)
                        i = 4 * g + 2 * w + c
                        nc.scalar.activation(hid[p][j][:, 0:n], ps_h[j][:, 0:n], ACT.Gelu, bias=b1_sel[:, i:i + 1]).then_inc(h_ready, 1)
                order(act, step)

            @block.vector
            def _(dve):
                for e in range(N_EXP):
                    for i in range(8):
                        g, w, c = i // 4, i // 2 % 2, i % 2
                        dst, own = w2_sel[:, i * C:(i + 1) * C], ew2[:, e * C:(e + 1) * C]
                        if e == 0:
                            ins = nc.vector.tensor_scalar(dst, own, spread[:, g, 1, w, c, 0:1], None, ALU.mult)
                        else:
                            dve.wait_ge(w2_ready, 8 * (e - 1) + i + 1)
                            ins = nc.vector.scalar_tensor_tensor(dst, own, spread[:, g, 1, w, c, e:e + 1], dst, ALU.mult, ALU.add)
                        ins.then_inc(w2_ready, 1)

                def step(k, w, p, at, n):
                    dve.wait_ge(y_ps, k + 1)
                    nc.vector.scalar_tensor_tensor(Y[:, ds(at, n)], ps_y[p][:, 0:n], b2_mix[:, w:w + 1], X3[:, ds(at, n)],
                                                   ALU.add, ALU.add).then_inc(y_ready, 1)
                order(dve, step)


def tail(nc, ctx, X, X2, H0, con, tail_w, ew1, ew2, out, debug):
    sb = lambda name, shape, dt=F32: ctx.enter_context(nc.sbuf_tensor(name, shape, dt))
    u_cols = X[:].rearrange("p t r -> p (t r)")
    f_cols = X2[:].rearrange("p t r -> p (t r)")
    Z = sb("Z", [P, (LANES + 2) * N1])
    w1_sel = sb("w1_sel", [P, 4 * FF])
    w2_sel = sb("w2_sel", [P, 8 * C])
    b1_sel = sb("b1_sel", [P, 8])
    b2_mix = sb("b2_mix", [P, 2])
    spread = sb("spread", [P, 2, 2, 2, 2, N_EXP])
    derived = sb("derived", [P, 6])
    extra = {"s": 0, "neg_dsa": 1, "ds": 2, "bCD": 3, "tmp": 4, "f_bias": 5}

    def tw(name):
        if name in extra:
            return derived[:, extra[name]:extra[name] + 1]
        at, n = TAIL_AT[name]
        return tail_w[:, at:at + n]

    class_tokens(nc, H0, tw("cls"))

    with nc.semaphore("coef") as coef:
        def coefficients(dve):
            count = [0]

            def link(ins):
                count[0] += 1
                ins.then_inc(coef, 1)
                dve.wait_ge(coef, count[0])

            link(nc.vector.tensor_scalar(tw("tmp"), tw("a"), DT * DT, 1.0, ALU.mult, ALU.add))
            link(nc.vector.reciprocal(tw("s"), tw("tmp")))
            link(nc.vector.tensor_scalar(tw("ds"), tw("s"), DT, None, ALU.mult))
            link(nc.vector.scalar_tensor_tensor(tw("neg_dsa"), tw("ds"), -1.0, tw("a"), ALU.mult, ALU.mult))
            link(nc.vector.tensor_tensor(tw("bCD"), tw("bC"), tw("bD"), ALU.add))

        def b_product(at, n, ps):
            return nc.tensor.matmul(ps[:, 0:n], tw("BBD"), u_cols[:, ds(at, n)], start=True, stop=True)

        def forcing(at, n, ps):
            return nc.vector.tensor_scalar(f_cols[:, ds(at, n)], ps[:, 0:n], tw("bB"), tw("ds"), ALU.add, ALU.mult)

        def mixer_in(dve, k, q, at, n, centred, rstd, done, inner, stored):
            nc.vector.tensor_tensor(u_cols[:, ds(at, n)], centred[:, 0:n], rstd[:, 0:n], ALU.mult).then_inc(done, 1)

        def add_u(at, n):
            nc.gpsimd.tensor_tensor(H0[:, ds(at, n)], H0[:, ds(at, n)], u_cols[:, ds(at, n)], ALU.add)

        channel_norm(nc, "cn0", H0, con, mixer_in, product=b_product, after_product=forcing, on_pool=add_u, setup=coefficients)
    H1 = Z
    mixer(nc, f_cols, Z, u_cols, f_cols, H0, H1, tw)
    if debug == "h1":
        return dump(nc, H1, out)
    X3 = u_cols

    def ffn_in(dve, k, q, at, n, centred, rstd, done, inner, stored):
        nc.vector.tensor_tensor(X3[:, ds(at, n)], centred[:, 0:n], rstd[:, 0:n], ALU.mult).then_inc(done, 1)

    channel_norm(nc, "cn1", H1, con, ffn_in)
    router(nc, X3, f_cols, tw, ew1, w1_sel, b1_sel, b2_mix, spread)
    Y = f_cols
    experts(nc, X3, Y, ew2, w1_sel, w2_sel, b1_sel, b2_mix, spread)
    res = [sb(f"res{i}", [P, CH]) for i in range(4)]
    scaled = [sb(f"scaled{i}", [P, CH]) for i in range(2)]

    def final(dve, k, q, at, n, centred, rstd, done, inner, stored):
        nc.vector.scalar_tensor_tensor(scaled[q % 2][:, 0:n], centred[:, 0:n], tw("gamma"), rstd[:, 0:n], ALU.mult, ALU.mult).then_inc(inner, 1)
        wait(dve, stored[q], 4 * k - 4 * q)
        dve.wait_ge(inner, k + 1)
        nc.vector.scalar_tensor_tensor(res[q][:, 0:n], scaled[q % 2][:, 0:n], tw("beta"), H1[:, ds(at, n)], ALU.add, ALU.add).then_inc(done, 1)

    def store(sp, q, at, n):
        return sp.dma_start(out[:, ds(at, n)], res[q][:, 0:n])

    channel_norm(nc, "cn2", Y, con, final, out_dma=store)


def _dup(a):
    return np.concatenate([a, a], axis=0)


def _col(v):
    return _dup(v.reshape(-1, 1))


def _blockdiag(a):
    z = np.zeros((2 * C, 2 * C), np.float32)
    z[:C, :C] = a
    z[C:, C:] = a
    return z


def _rows(v, n=P):
    return np.broadcast_to(v.reshape(1, -1), (n, v.size))


def _pack(order, parts):
    return np.ascontiguousarray(np.concatenate([parts[n] for n, _ in order], axis=1), dtype=np.float32)


def kernel(_debug=None, **inputs):
    import concourse.bacc as _bacc
    from concourse.bass_utils import run_bass_kernel_spmd as _run

    a = {k: np.asarray(v) for k, v in inputs.items()}
    x = a["x"].reshape(2, 2, NW, WS, 4, NW, WS, 4)
    x = x.transpose(4, 7, 2, 5, 0, 1, 3, 6).reshape(PATCH, U, 2, 2, TOK)
    pat = np.zeros((PATCH + 1, U, 2, 2, C), np.float32)
    pat[:PATCH, ..., :TOK] = x
    pat[PATCH, ..., :TOK] = 1.0
    pat = np.ascontiguousarray(pat.reshape(PATCH + 1, TILES // 8, 8 * P).transpose(1, 0, 2))
    patch_w = np.concatenate([a["L0_tok_pe_w"].reshape(C, PATCH).T, a["L0_tok_pe_b"].reshape(1, C)], axis=0)

    p = np.arange(P)
    same_half = (p[:, None] // C == p[None, :] // C)
    common = _pack(COMMON_COLS, {
        "ident": np.eye(P, dtype=np.float32),
        "mean_ones": same_half.astype(np.float32) / C,
        "head_mask": ((p[:, None] % C) // HD == np.arange(NH)[None, :]).astype(np.float32),
        "pg_row": _rows(a["L0_tok_pe_ng"]), "pbeta_row": _rows(a["L0_tok_pe_nb"])})
    blocks, biases = [], []
    coords = np.stack(np.meshgrid(np.arange(WS), np.arange(WS), indexing="ij")).reshape(2, -1)
    rel = coords[:, :, None] - coords[:, None, :] + WS - 1
    rpi = rel[0] * (2 * WS - 1) + rel[1]
    for b in range(2):
        w = a["L0_tok_qkv_w"][b]
        qb = a["L0_tok_qkv_b"][b]
        w1T = a["L0_tok_w1"][b].T
        w2 = a["L0_tok_w2"][b].T.reshape(2, P, C).transpose(1, 0, 2).reshape(P, 2 * C)
        blocks.append(_pack(BLOCK_COLS, {
            "qBD": _blockdiag(w[:C].T), "kBD": _blockdiag(w[C:2 * C].T), "vBD": _blockdiag(w[2 * C:].T),
            "pBD": _blockdiag(a["L0_tok_proj_w"][b].T), "w2T": w2,
            "w1T0": np.concatenate([w1T, np.zeros_like(w1T)]), "w1T1": np.concatenate([np.zeros_like(w1T), w1T]),
            "n1g": _col(a["L0_tok_n1g"][b]), "n1b": _col(a["L0_tok_n1b"][b]),
            "qb": _col(qb[:C]), "kb": _col(qb[C:2 * C]), "vb": _col(qb[2 * C:]),
            "n2g": _col(a["L0_tok_n2g"][b]), "n2b": _col(a["L0_tok_n2b"][b]),
            "b1": a["L0_tok_b1"][b].reshape(2, P).T,
            "pb_row": _rows(a["L0_tok_proj_b"][b]), "b2": _col(a["L0_tok_b2"][b])}))
        t = a["L0_tok_rpb"][b][rpi].transpose(0, 2, 1).reshape(TOK, NH * TOK)
        z = np.zeros((2, C, NH * TOK), np.float32)
        z[:, :TOK] = t
        biases.append(z.reshape(P, NH * TOK))
    part = np.arange(WS) >= WS - SHIFT
    row_part, col_part = np.repeat(part, WS), np.tile(part, WS)
    masks = np.zeros((2, C, 4, TOK), np.float32)
    for v in range(4):
        label = row_part * (v >> 1) * 2 + col_part * (v & 1)
        masks[:, :TOK, v] = np.where(label[:, None] != label[None, :], -100.0, 0.0)
    masks = masks.reshape(P, 4, TOK)
    pick = np.zeros((2, P, P), np.float32)
    pick[0, 0, :] = 1.0
    pick[1, C, :] = 1.0
    tail_w = _pack(TAIL_COLS, {
        "BBD": _blockdiag(a["L0_attn_W_B"].T), "CBD": _blockdiag(a["L0_attn_W_C"].T), "DBD": _blockdiag(a["L0_attn_W_D"].T),
        "a": _col(a["L0_attn_a"]), "bB": _col(a["L0_attn_b_B"]), "bC": _col(a["L0_attn_b_C"]), "bD": _col(a["L0_attn_b_D"]),
        "cls": _col(a["cls_tok"].reshape(C)), "Wr": _dup(a["L0_ffn_Wr"]),
        "br_row": np.concatenate([_rows(a["L0_ffn_br"])] * 2, axis=1),
        "gamma": _col(a["L0_ffn_gamma"]), "beta": _col(a["L0_ffn_beta"]), "b2T": _dup(a["L0_ffn_b2"].T), "b1T": a["L0_ffn_b1"].T,
        "group_ones": same_half.astype(np.float32), "all_ones": np.ones((P, P), np.float32),
        "pick0": pick[0], "pick1": pick[1],
        "index_row": _rows(np.arange(N_EXP, 0, -1).astype(np.float32))})
    ew1 = _dup(a["L0_ffn_W1"].transpose(1, 0, 2).reshape(C, N_EXP * FF))
    ew2 = np.ascontiguousarray(a["L0_ffn_W2"].transpose(1, 0, 2).reshape(FF, N_EXP * C))

    nc = _bacc.Bacc("TRN2", target_bir_lowering=False, num_devices=1)
    arrays, args = {}, []
    for name, v in (("patches", pat), ("patch_w", patch_w), ("common", common), ("blocks", np.stack(blocks)),
                    ("biases", np.stack(biases)), ("masks", masks), ("tail_w", tail_w), ("ew1", ew1), ("ew2", ew2)):
        v = np.ascontiguousarray(v)
        arrays[f"in_{name}"] = v
        args.append(nc.dram_tensor(f"in_{name}", v.shape, mybir.dt.from_np(v.dtype), kind="ExternalInput").ap())
    shape = {None: (P, 2 * SEQ), "m0": (P, TILES, ROW), "a1": (P, TILES, ROW), "h1": (P, COLS)}[_debug]
    out = nc.dram_tensor("out", shape, F32, kind="ExternalOutput").ap()
    build(nc, *args, out, debug=_debug)
    r = _run(nc, [arrays], core_ids=[0])
    got = r.results[0]["out"]
    got = got.reshape(2, C, 2 * SEQ)
    image = got[:, :, :2 * TIME].reshape(2, C, 2, TIME).transpose(0, 2, 3, 1).reshape(4, TIME, C)
    first = got[:, :, 2 * TIME:].transpose(0, 2, 1).reshape(4, 1, C)
    return np.ascontiguousarray(np.concatenate([first, image], axis=1))
```
